# Optimizing a Trainium2 kernel written in Bass

```python
import numpy as np
import jax
import jax.numpy as jnp

def _softmax(x, axis=-1):
    return jax.nn.softmax(x, axis=axis)

def _gelu(x):
    return jax.nn.gelu(x, approximate=True)

def _silu(x):
    return jax.nn.silu(x)

def _sigmoid(x):
    return jax.nn.sigmoid(x)

def _layernorm(x, axis=-1, eps=1e-05):
    m = jnp.mean(x, axis=axis, keepdims=True)
    v = jnp.var(x, axis=axis, keepdims=True)
    return (x - m) / jnp.sqrt(v + eps)

def _scatter_add(tgt, idx, src, axis=0):
    return tgt.at[idx].add(src)

def _segment_sum(src, seg, n):
    return jax.ops.segment_sum(src, seg, n)
kernel_name = 'mk_decoder_postln_d1_seqx_r4_393bab'

def setup_inputs(seed: int=0):
    np.random.seed(seed)
    _w = jnp.asarray

    def _rec_inputs():
        import jax
        import jax.numpy as jnp
        _rk = jax.random.key(seed)
        x = 0.0002417 + 0.9998 * jax.random.normal(jax.random.fold_in(_rk, 1), (4, 512, 256), jnp.float32)
        _lenS = 512 - jax.random.randint(jax.random.fold_in(_rk, 7), (4,), 0, max(1, 512 // 4) + 1, jnp.int32)
        _lenS2 = 1601 - jax.random.randint(jax.random.fold_in(_rk, 8), (4,), 0, max(1, 1601 // 4) + 1, jnp.int32)
        _ctx_1024P = jax.random.normal(jax.random.fold_in(_rk, 11), (4, 16, 256), jnp.float32)
        _ctx_1024c = jax.random.dirichlet(jax.random.fold_in(_rk, 511), 0.3 * jnp.ones((16,), jnp.float32), (4, 1601))
        _ctx_1024t = jnp.einsum('bsk,bkd->bsd', _ctx_1024c, _ctx_1024P)
        _ctx_1024t = _ctx_1024t * jax.lax.rsqrt(jnp.mean(jnp.square(_ctx_1024t)) + 1e-12) * 0.953939
        ctx_1024 = 7.22013e-05 + 1.00017 * (_ctx_1024t + 0.3 * jax.random.normal(jax.random.fold_in(_rk, 611), (4, 1601, 256), jnp.float32))
        return (x, ctx_1024)
    x, ctx_1024 = _rec_inputs()

    def _L0_attn_setup():
        import jax, jax.numpy as jnp
        import numpy as np
        B, L, D, H = (2, 512, 256, 4)
        DV = D // H
        P = 5
        CHUNK = 32
        CONV_K = 4
        FIR_K = (3, 15, 64)

        def _dwconv(x, w):
            K = w.shape[1]
            xt = jnp.pad(jnp.transpose(x, (0, 2, 1)), ((0, 0), (0, 0), (K - 1, 0)))
            y = jax.lax.conv_general_dilated(xt, w[:, None, :], (1,), 'VALID', dimension_numbers=('NCH', 'OIH', 'NCH'), feature_group_count=w.shape[0])
            return jnp.transpose(y, (0, 2, 1))

        def _l2norm(x):
            return x * jax.lax.rsqrt(jnp.sum(x * x, -1, keepdims=True) + 1e-06)

        def _delta_rule_chunkwise(q, k, v, beta, chunk=CHUNK):
            b, h, Lp, dk = q.shape
            dv = v.shape[-1]
            n = Lp // chunk
            q = _l2norm(q)
            k = _l2norm(k)
            v = v * beta[..., None]
            kb = k * beta[..., None]
            r = lambda t: t.reshape(b, h, n, chunk, -1)
            q, k, v, kb = (r(q), r(k), r(v), r(kb))
            sw = lambda t: jnp.swapaxes(t, -1, -2)
            strict = jnp.tril(jnp.ones((chunk, chunk), bool), -1)
            attn = jnp.where(strict, -(kb @ sw(k)), 0.0)
            T = jnp.linalg.inv(jnp.eye(chunk, dtype=q.dtype) - attn)
            u = T @ v
            w = T @ kb
            incl = jnp.tril(jnp.ones((chunk, chunk), bool), 0)
            qs, ks, us, ws = (jnp.moveaxis(t, 2, 0) for t in (q, k, u, w))
            S0 = jnp.zeros((b, h, dk, dv), q.dtype)

            def step(S, inp):
                q_i, k_i, u0, w_i = inp
                local = jnp.where(incl, q_i @ sw(k_i), 0.0)
                u_i = u0 - w_i @ S
                o_i = q_i @ S + local @ u_i
                return (S + sw(k_i) @ u_i, o_i)
            S, o = jax.lax.scan(step, S0, (qs, ks, us, ws))
            return (jnp.moveaxis(o, 0, 2).reshape(b, h, Lp, dv), S)

        def _stats(t):
            m = jnp.mean(t, -1, keepdims=True)
            v = jnp.mean(t * t, -1, keepdims=True)
            a = jnp.mean(jnp.abs(t), -1, keepdims=True)
            nrm = jnp.sqrt(jnp.sum(t * t, -1, keepdims=True))
            s = jnp.concatenate([jnp.broadcast_to(x, t.shape) for x in (m, v, a, nrm)], -1)
            return s.reshape(t.shape[0], t.shape[1], -1)

        def _forward(hs, Wq, Wk, Wv, conv_q, conv_k, conv_v, Wb, fir_s, fir_m, fir_l, gW1, gb1, gW2, gb2, log_tau, eps_logit, norm_w, Wo):
            b, Ln, _ = hs.shape
            q = jax.nn.silu(_dwconv(hs @ Wq, conv_q))
            k = jax.nn.silu(_dwconv(hs @ Wk, conv_k))
            v = jax.nn.silu(_dwconv(hs @ Wv, conv_v))
            beta = jax.nn.sigmoid(hs @ Wb)
            bh = lambda t: jnp.transpose(t.reshape(b, Ln, H, -1), (0, 2, 1, 3))
            o_d, _ = _delta_rule_chunkwise(bh(q), bh(k), bh(v), jnp.transpose(beta, (0, 2, 1)))
            delta_path = jnp.transpose(o_d, (0, 2, 1, 3))
            paths = jnp.stack([_dwconv(v, fir_s).reshape(b, Ln, H, DV), _dwconv(v, fir_m).reshape(b, Ln, H, DV), _dwconv(v, fir_l).reshape(b, Ln, H, DV), delta_path, v.reshape(b, Ln, H, DV)], axis=3)
            stats_flat = jnp.concatenate([_stats(paths[..., p, :]) for p in range(P)], -1)
            gate_in = jnp.concatenate([hs, stats_flat], -1)
            logits = jax.nn.gelu(gate_in @ gW1 + gb1, approximate=False) @ gW2 + gb2
            logits = logits.reshape(b, Ln, H, P)
            tau = jax.nn.softplus(log_tau) + 0.5
            probs = jax.nn.softmax(logits / tau[:, None], -1)
            eps = jax.nn.sigmoid(eps_logit) * 0.2
            probs = probs * (1.0 - jnp.sum(eps, -1, keepdims=True)) + eps
            o = jnp.einsum('blhp,blhpd->blhd', probs, paths)
            o = o * jax.lax.rsqrt(jnp.mean(o * o, -1, keepdims=True) + 1e-05) * norm_w
            return o.reshape(b, Ln, D) @ Wo
        key = jax.random.key(seed)
        ks = jax.random.split(key, 14)
        lin = lambda kk, fan_in, shape: jax.random.normal(kk, shape, jnp.float32) / np.float32(np.sqrt(fan_in))

        def fir(kk, K):
            w = np.zeros((D, K), np.float32)
            w[:, -1] = 1.0
            return jnp.asarray(w) + 0.001 * jax.random.normal(kk, (D, K), jnp.float32)
        in_gate = D + 4 * DV * H * P
        HF = 2 * D
        gb2 = np.zeros((H * P,), np.float32)
        gb2[np.arange(H) * P + P - 1] = 1.0
        return {'hidden_states': jax.random.normal(ks[0], (B, L, D), jnp.float32), 'Wq': lin(ks[1], D, (D, D)), 'Wk': lin(ks[2], D, (D, D)), 'Wv': lin(ks[3], D, (D, D)), 'conv_q': lin(ks[4], CONV_K, (D, CONV_K)), 'conv_k': lin(ks[5], CONV_K, (D, CONV_K)), 'conv_v': lin(ks[6], CONV_K, (D, CONV_K)), 'Wb': lin(ks[7], D, (D, H)), 'fir_s': fir(ks[8], FIR_K[0]), 'fir_m': fir(ks[9], FIR_K[1]), 'fir_l': fir(ks[10], FIR_K[2]), 'gW1': lin(ks[11], in_gate, (in_gate, HF)), 'gb1': jnp.zeros((HF,), jnp.float32), 'gW2': lin(ks[12], HF, (HF, H * P)), 'gb2': jnp.asarray(gb2), 'log_tau': jnp.zeros((H,), jnp.float32), 'eps_logit': jnp.zeros((H, P), jnp.float32), 'norm_w': jnp.ones((DV,), jnp.float32), 'Wo': lin(ks[13], D, (D, D))}
    _L0_attn_all = _L0_attn_setup()
    _L0_attn_in = {k: v for k, v in _L0_attn_all.items() if k in ('Wq', 'Wk', 'Wv', 'conv_q', 'conv_k', 'conv_v', 'Wb', 'fir_s', 'fir_m', 'fir_l', 'gW1', 'gb1', 'gW2', 'gb2', 'log_tau', 'eps_logit', 'norm_w', 'Wo')}
    del _L0_attn_all

    def _L0_xattn_setup():
        import jax, jax.numpy as jnp
        import numpy as np
        D_MODEL = 256
        B, S = (4, 512)
        key = jax.random.key(seed)
        ks = jax.random.split(key, 10)
        s = 1.0 / np.sqrt(D_MODEL)
        return {'k': jax.random.normal(ks[0], (B, S, D_MODEL), jnp.float32), 'v': jax.random.normal(ks[1], (B, S, D_MODEL), jnp.float32), 'q': jax.random.normal(ks[2], (B, S, D_MODEL), jnp.float32), 'Wk': jax.random.normal(ks[3], (D_MODEL, D_MODEL), jnp.float32) * s, 'Wv': jax.random.normal(ks[4], (D_MODEL, D_MODEL), jnp.float32) * s, 'bv': jnp.zeros((D_MODEL,), jnp.float32), 'Wq': jax.random.normal(ks[5], (D_MODEL, D_MODEL), jnp.float32) * s, 'bq': jnp.zeros((D_MODEL,), jnp.float32), 'Wo': jax.random.normal(ks[6], (D_MODEL, D_MODEL), jnp.float32) * s, 'bo': jnp.zeros((D_MODEL,), jnp.float32)}
    _L0_xattn_all = _L0_xattn_setup()
    _L0_xattn_in = {k: v for k, v in _L0_xattn_all.items() if k in ('Wk', 'Wv', 'bv', 'Wq', 'bq', 'Wo', 'bo')}
    del _L0_xattn_all

    def _L0_ffn_setup():
        import jax, jax.numpy as jnp
        import numpy as np
        DIM = 256
        HIDDEN = 768
        SCALE = 1.0 / 127.0

        def _dequant(w_int, dtype):
            return w_int.astype(dtype) * jnp.asarray(SCALE, dtype)
        key = jax.random.key(seed)
        k_x, k_g, k_u, k_d = jax.random.split(key, 4)
        x = jax.random.normal(k_x, (4, 512, DIM), dtype=jnp.float32)
        w_gate = jax.random.randint(k_g, (HIDDEN, DIM), -127, 128, dtype=jnp.int32)
        w_up = jax.random.randint(k_u, (HIDDEN, DIM), -127, 128, dtype=jnp.int32)
        w_down = jax.random.randint(k_d, (DIM, HIDDEN), -127, 128, dtype=jnp.int32)
        return {'x': x, 'w_gate': w_gate, 'w_up': w_up, 'w_down': w_down}
    _L0_ffn_all = _L0_ffn_setup()
    _L0_ffn_in = {k: v for k, v in _L0_ffn_all.items() if k in ('w_gate', 'w_up', 'w_down')}
    del _L0_ffn_all
    return {'x': x, 'ctx_1024': ctx_1024, 'L0_attn_Wq': _L0_attn_in['Wq'], 'L0_attn_Wk': _L0_attn_in['Wk'], 'L0_attn_Wv': _L0_attn_in['Wv'], 'L0_attn_conv_q': _L0_attn_in['conv_q'], 'L0_attn_conv_k': _L0_attn_in['conv_k'], 'L0_attn_conv_v': _L0_attn_in['conv_v'], 'L0_attn_Wb': _L0_attn_in['Wb'], 'L0_attn_fir_s': _L0_attn_in['fir_s'], 'L0_attn_fir_m': _L0_attn_in['fir_m'], 'L0_attn_fir_l': _L0_attn_in['fir_l'], 'L0_attn_gW1': _L0_attn_in['gW1'], 'L0_attn_gb1': _L0_attn_in['gb1'], 'L0_attn_gW2': _L0_attn_in['gW2'], 'L0_attn_gb2': _L0_attn_in['gb2'], 'L0_attn_log_tau': _L0_attn_in['log_tau'], 'L0_attn_eps_logit': _L0_attn_in['eps_logit'], 'L0_attn_norm_w': _L0_attn_in['norm_w'], 'L0_attn_Wo': _L0_attn_in['Wo'], 'L0_xattn_Wk': _L0_xattn_in['Wk'], 'L0_xattn_Wv': _L0_xattn_in['Wv'], 'L0_xattn_bv': _L0_xattn_in['bv'], 'L0_xattn_Wq': _L0_xattn_in['Wq'], 'L0_xattn_bq': _L0_xattn_in['bq'], 'L0_xattn_Wo': _L0_xattn_in['Wo'], 'L0_xattn_bo': _L0_xattn_in['bo'], 'L0_ffn_w_gate': _L0_ffn_in['w_gate'], 'L0_ffn_w_up': _L0_ffn_in['w_up'], 'L0_ffn_w_down': _L0_ffn_in['w_down']}

def reference(x, ctx_1024, L0_attn_Wq, L0_attn_Wk, L0_attn_Wv, L0_attn_conv_q, L0_attn_conv_k, L0_attn_conv_v, L0_attn_Wb, L0_attn_fir_s, L0_attn_fir_m, L0_attn_fir_l, L0_attn_gW1, L0_attn_gb1, L0_attn_gW2, L0_attn_gb2, L0_attn_log_tau, L0_attn_eps_logit, L0_attn_norm_w, L0_attn_Wo, L0_xattn_Wk, L0_xattn_Wv, L0_xattn_bv, L0_xattn_Wq, L0_xattn_bq, L0_xattn_Wo, L0_xattn_bo, L0_ffn_w_gate, L0_ffn_w_up, L0_ffn_w_down):
    import jax
    import jax.numpy as jnp

    def _L0_attn_ref(hidden_states, Wq, Wk, Wv, conv_q, conv_k, conv_v, Wb, fir_s, fir_m, fir_l, gW1, gb1, gW2, gb2, log_tau, eps_logit, norm_w, Wo):
        import jax, jax.numpy as jnp
        import numpy as np
        B, L, D, H = (2, 512, 256, 4)
        DV = D // H
        P = 5
        CHUNK = 32
        CONV_K = 4
        FIR_K = (3, 15, 64)

        def _dwconv(x, w):
            K = w.shape[1]
            xt = jnp.pad(jnp.transpose(x, (0, 2, 1)), ((0, 0), (0, 0), (K - 1, 0)))
            y = jax.lax.conv_general_dilated(xt, w[:, None, :], (1,), 'VALID', dimension_numbers=('NCH', 'OIH', 'NCH'), feature_group_count=w.shape[0])
            return jnp.transpose(y, (0, 2, 1))

        def _l2norm(x):
            return x * jax.lax.rsqrt(jnp.sum(x * x, -1, keepdims=True) + 1e-06)

        def _delta_rule_chunkwise(q, k, v, beta, chunk=CHUNK):
            b, h, Lp, dk = q.shape
            dv = v.shape[-1]
            n = Lp // chunk
            q = _l2norm(q)
            k = _l2norm(k)
            v = v * beta[..., None]
            kb = k * beta[..., None]
            r = lambda t: t.reshape(b, h, n, chunk, -1)
            q, k, v, kb = (r(q), r(k), r(v), r(kb))
            sw = lambda t: jnp.swapaxes(t, -1, -2)
            strict = jnp.tril(jnp.ones((chunk, chunk), bool), -1)
            attn = jnp.where(strict, -(kb @ sw(k)), 0.0)
            T = jnp.linalg.inv(jnp.eye(chunk, dtype=q.dtype) - attn)
            u = T @ v
            w = T @ kb
            incl = jnp.tril(jnp.ones((chunk, chunk), bool), 0)
            qs, ks, us, ws = (jnp.moveaxis(t, 2, 0) for t in (q, k, u, w))
            S0 = jnp.zeros((b, h, dk, dv), q.dtype)

            def step(S, inp):
                q_i, k_i, u0, w_i = inp
                local = jnp.where(incl, q_i @ sw(k_i), 0.0)
                u_i = u0 - w_i @ S
                o_i = q_i @ S + local @ u_i
                return (S + sw(k_i) @ u_i, o_i)
            S, o = jax.lax.scan(step, S0, (qs, ks, us, ws))
            return (jnp.moveaxis(o, 0, 2).reshape(b, h, Lp, dv), S)

        def _stats(t):
            m = jnp.mean(t, -1, keepdims=True)
            v = jnp.mean(t * t, -1, keepdims=True)
            a = jnp.mean(jnp.abs(t), -1, keepdims=True)
            nrm = jnp.sqrt(jnp.sum(t * t, -1, keepdims=True))
            s = jnp.concatenate([jnp.broadcast_to(x, t.shape) for x in (m, v, a, nrm)], -1)
            return s.reshape(t.shape[0], t.shape[1], -1)

        def _forward(hs, Wq, Wk, Wv, conv_q, conv_k, conv_v, Wb, fir_s, fir_m, fir_l, gW1, gb1, gW2, gb2, log_tau, eps_logit, norm_w, Wo):
            b, Ln, _ = hs.shape
            q = jax.nn.silu(_dwconv(hs @ Wq, conv_q))
            k = jax.nn.silu(_dwconv(hs @ Wk, conv_k))
            v = jax.nn.silu(_dwconv(hs @ Wv, conv_v))
            beta = jax.nn.sigmoid(hs @ Wb)
            bh = lambda t: jnp.transpose(t.reshape(b, Ln, H, -1), (0, 2, 1, 3))
            o_d, _ = _delta_rule_chunkwise(bh(q), bh(k), bh(v), jnp.transpose(beta, (0, 2, 1)))
            delta_path = jnp.transpose(o_d, (0, 2, 1, 3))
            paths = jnp.stack([_dwconv(v, fir_s).reshape(b, Ln, H, DV), _dwconv(v, fir_m).reshape(b, Ln, H, DV), _dwconv(v, fir_l).reshape(b, Ln, H, DV), delta_path, v.reshape(b, Ln, H, DV)], axis=3)
            stats_flat = jnp.concatenate([_stats(paths[..., p, :]) for p in range(P)], -1)
            gate_in = jnp.concatenate([hs, stats_flat], -1)
            logits = jax.nn.gelu(gate_in @ gW1 + gb1, approximate=False) @ gW2 + gb2
            logits = logits.reshape(b, Ln, H, P)
            tau = jax.nn.softplus(log_tau) + 0.5
            probs = jax.nn.softmax(logits / tau[:, None], -1)
            eps = jax.nn.sigmoid(eps_logit) * 0.2
            probs = probs * (1.0 - jnp.sum(eps, -1, keepdims=True)) + eps
            o = jnp.einsum('blhp,blhpd->blhd', probs, paths)
            o = o * jax.lax.rsqrt(jnp.mean(o * o, -1, keepdims=True) + 1e-05) * norm_w
            return o.reshape(b, Ln, D) @ Wo
        return _forward(hidden_states, Wq, Wk, Wv, conv_q, conv_k, conv_v, Wb, fir_s, fir_m, fir_l, gW1, gb1, gW2, gb2, log_tau, eps_logit, norm_w, Wo)

    def _L0_xattn_ref(k, v, q, Wk, Wv, bv, Wq, bq, Wo, bo):
        import jax, jax.numpy as jnp
        import numpy as np
        D_MODEL = 256
        B, S = (4, 512)
        kp = jnp.einsum('bsd,ed->bse', k, Wk)
        vp = jnp.einsum('bsd,ed->bse', v, Wv) + bv
        qp = jnp.einsum('bsd,ed->bse', q, Wq) + bq
        scale = 1.0 / jnp.sqrt(jnp.float32(kp.shape[-1]))
        scores = jnp.einsum('bqd,bkd->bqk', qp, kp) * scale
        probs = jax.nn.softmax(scores, axis=-1)
        ctx = jnp.einsum('bqk,bkd->bqd', probs, vp)
        return jnp.einsum('bqd,ed->bqe', ctx, Wo) + bo

    def _L0_ffn_ref(x, w_gate, w_up, w_down):
        import jax, jax.numpy as jnp
        import numpy as np
        DIM = 256
        HIDDEN = 768
        SCALE = 1.0 / 127.0

        def _dequant(w_int, dtype):
            return w_int.astype(dtype) * jnp.asarray(SCALE, dtype)
        wg = _dequant(w_gate, x.dtype)
        wu = _dequant(w_up, x.dtype)
        wd = _dequant(w_down, x.dtype)
        gate = jnp.einsum('bsd,hd->bsh', x, wg)
        up = jnp.einsum('bsd,hd->bsh', x, wu)
        h = jax.nn.silu(gate) * up
        return jnp.einsum('bsh,dh->bsd', h, wd)
    x = _layernorm(x + _L0_attn_ref(x, L0_attn_Wq, L0_attn_Wk, L0_attn_Wv, L0_attn_conv_q, L0_attn_conv_k, L0_attn_conv_v, L0_attn_Wb, L0_attn_fir_s, L0_attn_fir_m, L0_attn_fir_l, L0_attn_gW1, L0_attn_gb1, L0_attn_gW2, L0_attn_gb2, L0_attn_log_tau, L0_attn_eps_logit, L0_attn_norm_w, L0_attn_Wo), axis=-1)
    x = _layernorm(x + _L0_xattn_ref(ctx_1024, ctx_1024, x, L0_xattn_Wk, L0_xattn_Wv, L0_xattn_bv, L0_xattn_Wq, L0_xattn_bq, L0_xattn_Wo, L0_xattn_bo), axis=-1)
    x = _layernorm(x + _L0_ffn_ref(x, L0_ffn_w_gate, L0_ffn_w_up, L0_ffn_w_down), axis=-1)
    return x

_drawn_inputs = setup_inputs


def setup_inputs(seed=0):
    import zlib

    import numpy as np

    out = dict(_drawn_inputs(seed))
    spreads = {'L0_attn_gb1': (0.0, 2.0),
     'L0_attn_log_tau': (0.0, 2.0),
     'L0_attn_eps_logit': (0.0, 2.0),
     'L0_attn_norm_w': (1.0, 0.2),
     'L0_xattn_bv': (0.0, 0.1),
     'L0_xattn_bq': (0.0, 0.277),
     'L0_xattn_bo': (0.0, 0.1)}
    factors = {'L0_attn_gb2': 3.209, 'L0_attn_gW1': 6.95}
    for name, (base, spread) in spreads.items():
        noise = np.random.default_rng([zlib.crc32(name.encode()), seed]).standard_normal(out[name].shape)
        drawn = base * np.exp(spread * noise) if base else spread * noise
        out[name] = jnp.asarray(drawn.astype(out[name].dtype))
    for name, factor in factors.items():
        out[name] = (out[name] * factor).astype(out[name].dtype)
    return out
```

```python
from contextlib import ExitStack

import concourse.bass as bass
from concourse import mybir

F32 = mybir.dt.float32
I32 = mybir.dt.int32
ALU = mybir.AluOpType
ACT = mybir.ActivationFunctionType
AX = mybir.AxisListType

P = 128
NB, L, D, H = 4, 512, 256, 4
DV = D // H
CT = D // P
TOK = NB * L
TILES = TOK // P
TPB = L // P
C = 32
QC = P // C
NCHUNK = TOK // C
BLK = TOK // C
CONV_K = 4
FIRS = (3, 15, 64)
NF = len(FIRS)
HALO = 64
WIN = HALO + C
NPATH = 5
NKIND = 4
HF = 2 * D
S_CTX = 1601
KV = [min(P, S_CTX - P * i) for i in range(-(-S_CTX // P))]
HID = 768
FT = HID // P
LN_EPS = 1e-5


def sl(buf, p0, n, off, *dims):
    pitch = buf.ap[0][0]
    return bass.AP(buf.tensor, buf.offset + p0 * pitch + off, [[pitch, n]] + [[s, c] for s, c in dims])


def dr(x, off, *dims):
    return bass.AP(x.tensor, off, [[s, c] for s, c in dims])


def phase_one_order():
    steps = [(n, 0, "project", n) for n in range(6 * NB + 1)]
    for b in range(NB):
        t0 = 6 * (b + 1)
        for r in range(TPB):
            steps += [(t0 + 2 + r, 1, "turn", TPB * b + r), (t0 + 7 + r, 3, "turn_back", TPB * b + r),
                      (t0 + 8 + r, 4, "gram", TPB * b + r)]
        steps.append((t0 + 6, 2, "normalise", b))
    return [(kind, n) for _, _, kind, n in sorted(steps)]


def build(nc, a, out):
    with ExitStack() as ctx:
        WORDS = 53200
        arena = ctx.enter_context(nc.sbuf_tensor("arena", [P, WORDS], F32))
        ps = ctx.enter_context(nc.psum_tensor("ps", [P, 8, 512], F32))
        psv = ps[:, :, :].rearrange("p b n -> p (b n)")

        def sem(name):
            return ctx.enter_context(nc.semaphore(name))

        def at(start, n):
            assert start + n <= WORDS
            return arena[:, start:start + n]

        def bank(i, p0, n, off, *dims):
            return sl(psv, p0, n, 512 * i + off, *dims)

        ident = at(0, 128)
        mask_gram = at(128, 128)
        mask_heads = at(256, 128)
        eps_col = at(384, 4)
        conv_w = at(388, CT * 3 * CONV_K)
        beta = at(416, TILES * H)
        ss = at(480, TPB * 8)
        nrm = at(512, TPB * 8)
        rn = at(544, TPB * 8)
        vT = at(2048 + HALO, CT * TOK)
        kn = at(6656, TILES * D)
        vk = at(10752, TILES * H * 2 * DV)
        al = at(18944, TILES * CT * 4 * C)
        wq = at(23040, CT * NCHUNK * 2 * C)
        xT = at(31232, CT * TOK)
        o_tok = xT
        w_in = at(35328, CT * 3 * D)
        w_beta = at(36864, CT * H)
        y_buf = at(36880, 2 * L)
        qkT = at(37904, 2 * 2 * CT * L)
        raw = at(42000, TPB * 2 * D)
        sq = at(44048, 2 * D)
        qn = at(44688, TPB * D)
        knT = at(45712, 2 * CT * P)
        bd = at(46224, 2 * CT * 4 * P)
        a_row = at(48384, C * C)
        u_row = at(49408, C * C)
        u_tmp = at(50432, C * C)
        ubd = at(35328, 2 * 8 * H * P)
        state = at(43520, 2 * 4 * P)
        u_new = at(44544, 2 * 2 * 4 * P)

        SETS = 2
        s_const = sem("s_const")
        s_par = sem("s_par")
        s_x = [sem(f"s_x{b}") for b in range(NB)]
        s_win = sem("s_win")
        zeroed = sem("zeroed")
        beta_mm, beta_ready = sem("beta_mm"), sem("beta_ready")
        projected, tap_first, tap_step, conv_done, silu_done = (
            sem("projected"), sem("tap_first"), sem("tap_step"), sem("conv_done"), sem("silu_done"))
        kq_turned, v_turned = sem("kq_turned"), sem("v_turned")
        raw_done, ss_done, vb_done = sem("raw_done"), sem("ss_done"), sem("vb_done")
        sqrt_done, rn_done, kn_done, kb_done, qn_done = (
            sem("sqrt_done"), sem("rn_done"), sem("kn_done"), sem("kb_done"), sem("qn_done"))
        back_turned, back_act, back_dve, wq_q = sem("back_turned"), sem("back_act"), sem("back_dve"), sem("wq_q")
        gram_done, gram_masked = sem("gram_done"), sem("gram_masked")
        a_out, a_in, u_out, u_in = sem("a_out"), sem("a_in"), sem("u_out"), [sem(f"u_in{s}") for s in range(SETS)]
        u_init, solve_step, solved = sem("u_init"), sem("solve_step"), sem("solved")
        ubd_zero = sem("ubd_zero")
        uw_mm, uw_act, uw_dve = sem("uw_mm"), sem("uw_act"), sem("uw_dve")
        w_turned, w_act, w_dve = sem("w_turned"), sem("w_act"), sem("w_dve")
        state_zero = sem("state_zero")
        wq_mm = [sem(f"wq_mm{g}") for g in range(2)]
        u_ready = [sem(f"u_ready{g}") for g in range(2)]
        o_mm = [sem(f"o_mm{g}") for g in range(2)]
        s_mm = [sem(f"s_mm{g}") for g in range(2)]
        state_ready = [sem(f"state_ready{g}") for g in range(2)]
        o_kept = [sem(f"o_kept{g}") for g in range(2)]

        win = at(6656, CT * P * BLK)
        fir = at(35328, NF * C * P)
        taps_ring = at(47616, 3 * CT * 4 * C * NF)
        expand = at(49920, NPATH * P)
        w1_part = at(50560, NPATH * HF)
        w1_raw = at(35328, 2 * 8 * HF)
        v_blk = at(23040, C * P)
        oT = at(2112, CT * TOK)
        o_blk = at(31232, C * P)
        xT2 = at(27136, CT * TOK)
        st = at(640, C * 40)
        w2_sb = at(1920, 4 * 20)
        b1_col, gb2_row, tau_in, tau_inv = at(2000, 4), at(2004, 10), at(2014, 2), at(2016, 2)
        eps_row, eps_keep, tau_t, nw_col = at(2018, 10), at(2028, 2), at(2030, 4), at(2034, 1)
        sqt = at(2112, C * P)
        hT = at(6656, 4 * TOK)
        statsT = at(14848, TOK)
        w1_s = at(16896, HF)
        w1_x = at(17408, CT * HF)
        lT = at(18432, TOK)
        pr, lg, mx, sm, rs, r64 = at(640, 320), at(960, 320), at(1280, 64), at(1344, 64), at(1408, 64), at(1472, 64)
        mix = sl(fir, 0, P, 2 * C * P, (1, C * P))
        onT = xT2
        x1 = at(31232, TILES * D)
        x1T = at(27136, CT * TOK)
        w_o = at(20480, 512)
        x_q, x_k, x_v, x_oT = (at(35840 + 512 * i, 512) for i in range(4))
        w_qk, w_vo, b_vo = at(37888, 512), at(38400, 512), at(38912, 256)
        p_sb = at(39168, 2 * 1664)
        stage_i = at(20992, 1536)
        x2 = at(42496, TPB * D)
        hF = at(43520, FT * L)
        x2T = at(46592, CT * L)
        w_g, w_u, w_d = at(47616, 1536), at(49152, 1536), at(50688, 1536)
        bv_rep = at(52224, CT * P)
        sg = at(52480, 512)
        qk_sb = at(2048, CT * L)
        pcT = at(3072, CT * L)
        y_out = at(4096, TPB * D)
        ctx_n = at(6656, 2 * 13 * D)
        ctx_t = at(13312, 2 * CT * S_CTX)
        pT = at(19716, 13 * L)
        bn6, mv, rstd = at(388, 6), at(400, 32), at(432, 16)
        bqk, bq_col, bo_row = at(448, 2), at(450, 2), at(5120, 256)
        sm_max, sm_neg, sm_sum, sm_inv = at(456, 8), at(464, 8), at(472, 8), at(480, 8)
        mv2, rstd2 = at(488, 8), at(496, 4)
        bv_col = at(500, 2)
        sm_part = at(502, 4)

        win_mm, win_act, win_dve, win_fixed = sem("win_mm"), sem("win_act"), sem("win_dve"), sem("win_fixed")
        blk_mm, blk_act, blk_dve = sem("blk_mm"), sem("blk_act"), sem("blk_dve")
        fir_mm, fir_act = sem("fir_mm"), sem("fir_act")
        taps_in = [sem(f"taps_in{i}") for i in range(3)]
        w1_in = [sem(f"w1_in{i}") for i in range(2)]
        w1_add, w1x_in, xT2_in, gate_in = sem("w1_add"), sem("w1x_in"), sem("xT2_in"), sem("gate_in")
        par_act, par_dve = sem("par_act"), sem("par_dve")
        sq_ready, stat_abs, stat_sq, st_norm, st_ready = (
            sem("sq_ready"), sem("stat_abs"), sem("stat_sq"), sem("st_norm"), sem("st_ready"))
        statsT_zero, st_mm, st_act, st_dve = sem("statsT_zero"), sem("st_mm"), sem("st_act"), sem("st_dve")
        w1s_mm, w1s_ready, hid_mm, hid_act = sem("w1s_mm"), sem("w1s_ready"), sem("hid_mm"), sem("hid_act")
        lT_mm, lT_dve, lg_mm, gate_step, exp_done, pr_ready = (
            sem("lT_mm"), sem("lT_dve"), sem("lg_mm"), sem("gate_step"), sem("exp_done"), sem("pr_ready"))
        mix_pool, mix_dve, mix_sq, mix_sum, mix_sqrt, on_ready = (
            sem("mix_pool"), sem("mix_dve"), sem("mix_sq"), sem("mix_sum"), sem("mix_sqrt"), sem("on_ready"))
        on_mm, on_act, on_dve = sem("on_mm"), sem("on_act"), sem("on_dve")
        x_in = [sem(f"x_in{b}") for b in range(NB)]
        wts_in, wo_in, int_in, int_done = sem("wts_in"), sem("wo_in"), sem("int_in"), sem("int_done")
        wo_scaled, wo_mm, res1, bn, agg, sqrt1, rstd1, x1_ready = (
            sem("wo_scaled"), sem("wo_mm"), sem("res1"), sem("bn"), sem("agg"), sem("sqrt1"), sem("rstd1"), sem("x1_ready"))
        x1_mm, x1T_act, x1_bias = sem("x1_mm"), sem("x1T_act"), sem("x1_bias")
        fold_mm, fold_done, bvo_ready = sem("fold_mm"), sem("fold_done"), sem("bvo_ready")
        ctx_in = [sem(f"ctx_in{i}") for i in range(2)]
        scored, maxed, neg_ready, exped = sem("scored"), sem("maxed"), sem("neg_ready"), sem("exped")
        p_mm, p_kept = [sem(f"p_mm{i}") for i in range(2)], [sem(f"p_kept{i}") for i in range(2)]
        full, free = [sem(f"bank_full{i}") for i in range(2)], [sem(f"bank_free{i}") for i in range(2)]
        inv_ready, res2, sqrt2, rstd2_ready, x2_ready = (
            sem("inv_ready"), sem("res2"), sem("sqrt2"), sem("rstd2_ready"), sem("x2_ready"))
        mix_step, bv_ready = sem("mix_step"), sem("bv_ready")
        silu_g, h_ready, y_ready, stored = sem("silu_g"), sem("h_ready"), sem("y_ready"), sem("stored")

        PATHS = [sl(fir, 0, P, i * C * P, (1, C * P)) for i in range(NF)] + [o_blk, v_blk]
        STATS = [(4, 0), (4, 1), (3, 0), (3, 1)] + [(p, h) for h in range(2) for p in range(NF)]

        def fir_between(j):
            ends = (0, 2, 6, 10, 16, 20, 24, 32)
            return (ends[j - 1], ends[j]) if 0 < j < 8 else (0, 0)


        def tail_order():
            steps = []
            for b in range(NB + 1):
                if b < NB:
                    steps += [("qk", b, 0), ("qk", b, 1)]
                for r in range(TPB):
                    if b < NB:
                        steps.append(("scores", b, r))
                    if b:
                        steps += {0: [("post", b - 1, i) for i in range(TPB)],
                                  1: [("turn_x2", b - 1, 0), ("turn_x2", b - 1, 1)]
                                     + [(k, b - 1, m) for m in range(3) for k in ("gate", "up")],
                                  2: [(k, b - 1, m) for m in range(3, FT) for k in ("gate", "up")],
                                  3: [("down", b - 1, i) for i in range(TPB)]}[r]
                    if b < NB and r:
                        steps.append(("turn_p", b, r - 1))
                if b < NB:
                    steps.append(("turn_p", b, TPB - 1))
                    steps += [("pv", b, 0), ("pv", b, 1)]
            return steps

        TAIL = tail_order()
        MISC = {step: i for i, step in enumerate(x for x in TAIL if x[0] not in ("scores", "turn_p"))}

        def misc(*step):
            i = MISC[step]
            return 6 + i % 2, i // 2

        ORDER = phase_one_order()
        NPROJ = 6 * NB
        PROJ_V, PROJ_K, PROJ_Q = 0, 1, 2
        TPS = TILES // SETS
        STEPS = L // C

        def y_of(n):
            return sl(y_buf, 0, P, (n % 2) * L, (1, L))

        def silu_dst(n):
            b, j = divmod(n, 6)
            proj, ct = divmod(j, 2)
            if proj == PROJ_V:
                return sl(vT, 0, P, ct * TOK + b * L, (1, L))
            return sl(qkT, 0, P, ((b % 2) * 2 + proj - 1) * CT * L + ct * L, (1, L))

        def win_dst(n):
            ct, g = divmod(n, 16)
            return sl(win, 0, WIN, ct * P * BLK + 4 * g, (BLK, P), (1, 4))

        def blk_dst(n):
            k, i = divmod(n, 8)
            if k == 1:
                return sl(oT, 0, P, i * 2 * P, (P, 2), (TOK, CT), (1, P))
            return sl((v_blk, None, o_blk)[k], 0, P, i * 512, (1, 512))

        def blk_src(n):
            if n // 8 == 1:
                return bank(n % 4, 0, P, 0, (256, 2), (P, CT), (1, P))
            return bank(n % 4, 0, P, 0, (1, 512))

        def fir_dst(n):
            return sl(fir, 0, P, 4 * n, (P, C), (C * P, NF), (1, 4))

        def fir_src(n):
            return bank(6 + n % 2, 0, P, (C - 1) * NF, (-NF, C), (1, NF), (C * NF, 4))

        def stats_dst(n, ct):
            return sl(statsT, DV * ct, 40, 4 * n, (1, 4), (C, BLK))

        def on_dst(n):
            return sl(onT, 0, P, 4 * n, (1, 4), (TOK, CT), (C, BLK))

        def on_src(n):
            return bank(n % 4, 0, P, 0, (P, 4), (DV, CT), (1, DV))

        def p_dst(r, g):
            return sl(pT, 0, P, 4 * g * L + r * P, (L, 4), (1, P))

        block = ctx.enter_context(nc.Block())

        @block.sync
        def _(sp):
            sp.dma_start(sl(xT, 0, P, 0, (TOK, CT), (1, L)),
                         dr(a["xT"], 0, (TOK, P), (P * TOK, CT), (1, L))).then_inc(s_x[0], 16)
            for i, w in enumerate((a["Wv"], a["Wk"], a["Wq"])):
                sp.dma_start(sl(w_in, 0, P, i * D, (3 * D, CT), (1, D)),
                             w.rearrange("(c p) n -> p c n", p=P)).then_inc(s_win, 16)
            sp.dma_start(sl(w_beta, 0, P, 0, (H, CT), (1, H)),
                         a["Wb"].rearrange("(c p) n -> p c n", p=P)).then_inc(s_win, 16)
            for i, w in enumerate((a["conv_v"], a["conv_k"], a["conv_q"])):
                sp.dma_start(sl(conv_w, 0, P, i * CONV_K, (3 * CONV_K, CT), (1, CONV_K)),
                             w.rearrange("(c p) k -> p c k", p=P)).then_inc(s_const, 16)
            sp.dma_start(ident, a["ident"]).then_inc(s_const, 16)
            sp.dma_start(mask_gram, a["mask_gram"]).then_inc(s_const, 16)
            sp.dma_start(mask_heads, a["mask_heads"]).then_inc(s_const, 16)
            sp.dma_start(eps_col, a["eps"]).then_inc(s_const, 16)
            for b in range(1, NB):
                sp.dma_start(sl(xT, 0, P, b * L, (TOK, CT), (1, L)),
                             dr(a["xT"], b * L, (TOK, P), (P * TOK, CT), (1, L))).then_inc(s_x[b], 16)
            for ct in range(CT):
                half = (DV * ct, DV)
                sp.dma_start(sl(gb2_row, *half, 0, (1, 10)), dr(a["gb2"], 10 * ct, (0, DV), (1, 10))).then_inc(s_par, 16)
                sp.dma_start(sl(tau_in, *half, 0, (1, 2)), dr(a["log_tau"], 2 * ct, (0, DV), (1, 2))).then_inc(s_par, 16)
                sp.dma_start(sl(eps_row, *half, 0, (1, 10)), dr(a["eps_logit"], 10 * ct, (0, DV), (1, 10))
                             ).then_inc(s_par, 16)
                sp.dma_start(sl(nw_col, *half, 0, (1, 1)), a["norm_w"].rearrange("(a b) -> a b", b=1)).then_inc(s_par, 16)

            for s in range(SETS):
                sp.wait_ge(gram_masked, QC * TPS * (s + 1))
                for q in range(QC):
                    for h in range(2):
                        sp.dma_start(dr(a["scr_a"], s * P * C * C + (h * QC + q) * C * C,
                                        (C, C), (2 * QC * C * C, CT * TPS), (1, C)),
                                     sl(al, C * q, C, s * TPS * 256 + h * C, (P, CT * TPS), (1, C))).then_inc(a_out, 16)
                sp.wait_ge(a_out, 16 * 2 * QC * (s + 1))
                if s:
                    sp.wait_ge(solved, s)
                sp.dma_start(a_row, dr(a["scr_a"], s * P * C * C, (C * C, P), (1, C * C))).then_inc(a_in, 16)
                sp.wait_ge(solved, s + 1)
                sp.dma_start(dr(a["scr_u"], s * P * C * C, (C * C, P), (1, C * C)), u_row).then_inc(u_out, 16)
                sp.wait_ge(u_out, 16 * (s + 1))
                sp.wait_ge(ubd_zero, 1)
                for q in range(QC):
                    sp.dma_start(sl(ubd, C * q, C, s * TPS * H * P + C * q, (P, H * TPS), (1, C)),
                                 dr(a["scr_u"], s * P * C * C + q * C * C, (C, C), (QC * C * C, 4 * TPS), (1, C)),
                                 ).then_inc(u_in[s], 16)
            for s in range(SETS):
                sp.wait_ge(u_in[s], 16 * QC)
            sp.dma_start(sl(w2_sb, 0, P, 0, (20, 4), (1, 20)), a["gW2"].rearrange("(m p) n -> p m n", p=P)).then_inc(gate_in, 16)
            sp.dma_start(b1_col, a["gb1"]).then_inc(gate_in, 16)
            sp.dma_start(expand, a["expand"]).then_inc(gate_in, 16)

            def load_taps(n):
                if n >= 3:
                    sp.wait_ge(fir_mm, n - 2)
                for ct in range(CT):
                    sp.dma_start(sl(taps_ring, 0, WIN, (n % 3) * 768 + ct * 384, (96, 4), (1, 96)),
                                 dr(a["taps"], (ct * P + 4 * n) * NF * (WIN + C - 1),
                                    (NF, WIN), (NF * (WIN + C - 1), 4), (1, C * NF))).then_inc(taps_in[n % 3], 16)

            for n in range(3):
                load_taps(n)
            for n in range(3, 32):
                load_taps(n)
            sp.wait_ge(win_mm, 1)
            sp.dma_start(sl(xT2, 0, P, 0, (TOK, CT), (1, TOK)), a["xT"].rearrange("(c p) n -> p c n", p=P)).then_inc(xT2_in, 16)
            sp.wait_ge(fir_mm, 32)
            sp.dma_start(sl(w1_x, 0, P, 0, (HF, CT), (1, HF)), a["gW1"][0:D, :].rearrange("(c p) n -> p c n", p=P)).then_inc(w1x_in, 16)
            sp.dma_start(sl(w_o, 0, P, 0, (D, CT), (1, D)), a["Wo"].rearrange("(c p) n -> p c n", p=P)).then_inc(wo_in, 16)
            sp.wait_ge(w1s_mm, 1)
            for i, (name, w) in enumerate((("wgT", w_g), ("wuT", w_u), ("wdT", w_d))):
                if i:
                    sp.wait_ge(int_done, i)
                n = a[name].shape[1]
                sp.dma_start(sl(stage_i, 0, P, 0, (n, 1536 // n), (1, n)).bitcast(I32),
                             a[name].rearrange("(c p) n -> p c n", p=P)).then_inc(int_in, 16)
            sp.wait_ge(mix_dve, 6)
            for w, name in ((x_q, "xWq"), (x_k, "xWk"), (x_v, "xWv"), (x_oT, "xWoT")):
                sp.dma_start(sl(w, 0, P, 0, (D, CT), (1, D)), a[name].rearrange("(c p) n -> p c n", p=P)).then_inc(wts_in, 16)
            sp.dma_start(bq_col, a["xbq"]).then_inc(wts_in, 16)
            sp.dma_start(bv_col, a["xbv"]).then_inc(wts_in, 16)
            sp.wait_ge(mix_sum, 1)
            sp.dma_start(bo_row, dr(a["xbo"], 0, (0, P), (1, D))).then_inc(wts_in, 16)
            for t in range(0, TILES, TPB):
                sp.dma_start(sl(x1, 0, P, t * D, (D, TPB), (1, D)),
                             dr(a["x"], t * P * D, (D, P), (P * D, TPB), (1, D))).then_inc(x_in[t // TPB], 16)

            def load_ctx(b):
                n = S_CTX // P
                if b == 0:
                    sp.wait_ge(lg_mm, 1)
                if b >= 2:
                    bk, i = misc("pv", b - 2, 1)
                    sp.wait_ge(full[bk - 6], i + 1)
                sp.dma_start(sl(ctx_t, 0, P, (b % 2) * CT * S_CTX, (S_CTX, CT), (1, S_CTX)),
                             dr(a["ctxT"], b * D * S_CTX, (S_CTX, P), (P * S_CTX, CT), (1, S_CTX))
                             ).then_inc(ctx_in[b % 2], 16)
                sp.dma_start(sl(ctx_n, 0, P, (b % 2) * 13 * D, (D, n), (1, D)),
                             dr(a["ctx"], b * S_CTX * D, (D, P), (P * D, n), (1, D))).then_inc(ctx_in[b % 2], 16)
                sp.dma_start(sl(ctx_n, 0, S_CTX - n * P, ((b % 2) * 13 + n) * D, (1, D)),
                             dr(a["ctx"], (b * S_CTX + n * P) * D, (D, S_CTX - n * P), (1, D))
                             ).then_inc(ctx_in[b % 2], 16)

            load_ctx(0)
            load_ctx(1)
            load_ctx(2)
            load_ctx(3)
            for b in range(NB):
                sp.wait_ge(y_ready, TPB * (b + 1))
                sp.dma_start(dr(out, b * L * D, (D, P), (P * D, TPB), (1, D)),
                             sl(y_out, 0, P, 0, (D, TPB), (1, D))).then_inc(stored, 16)
            sp.wait_ge(stored, 16 * NB)

        @block.gpsimd
        def _(pool):
            pool.memset(sl(vT, 0, P, -HALO, (1, HALO)), 0.0).then_inc(zeroed, 1)
            pool.memset(bd, 0.0).then_inc(zeroed, 1)

            def normalise(b):
                pool.wait_ge(rn_done, b + 1)
                pool.wait_ge(zeroed, 2)
                pool.wait_ge(u_init, 2)
                if b:
                    pool.wait_ge(back_turned, TPB * b)
                    pool.wait_ge(wq_q, 2 * TPB * b)
                pool.tensor_tensor(sl(qn, 0, P, 0, (D, TPB), (DV, H), (1, DV)),
                                   sl(raw, 0, P, D, (2 * D, TPB), (DV, H), (1, DV)),
                                   sl(rn, 0, P, H, (8, TPB), (1, H), (0, DV)), ALU.mult).then_inc(qn_done, 1)

            def turn_back(t):
                pool.wait_ge(back_act, t + 1)
                pool.wait_ge(back_dve, t + 1)
                for h in range(2):
                    pool.wait_ge(qn_done, (t // TPB) + 1)
                    if t or h:
                        pool.wait_ge(wq_q, 2 * t + h)
                    pool.tensor_copy(
                        sl(wq, DV * h, DV, t * QC * 2 * C + C, (NCHUNK * 2 * C, CT), (2 * C, QC), (1, C)),
                        sl(bd, DV * h, DV, (t % 2) * CT * 512 + 256 + h * P, (512, CT), (C, QC), (1, C))
                        ).then_inc(wq_q, 1)

            def start_solver():
                pool.memset(u_row, 0.0).then_inc(u_init, 1)
                pool.wait_ge(u_init, 1)
                pool.memset(sl(u_row, 0, P, 0, (C + 1, C)), 1.0).then_inc(u_init, 1)

            start_solver()
            for kind, n in ORDER:
                if kind == "normalise":
                    normalise(n)
                elif kind == "turn_back":
                    turn_back(n)
            pool.wait_ge(gram_done, TILES)
            pool.wait_ge(silu_done, NPROJ)
            pool.wait_ge(wq_q, 2 * TILES)
            pool.memset(ubd, 0.0).then_inc(ubd_zero, 1)
            pool.memset(state, 0.0).then_inc(state_zero, 1)
            pool.wait_ge(u_out, 16)
            pool.memset(u_row, 0.0).then_inc(u_init, 1)
            pool.wait_ge(u_init, 3)
            pool.memset(sl(u_row, 0, P, 0, (C + 1, C)), 1.0).then_inc(u_init, 1)

            pool.wait_ge(w_turned, TILES)
            pool.wait_ge(solved, SETS)
            pool.wait_ge(u_out, 16 * SETS)

            def load_w1(p):
                pool.dma_start(sl(w1_raw, 0, P, (p % 2) * 8 * HF, (1, 8 * HF)),
                               dr(a["gW1"], (D + p * 1024) * HF, (8 * HF, P), (1, 8 * HF))).then_inc(w1_in[p % 2], 16)

            load_w1(0)
            load_w1(1)
            adds = 0
            for p in range(NPATH):
                pool.wait_ge(w1_in[p % 2], 16 * (p // 2 + 1))
                r0 = (p % 2) * 8 * HF
                for n in (4, 2, 1):
                    if adds:
                        pool.wait_ge(w1_add, adds)
                    x = sl(w1_raw, 0, P, r0, (1, n * HF))
                    y = x if n > 1 else sl(w1_part, 0, P, p * HF, (1, HF))
                    pool.tensor_tensor(y, x, sl(w1_raw, 0, P, r0 + n * HF, (1, n * HF)), ALU.add).then_inc(w1_add, 1)
                    adds += 1
                if p + 2 < NPATH:
                    pool.wait_ge(w1_add, adds)
                    load_w1(p + 2)

            pool.wait_ge(w1_add, adds)
            pool.wait_ge(win_act, 16)
            pool.wait_ge(win_dve, 16)
            pool.memset(sl(win, 0, HALO, 0, (BLK, CT * P), (BLK // NB, NB)), 0.0).then_inc(win_fixed, 1)
            pool.wait_ge(win_fixed, 1)
            pool.memset(sl(win, 0, C, 1, (BLK, CT * P), (BLK // NB, NB)), 0.0).then_inc(win_fixed, 1)
            pool.wait_ge(win_fixed, 2)
            pool.wait_ge(fir_mm, 32)
            pool.memset(statsT, 0.0).then_inc(statsT_zero, 1)

            pool.wait_ge(statsT_zero, 1)
            pool.wait_ge(wo_in, 16)
            pool.wait_ge(s_par, 16 * 8)
            pool.tensor_scalar(w_o, w_o, nw_col, None, ALU.mult).then_inc(wo_scaled, 1)
            pool.wait_ge(wo_scaled, 1)
            for i, w in enumerate((w_g, w_u, w_d)):
                pool.wait_ge(int_in, 16 * (i + 1))
                if i:
                    pool.wait_ge(int_done, i)
                pool.tensor_scalar(w, stage_i.bitcast(I32), 1.0 / 127.0, None, ALU.mult).then_inc(int_done, 1)
            pool.wait_ge(int_done, 3)

            pool.wait_ge(pr_ready, 1)
            pool.wait_ge(statsT_zero, 1)
            for p in range(2):
                if p:
                    pool.wait_ge(mix_pool, p)
                x = sl(PATHS[p], 0, P, 0, (DV, 2 * C), (1, DV))
                pool.tensor_tensor(x, x, sl(pr, 0, P, p, (NPATH, 2 * C), (0, DV)), ALU.mult).then_inc(mix_pool, 1)
            pool.wait_ge(mix_pool, 2)
            pool.tensor_tensor(PATHS[0], PATHS[0], PATHS[1], ALU.add).then_inc(mix_pool, 1)
            pool.wait_ge(mix_pool, 3)

            pool.wait_ge(bvo_ready, 1)
            for b in range(NB):
                pool.wait_ge(x1_mm, 2 * (b + 1))
                if b:
                    pool.wait_ge(x1_bias, b)
                x = sl(x1, 0, P, b * TPB * D, (D, TPB), (1, D))
                pool.tensor_tensor(x, x, sl(b_vo, 0, P, 0, (0, TPB), (1, D)), ALU.add).then_inc(x1_bias, 1)

        @block.scalar
        def _(act):
            def silu(n):
                act.wait_ge(conv_done, n + 1)
                b, j = divmod(n, 6)
                if j >= 2 and b >= 2:
                    act.wait_ge(kq_turned, TPB * (b - 1))
                if n == 0:
                    act.wait_ge(zeroed, 1)
                act.activation(silu_dst(n), y_of(n), ACT.Silu).then_inc(silu_done, 1)

            def project(n):
                if n < NPROJ:
                    b, j = divmod(n, 6)
                    proj, ct = divmod(j, 2)
                    act.wait_ge(projected, n + 1)
                    if n >= 2:
                        act.wait_ge(silu_done, n - 1)
                    act.activation(y_of(n), bank(n % 2, 0, P, 0, (1, L)), ACT.Copy,
                                   scale=sl(conv_w, 0, P, ct * 12 + proj * CONV_K + CONV_K - 1, (1, 1))
                                   ).then_inc(tap_first, 1)
                if n:
                    silu(n - 1)

            def turn(t):
                b, r = divmod(t, TPB)
                if t == 0:
                    act.wait_ge(beta_mm, 1)
                    act.activation(beta, bank(7, 0, P, 0, (1, TILES * H)), ACT.Sigmoid).then_inc(beta_ready, 1)
                act.wait_ge(kq_turned, t + 1)
                if b and r == 0:
                    act.wait_ge(kn_done, b)
                    act.wait_ge(qn_done, b)
                act.activation(sl(raw, 0, P, r * 2 * D, (1, 2 * D)), bank(2, 0, P, 0, (1, 512)), ACT.Copy)
                if t:
                    act.wait_ge(ss_done, t)
                act.activation(sq, bank(2, 0, P, 0, (1, 512)), ACT.Square).then_inc(raw_done, 1)

            def normalise(b):
                act.wait_ge(ss_done, TPB * (b + 1))
                if b:
                    act.wait_ge(rn_done, b)
                act.activation(nrm, ss, ACT.Sqrt, bias=sl(eps_col, 0, P, 0, (1, 1))).then_inc(sqrt_done, 1)

            def turn_back(t):
                act.wait_ge(back_turned, t + 1)
                if t >= 2:
                    act.wait_ge(gram_done, t - 1)
                    act.wait_ge(wq_q, 2 * (t - 1))
                if t == 0:
                    act.wait_ge(zeroed, 2)
                act.activation(sl(knT, 0, P, (t % 2) * CT * P, (1, CT * P)), bank(4, 0, P, 0, (1, CT * P)), ACT.Copy)
                act.activation(sl(bd, 0, DV, (t % 2) * CT * 512, (256, 2 * CT), (1, P)),
                               bank(5, 0, DV, 0, (P, 2 * CT), (1, P)), ACT.Copy).then_inc(back_act, 1)

            act.wait_ge(s_const, 16 * 7)
            for kind, n in ORDER:
                if kind == "project":
                    project(n)
                elif kind == "turn":
                    turn(n)
                elif kind == "normalise":
                    normalise(n)
                elif kind == "turn_back":
                    turn_back(n)

            for t in range(TILES + 1):
                if t < TILES and t % 2 == 0:
                    act.wait_ge(uw_mm, t + 1)
                    act.activation(sl(vk, 0, P, t * 512, (D, 2), (DV, H), (1, DV)), bank(0, 0, P, 0, (DV, 2), (P, H), (1, DV)), ACT.Copy
                                   ).then_inc(uw_act, 1)
                if t and t % 2 == 0:
                    act.wait_ge(w_turned, t)
                    act.activation(sl(wq, 0, P, (t - 1) * QC * 2 * C, (NCHUNK * 2 * C, CT), (2 * C, QC), (1, C)),
                                   bank(3, 0, P, 0, (P, CT), (C, QC), (1, C)), ACT.Copy).then_inc(w_act, 1)
            for n in range(STEPS):
                g, q = divmod(n, QC)
                for s in range(SETS):
                    act.wait_ge(o_mm[s], n + 1)
                    act.activation(sl(o_tok, C * q, C, (s * TPS + g) * D, (TPB * D, 2), (1, D)),
                                   bank(2 * s + n % 2, C, C, 0, (D, 2), (1, D)), ACT.Copy).then_inc(o_kept[s], 1)

            for n in range(0, 32, 2):
                act.wait_ge(win_mm, n + 1)
                act.activation(win_dst(n), bank(n % 4, 0, WIN, 0, (1, P), (P, 4)), ACT.Copy).then_inc(win_act, 1)
            for n in range(0, 24, 2):
                act.wait_ge(blk_mm, n + 1)
                act.activation(blk_dst(n), blk_src(n), ACT.Copy).then_inc(blk_act, 1)
            act.wait_ge(blk_act, 12)
            act.wait_ge(blk_dve, 12)
            for j, (p, h) in enumerate(STATS):
                if j < 2:
                    pass
                else:
                    act.wait_ge(stat_sq, j - 1)
                for n in range(*fir_between(j)):
                    act.wait_ge(fir_mm, n + 1)
                    act.activation(fir_dst(n), fir_src(n), ACT.Copy).then_inc(fir_act, 1)
                if p < NF:
                    act.wait_ge(fir_act, 16 * (h + 1))
                act.activation(sl(sqt, 0, P, (j % 2) * C * DV, (DV, C), (1, DV)), sl(PATHS[p], 0, P, h * DV, (P, C), (1, DV)),
                               ACT.Square).then_inc(sq_ready, 1)
            act.wait_ge(stat_sq, 2 * NPATH)
            act.activation(sl(st, 0, P, 3, (4, 320)), sl(st, 0, P, 1, (4, 320)), ACT.Sqrt).then_inc(st_norm, 1)
            act.wait_ge(par_dve, 2)
            act.activation(tau_inv, tau_t[:, 0:2], ACT.Exp, scale=-1.0).then_inc(par_act, 1)
            act.wait_ge(par_act, 1)
            act.activation(tau_t[:, 2:4], tau_inv, ACT.Ln, bias=1.0).then_inc(par_act, 1)
            act.activation(eps_row, eps_row, ACT.Sigmoid).then_inc(par_act, 1)
            act.wait_ge(statsT_zero, 1)
            for n in range(0, 8, 2):
                act.wait_ge(st_mm, n + 1)
                for ct in range(CT):
                    last = act.activation(stats_dst(n, ct), bank(4 + n % 4, 0, 40, ct * DV, (P, 4), (1, DV)), ACT.Copy)
                last.then_inc(st_act, 1)
            for n in range(16):
                b, m = divmod(n, 4)
                act.wait_ge(hid_mm, n + 1)
                act.activation(sl(hT, 0, P, m * TOK + b * L, (1, L)), bank(n % 4, 0, P, 0, (1, L)), ACT.Gelu,
                               bias=b1_col[:, m:m + 1]).then_inc(hid_act, 1)
            act.wait_ge(gate_step, 3)
            act.activation(pr, lg, ACT.Exp).then_inc(exp_done, 1)
            act.wait_ge(mix_dve, 6)
            act.activation(sqt, mix, ACT.Square).then_inc(mix_sq, 1)
            act.wait_ge(mix_sum, 1)
            act.activation(rs, r64, ACT.Sqrt, bias=eps_col[:, 1:2], scale=1.0 / DV).then_inc(mix_sqrt, 1)
            for n in range(0, 8, 2):
                act.wait_ge(on_mm, n + 1)
                act.activation(on_dst(n), on_src(n), ACT.Copy).then_inc(on_act, 1)

            for b in range(NB):
                act.wait_ge(agg, TPB * (b + 1))
                act.activation(rstd[:, TPB * b:TPB * b + TPB], sl(mv, 0, P, 2 * TPB * b + 1, (2, TPB)), ACT.Sqrt,
                               bias=eps_col[:, 1:2]).then_inc(sqrt1, 1)
            for i, w in enumerate((w_qk, w_vo)):
                act.wait_ge(fold_mm, i + 1)
                act.activation(w, bank(6 + i, 0, P, 0, (1, 512)), ACT.Copy).then_inc(fold_done, 1)
            act.wait_ge(fold_mm, 3)
            act.activation(bqk, bank(4, 0, P, 0, (1, 2)), ACT.Copy).then_inc(fold_done, 1)

            for n in range(8):
                act.wait_ge(x1_mm, n + 1)
                act.activation(sl(x1T, 0, P, n * 256, (P, 2), (TOK, CT), (1, P)),
                               bank(n % 4, 0, P, 0, (256, 2), (P, CT), (1, P)), ACT.Copy).then_inc(x1T_act, 1)

            def filled(*step):
                bk, i = misc(*step)
                act.wait_ge(full[bk - 6], i + 1)
                return bk, free[bk - 6]

            p_jobs = [0]
            for kind, b, i in TAIL:
                if kind == "qk":
                    bk, done = filled(kind, b, i)
                    act.activation(sl(qk_sb, 0, P, i * L, (1, L)), bank(bk, 0, P, 0, (1, L)), ACT.Identity,
                                   bias=bqk[:, i:i + 1]).then_inc(done, 1)
                elif kind == "scores":
                    n = TPB * b + i
                    act.wait_ge(neg_ready, n + 1)
                    if n >= 2:
                        act.wait_ge(p_mm[1], 2 * (n - 1))
                    act.activation(sl(p_sb, 0, P, (n % 2) * 1664, (1, S_CTX)), bank(0, 0, P, 0, (1, S_CTX)), ACT.Exp,
                                   bias=sl(sm_neg, 0, P, n % 8, (1, 1)), scale=1.0 / 16.0,
                                   accum_out=sl(sm_sum, 0, P, n % 8, (1, 1))).then_inc(exped, 1)
                elif kind == "turn_p":
                    n = TPB * b + i
                    for g in (0, 2):
                        act.wait_ge(p_mm[0], 2 * n + g // 2 + 1)
                        act.activation(p_dst(i, g), bank(4, 0, P, 0, (P, 4), (1, P)), ACT.Copy).then_inc(p_kept[0], 1)
                elif kind == "pv":
                    bk, done = filled(kind, b, i)
                    act.activation(sl(pcT, 0, P, i * L, (1, L)), bank(bk, 0, P, 0, (1, L)), ACT.Copy).then_inc(done, 1)
                elif kind == "turn_x2":
                    bk, done = filled(kind, b, i)
                    act.activation(sl(x2T, 0, P, i * 256, (P, 2), (L, CT), (1, P)),
                                   bank(bk, 0, P, 0, (256, 2), (P, CT), (1, P)), ACT.Copy).then_inc(done, 1)
                elif kind == "gate":
                    bk, done = filled(kind, b, i)
                    if FT * b + i:
                        act.wait_ge(h_ready, FT * b + i)
                    act.activation(sg, bank(bk, 0, P, 0, (1, L)), ACT.Silu).then_inc(silu_g, 1)
                    act.wait_ge(silu_g, FT * b + i + 1)
                    act.sem_inc(done, 1)
                if kind in ("post", "down") and i == TPB - 1:
                    k = 2 * b + (kind == "down")
                    act.wait_ge(agg, TILES + TPB * (k + 1))
                    act.activation(rstd2, sl(mv2, 0, P, 1, (2, TPB)), ACT.Sqrt, bias=eps_col[:, 1:2]).then_inc(sqrt2, 1)

        @block.tensor
        def _(pe):
            def betas():
                for b in range(NB):
                    pe.wait_ge(s_x[b], 16)
                for t in range(TILES):
                    for ct in range(CT):
                        last = pe.matmul(bank(7, 0, P, t * H, (1, H)), sl(xT, 0, P, ct * TOK + t * P, (1, P)),
                                         sl(w_beta, 0, P, ct * H, (1, H)), start=(ct == 0), stop=(ct == CT - 1))
                last.then_inc(beta_mm, 1)

            def project(n):
                if n >= NPROJ:
                    return
                b, j = divmod(n, 6)
                proj, ct = divmod(j, 2)
                if j == 0:
                    pe.wait_ge(s_x[b], 16)
                if n >= 2:
                    pe.wait_ge(conv_done, n - 1)
                for k in range(CT):
                    last = pe.matmul(bank(n % 2, 0, P, 0, (1, L)),
                                     sl(w_in, 0, P, k * 3 * D + proj * D + ct * P, (1, P)),
                                     sl(xT, 0, P, k * TOK + b * L, (1, L)), start=(k == 0), stop=(k == CT - 1))
                last.then_inc(projected, 1)

            def turn(t):
                b, r = divmod(t, TPB)
                if t == 0:
                    betas()
                    pe.wait_ge(s_const, 16 * 7)
                pe.wait_ge(silu_done, 6 * (b + 1))
                if t:
                    pe.wait_ge(raw_done, t)
                for kq in range(2):
                    for ct in range(CT):
                        last = pe.transpose(bank(2, 0, P, kq * D + ct * P, (1, P)),
                                            sl(qkT, 0, P, ((b % 2) * 2 + kq) * CT * L + ct * L + r * P, (1, P)), ident)
                last.then_inc(kq_turned, 1)
                if t:
                    pe.wait_ge(vb_done, t)
                for ct in range(CT):
                    last = pe.transpose(bank(3, 0, P, ct * P, (1, P)),
                                        sl(vT, 0, P, ct * TOK + t * P, (1, P)), ident)
                last.then_inc(v_turned, 1)

            def turn_back(t):
                b, r = divmod(t, TPB)
                pe.wait_ge(kb_done, b + 1)
                pe.wait_ge(qn_done, b + 1)
                if t:
                    pe.wait_ge(back_act, t)
                    pe.wait_ge(back_dve, t)
                for ct in range(CT):
                    pe.transpose(bank(4, 0, P, ct * P, (1, P)), sl(kn, 0, P, t * D + ct * P, (1, P)), ident)
                    pe.transpose(bank(5, 0, P, ct * 256, (1, P)),
                                 sl(vk, 0, P, t * 512 + D + ct * P, (1, P)), ident)
                    last = pe.transpose(bank(5, 0, P, ct * 256 + P, (1, P)),
                                        sl(qn, 0, P, r * D + ct * P, (1, P)), ident)
                last.then_inc(back_turned, 1)

            def gram(t):
                pe.wait_ge(back_act, t + 1)
                pe.wait_ge(back_dve, t + 1)
                if t:
                    pe.wait_ge(gram_masked, QC * t)
                for ct in range(CT):
                    last = pe.matmul(bank(6 + ct, 0, P, 0, (1, 512)), sl(knT, 0, P, ((t % 2) * CT + ct) * P, (1, P)),
                                     sl(bd, 0, P, ((t % 2) * CT + ct) * 512, (1, 512)), start=True, stop=True)
                last.then_inc(gram_done, 1)

            pe.wait_ge(s_win, 16 * 4)
            for kind, n in ORDER:
                if kind == "project":
                    project(n)
                elif kind == "turn":
                    turn(n)
                elif kind == "turn_back":
                    if n == 0:
                        pe.wait_ge(beta_ready, 1)
                    turn_back(n)
                elif kind == "gram":
                    gram(n)

            def make_uw(t):
                s = t // TPS
                pe.wait_ge(u_in[s], 16 * QC)
                if t == 0:
                    pe.wait_ge(conv_done, NPROJ)
                    pe.wait_ge(raw_done, TILES)
                    pe.wait_ge(vb_done, TILES)
                if t >= 2:
                    pe.wait_ge((uw_act, uw_dve)[t % 2], t // 2)
                for h in range(H):
                    last = pe.matmul(bank(t % 2, 0, P, h * P, (1, P)), sl(ubd, 0, P, (t * H + h) * P, (1, P)),
                                     sl(vk, 0, P, t * 512 + h * DV, (D, 2), (1, DV)), start=True, stop=True)
                last.then_inc(uw_mm, 1)

            def turn_w(t):
                pe.wait_ge((uw_act, uw_dve)[t % 2], t // 2 + 1)
                if t >= 2:
                    pe.wait_ge((w_dve, w_act)[t % 2], t // 2)
                for ct in range(CT):
                    last = pe.transpose(bank(2 + t % 2, 0, P, ct * P, (1, P)),
                                        sl(vk, 0, P, t * 512 + D + ct * P, (1, P)), ident)
                last.then_inc(w_turned, 1)

            for t in range(TILES + 1):
                if t < TILES:
                    make_uw(t)
                if t:
                    turn_w(t - 1)

            def scan_in(n, s):
                g, q = divmod(n, QC)
                if n == 0:
                    pe.wait_ge(w_act, TILES // 2)
                    pe.wait_ge(w_dve, TILES // 2)
                    pe.wait_ge(uw_act, TILES // 2)
                    pe.wait_ge(uw_dve, TILES // 2)
                    pe.wait_ge(wq_q, 2 * TILES)
                    pe.wait_ge(state_zero, 1)
                    pe.wait_ge(gram_masked, QC * TILES)
                else:
                    pe.wait_ge(state_ready[s], n)
                if n >= 2:
                    pe.wait_ge(o_kept[s], n - 1)
                for i in range(4):
                    b, ct = divmod(i, CT)
                    chunk = (s * TPS + b * TPB + g) * QC + q
                    last = pe.matmul(bank(2 * s + n % 2, 0, 2 * C, i * P, (1, P)),
                                     sl(wq, 0, P, (ct * NCHUNK + chunk) * 2 * C, (1, 2 * C)),
                                     sl(state, 0, P, (s * 4 + i) * P, (1, P)), start=(i == 0), stop=(i == 3),
                                     skip_group_check=True)
                last.then_inc(wq_mm[s], 1)

            def scan_out(n, s):
                g, q = divmod(n, QC)
                pe.wait_ge(u_ready[s], n + 1)
                for i in range(4):
                    b, ct = divmod(i, CT)
                    t = s * TPS + b * TPB + g
                    for h in range(2):
                        last = pe.matmul(bank(2 * s + n % 2, C, C, i * P + h * DV, (1, DV)),
                                         sl(al, C * q, C, ((t * CT + ct) * 4 + 2 + h) * C, (1, C)),
                                         sl(u_new, C * q, C, (s * 2 + n % 2) * 512 + i * P + h * DV, (1, DV)),
                                         start=False, stop=True, skip_group_check=True)
                last.then_inc(o_mm[s], 1)
                if n == STEPS - 1:
                    return
                for i in range(4):
                    b, ct = divmod(i, CT)
                    t = s * TPS + b * TPB + g
                    last = pe.matmul(bank(4 + s, 0, P, i * P, (1, P)), sl(kn, C * q, C, t * D + ct * P, (1, P)),
                                     sl(u_new, C * q, C, (s * 2 + n % 2) * 512 + i * P, (1, P)),
                                     start=(n == 0 and i == 0), stop=True, skip_group_check=True)
                last.then_inc(s_mm[s], 1)

            for n in range(STEPS):
                for s in range(SETS):
                    scan_in(n, s)
                for s in range(SETS):
                    scan_out(n, s)

            def ring(n, n_before, by_act, by_dve):
                if n >= 4:
                    pe.wait_ge((by_act, by_dve)[n % 2], (n - 4) // 2 + 1)

            for s in range(SETS):
                pe.wait_ge(o_kept[s], STEPS)
            for n in range(32):
                ct, g = divmod(n, 16)
                ring(n, 0, win_act, win_dve)
                for w in range(4):
                    last = pe.transpose(bank(n % 4, 0, WIN, w * P, (1, P)),
                                        sl(vT, 0, P, ct * TOK + (4 * g + w) * C - HALO, (1, WIN)), ident)
                last.then_inc(win_mm, 1)
            for n in range(24):
                k, i = divmod(n, 8)
                if n < 4:
                    pe.wait_ge((win_act, win_dve)[n % 2], 16)
                ring(n, 0, blk_act, blk_dve)
                if k == 1 and i == 0:
                    pass
                if k == 2:
                    pe.wait_ge(blk_act, 8)
                    pe.wait_ge(blk_dve, 8)
                for w in range(4):
                    if k == 1:
                        src = sl(o_tok, 0, P, i * 512 + w * P, (1, P))
                    else:
                        src = sl((vT, None, oT)[k], 0, P, 4 * i + w, (C, P))
                    last = pe.transpose(bank(n % 4, 0, P, w * P, (1, P)), src, ident)
                last.then_inc(blk_mm, 1)

            pe.wait_ge(win_fixed, 2)
            for n in range(32):
                pe.wait_ge(taps_in[n % 3], 32 * (n // 3 + 1))
                if n >= 2:
                    pe.wait_ge(fir_act, n - 1)
                for c in range(4):
                    for ct in range(CT):
                        last = pe.matmul(bank(6 + n % 2, DV * ct, DV, c * 96, (1, 96)),
                                         sl(win, 0, WIN, (ct * P + 4 * n + c) * BLK, (1, BLK)),
                                         sl(taps_ring, 0, WIN, (n % 3) * 768 + ct * 384 + c * 96, (1, 96)),
                                         start=True, stop=True, skip_group_check=True)
                last.then_inc(fir_mm, 1)

            pe.wait_ge(w1_add, 3 * NPATH)
            pe.wait_ge(gate_in, 48)
            for p in range(NPATH):
                last = pe.matmul(bank(4, 0, P, 0, (1, HF)), sl(expand, 0, P, p * P, (1, P)),
                                 sl(w1_part, 0, P, p * HF, (1, HF)), start=(p == 0), stop=(p == NPATH - 1))
            last.then_inc(w1s_mm, 1)
            def hidden_x(n):
                b, m = divmod(n, 4)
                for k in range(CT):
                    pe.matmul(bank(n % 4, 0, P, 0, (1, L)), sl(w1_x, 0, P, k * HF + m * P, (1, P)),
                              sl(xT2, 0, P, k * TOK + b * L, (1, L)), start=(k == 0), stop=False)

            pe.wait_ge(w1x_in, 16)
            pe.wait_ge(xT2_in, 16)
            for n in range(4):
                hidden_x(n)
            pe.wait_ge(st_ready, 1)
            pe.wait_ge(w1s_ready, 1)
            pe.wait_ge(fir_act, 32)
            for n in range(8):
                ring(n, 0, st_act, st_dve)
                for w in range(4):
                    last = pe.transpose(bank(4 + n % 4, 0, 40, w * P, (1, P)), sl(st, 0, P, (4 * n + w) * 40, (1, 40)), ident)
                last.then_inc(st_mm, 1)
            pe.wait_ge(st_act, 4)
            pe.wait_ge(st_dve, 4)
            for n in range(16):
                b, m = divmod(n, 4)
                if n >= 4:
                    pe.wait_ge(hid_act, n - 3)
                    hidden_x(n)
                pe.matmul(bank(n % 4, 0, P, 0, (1, L)), sl(w1_s, 0, P, m * P, (1, P)),
                          sl(statsT, 0, P, b * L, (1, L)), start=False, stop=True).then_inc(hid_mm, 1)
            for b in range(NB):
                pe.wait_ge(hid_act, 4 * (b + 1))
                if b >= 2:
                    pe.wait_ge(lT_dve, b - 1)
                for m in range(4):
                    last = pe.matmul(bank(6 + b % 2, 0, 20, 0, (1, L)), sl(w2_sb, 0, P, m * 20, (1, 20)),
                                     sl(hT, 0, P, m * TOK + b * L, (1, L)), start=(m == 0), stop=(m == 3))
                last.then_inc(lT_mm, 1)
            pe.wait_ge(lT_dve, NB)
            for j in range(C):
                for ct in range(CT):
                    last = pe.matmul(bank(5, DV * ct, DV, j * 10, (1, 10)), sl(lT, 0, 20, j, (C, BLK)),
                                     sl(ident, 0, 20, ct * 10, (1, 10)), start=True, stop=True, skip_group_check=True)
            last.then_inc(lg_mm, 1)

            pe.wait_ge(on_ready, 1)
            for n in range(8):
                ring(n, 0, on_act, on_dve)
                for w in range(4):
                    last = pe.transpose(bank(n % 4, 0, P, w * P, (1, P)), sl(mix, 0, P, (4 * n + w) * P, (1, P)), ident)
                last.then_inc(on_mm, 1)
            pe.wait_ge(on_act, 4)
            pe.wait_ge(on_dve, 4)
            pe.wait_ge(wo_scaled, 1)
            for t in range(TILES):
                if t >= 4:
                    pe.wait_ge(res1, t - 3)
                for k in range(CT):
                    last = pe.matmul(bank(t % 4, 0, P, 0, (1, D)), sl(onT, 0, P, k * TOK + t * P, (1, P)),
                                     sl(w_o, 0, P, k * D, (1, D)), start=(k == 0), stop=(k == CT - 1))
                last.then_inc(wo_mm, 1)
            pe.wait_ge(wts_in, 16 * 7)
            for i, (x, y) in enumerate(((x_q, x_k), (x_v, x_oT))):
                for m in range(CT):
                    for k in range(CT):
                        last = pe.matmul(bank(6 + i, 0, P, m * D, (1, D)), sl(x, 0, P, k * D + m * P, (1, P)),
                                         sl(y, 0, P, k * D, (1, D)), start=(k == 0), stop=(k == CT - 1),
                                         skip_group_check=True)
                last.then_inc(fold_mm, 1)
            for m in range(CT):
                for k in range(CT):
                    last = pe.matmul(bank(4, 0, P, m, (1, 1)), sl(x_k, 0, P, k * D + m * P, (1, P)),
                                     sl(bq_col, 0, P, k, (1, 1)), start=(k == 0), stop=(k == CT - 1))
            last.then_inc(fold_mm, 1)
            pe.wait_ge(bv_ready, 1)
            for k in range(CT):
                last = pe.matmul(bank(5, 0, P, 0, (1, D)), sl(bv_rep, 0, P, k * P, (1, P)), sl(x_oT, 0, P, k * D, (1, D)),
                                 start=(k == 0), stop=(k == CT - 1))
            last.then_inc(fold_mm, 1)

            pe.wait_ge(res1, TILES)
            for n in range(8):
                pe.wait_ge(x1_ready, 2 * (n + 1))
                if n >= 4:
                    pe.wait_ge(x1T_act, n - 3)
                for w in range(4):
                    t, ct = divmod(w, CT)
                    last = pe.transpose(bank(n % 4, 0, P, w * P, (1, P)),
                                        sl(x1, 0, P, (2 * n + t) * D + ct * P, (1, P)), ident)
                last.then_inc(x1_mm, 1)

            def claim(*step):
                bk, i = misc(*step)
                if i:
                    pe.wait_ge(free[bk - 6], i)
                return bk, full[bk - 6]

            pe.wait_ge(fold_done, 3)
            pe.wait_ge(bvo_ready, 1)
            for kind, b, i in TAIL:
                if kind not in ("scores", "turn_p"):
                    bk, done = claim(kind, b, i)
                if kind == "qk":
                    pe.wait_ge(x1T_act, 2 * (b + 1))
                    for k in range(CT):
                        last = pe.matmul(bank(bk, 0, P, 0, (1, L)), sl(w_qk, 0, P, k * D + i * P, (1, P)),
                                         sl(x1T, 0, P, k * TOK + b * L, (1, L)), start=(k == 0), stop=(k == CT - 1))
                    last.then_inc(done, 1)
                elif kind == "scores":
                    n = TPB * b + i
                    for k in range(CT):
                        bq_, j_ = misc("qk", b, k)
                        pe.wait_ge(free[bq_ - 6], j_ + 1)
                    pe.wait_ge(ctx_in[b % 2], 48 * (b // 2 + 1))
                    if n == 0:
                        pe.wait_ge(x1T_act, 8)
                    else:
                        pe.wait_ge(exped, n)
                    for c in range(4):
                        w = min(512, S_CTX - 512 * c)
                        for k in range(CT):
                            last = pe.matmul(bank(c, 0, P, 0, (1, w)), sl(qk_sb, 0, P, k * L + i * P, (1, P)),
                                             sl(ctx_t, 0, P, ((b % 2) * CT + k) * S_CTX + 512 * c, (1, w)),
                                             start=(k == 0), stop=(k == CT - 1))
                        last.then_inc(scored, 1)
                elif kind == "turn_p":
                    n = TPB * b + i
                    pe.wait_ge(exped, n + 1)
                    for g in range(4):
                        if 2 * n + g // 2:
                            pe.wait_ge(p_kept[g % 2], 2 * n + g // 2)
                        if n and i == 0:
                            bv_, j_ = misc("pv", b - 1, 1)
                            pe.wait_ge(free[bv_ - 6], j_ + 1)
                        for w in range(4 if g < 3 else 1):
                            kv = KV[4 * g + w]
                            last = pe.transpose(bank(4 + g % 2, 0, kv, w * P, (1, P)),
                                                sl(p_sb, 0, P, (n % 2) * 1664 + (4 * g + w) * P, (1, kv)), ident)
                        last.then_inc(p_mm[g % 2], 1)
                elif kind == "pv":
                    pe.wait_ge(p_kept[0], 2 * TPB * (b + 1))
                    pe.wait_ge(p_kept[1], 2 * TPB * (b + 1))
                    for g, kv in enumerate(KV):
                        last = pe.matmul(bank(bk, 0, P, 0, (1, L)),
                                         sl(ctx_n, 0, kv, ((b % 2) * 13 + g) * D + i * P, (1, P)),
                                         sl(pT, 0, kv, g * L, (1, L)), start=(g == 0), stop=(g == 12))
                    last.then_inc(done, 1)
                elif kind == "post":
                    for k in range(CT):
                        bv_, j_ = misc("pv", b, k)
                        pe.wait_ge(free[bv_ - 6], j_ + 1)
                    for k in range(CT):
                        last = pe.matmul(bank(bk, 0, P, 0, (1, D)), sl(pcT, 0, P, k * L + i * P, (1, P)),
                                         sl(w_vo, 0, P, k * D, (1, D)), start=(k == 0), stop=(k == CT - 1))
                    last.then_inc(done, 1)
                elif kind == "turn_x2":
                    pe.wait_ge(x2_ready, TPB * (b + 1))
                    for w in range(4):
                        t, ct = divmod(w, CT)
                        last = pe.transpose(bank(bk, 0, P, w * P, (1, P)),
                                            sl(x2, 0, P, (2 * i + t) * D + ct * P, (1, P)), ident)
                    last.then_inc(done, 1)
                elif kind in ("gate", "up"):
                    for k in range(2):
                        bx, j_ = misc("turn_x2", b, k)
                        pe.wait_ge(free[bx - 6], j_ + 1)
                    pe.wait_ge(int_done, 3)
                    w = w_g if kind == "gate" else w_u
                    for k in range(CT):
                        last = pe.matmul(bank(bk, 0, P, 0, (1, L)), sl(w, 0, P, k * HID + i * P, (1, P)),
                                         sl(x2T, 0, P, k * L, (1, L)), start=(k == 0), stop=(k == CT - 1))
                    last.then_inc(done, 1)
                elif kind == "down":
                    pe.wait_ge(h_ready, FT * (b + 1))
                    for m in range(FT):
                        last = pe.matmul(bank(bk, 0, P, 0, (1, D)), sl(hF, 0, P, m * L + i * P, (1, P)),
                                         sl(w_d, 0, P, m * D, (1, D)), start=(m == 0), stop=(m == FT - 1))
                    last.then_inc(done, 1)

        @block.vector
        def _(dve):
            def project(n):
                if n >= NPROJ:
                    return
                b, j = divmod(n, 6)
                proj, ct = divmod(j, 2)
                dve.wait_ge(tap_first, n + 1)
                for k in range(1, CONV_K):
                    if k > 1:
                        dve.wait_ge(tap_step, 2 * n + k - 1)
                    y = sl(y_buf, 0, P, (n % 2) * L + k, (1, L - k))
                    dve.scalar_tensor_tensor(
                        out=y, in0=bank(n % 2, 0, P, 0, (1, L - k)),
                        scalar=sl(conv_w, 0, P, ct * 12 + proj * CONV_K + CONV_K - 1 - k, (1, 1)), in1=y,
                        op0=ALU.mult, op1=ALU.add).then_inc(tap_step if k < CONV_K - 1 else conv_done, 1)

            def turn(t):
                b, r = divmod(t, TPB)
                dve.wait_ge(raw_done, t + 1)
                if b and r == 0:
                    dve.wait_ge(sqrt_done, b)
                dve.tensor_reduce(sl(ss, 0, P, r * 8, (1, 8)), sl(sq, 0, P, 0, (DV, 8), (1, DV)), AX.X, ALU.add
                                  ).then_inc(ss_done, 1)
                dve.wait_ge(v_turned, t + 1)
                if t == 0:
                    dve.wait_ge(beta_ready, 1)
                dve.tensor_tensor(sl(vk, 0, P, t * 512, (DV, H), (1, DV)), bank(3, 0, P, 0, (DV, H), (1, DV)),
                                  sl(beta, 0, P, t * H, (1, H), (0, DV)), ALU.mult).then_inc(vb_done, 1)

            def normalise(b):
                dve.wait_ge(sqrt_done, b + 1)
                if b:
                    dve.wait_ge(qn_done, b)
                dve.reciprocal(rn, nrm).then_inc(rn_done, 1)
                dve.wait_ge(rn_done, b + 1)
                knb = sl(kn, 0, P, b * TPB * D, (D, TPB), (DV, H), (1, DV))
                dve.tensor_tensor(knb, sl(raw, 0, P, 0, (2 * D, TPB), (DV, H), (1, DV)),
                                  sl(rn, 0, P, 0, (8, TPB), (1, H), (0, DV)), ALU.mult).then_inc(kn_done, 1)
                dve.wait_ge(kn_done, b + 1)
                dve.tensor_tensor(sl(vk, 0, P, b * TPB * 512 + D, (512, TPB), (DV, H), (1, DV)),
                                  sl(kn, 0, P, b * TPB * D, (D, TPB), (DV, H), (1, DV)),
                                  sl(beta, 0, P, b * TPB * H, (H, TPB), (1, H), (0, DV)), ALU.mult).then_inc(kb_done, 1)

            def turn_back(t):
                dve.wait_ge(back_turned, t + 1)
                if t >= 2:
                    dve.wait_ge(gram_done, t - 1)
                    dve.wait_ge(wq_q, 2 * (t - 1))
                if t == 0:
                    dve.wait_ge(zeroed, 2)
                dve.tensor_copy(sl(bd, DV, DV, (t % 2) * CT * 512 + P, (256, 2 * CT), (1, P)),
                                bank(5, DV, DV, 0, (P, 2 * CT), (1, P))).then_inc(back_dve, 1)

            def gram(t):
                dve.wait_ge(gram_done, t + 1)
                for q in range(QC):
                    dve.tensor_tensor(sl(al, C * q, C, t * 256, (P, CT), (C, 4), (1, C)),
                                      bank(6, C * q, C, C * q, (512, CT), (P, 4), (1, C)),
                                      sl(mask_gram, C * q, C, 0, (0, CT), (C, 4), (1, C)), ALU.mult
                                      ).then_inc(gram_masked, 1)

            steps_before = [0]

            def solve(s):
                dve.wait_ge(a_in, 16 * (s + 1))
                dve.wait_ge(u_init, 2 * (s + 1))
                for l in range(C - 1):
                    n = C - 1 - l
                    if l:
                        dve.wait_ge(solve_step, steps_before[0])
                    dve.tensor_tensor(sl(u_tmp, 0, P, 0, (n, l + 1), (1, n)),
                                      sl(u_row, 0, P, l, (C, l + 1), (0, n)),
                                      sl(a_row, 0, P, l * C + l + 1, (0, l + 1), (1, n)), ALU.mult
                                      ).then_inc(solve_step, 1)
                    steps_before[0] += 1
                    dve.wait_ge(solve_step, steps_before[0])
                    u = sl(u_row, 0, P, l + 1, (C, l + 1), (1, n))
                    last = dve.tensor_tensor(u, u, sl(u_tmp, 0, P, 0, (n, l + 1), (1, n)), ALU.add)
                    if l < C - 2:
                        last.then_inc(solve_step, 1)
                        steps_before[0] += 1
                last.then_inc(solved, 1)

            for kind, n in ORDER:
                if kind == "project":
                    project(n)
                elif kind == "turn":
                    turn(n)
                elif kind == "normalise":
                    normalise(n)
                elif kind == "turn_back":
                    turn_back(n)
                elif kind == "gram":
                    gram(n)
            for s in range(SETS):
                solve(s)
            dve.wait_ge(s_const, 16 * 7)
            for t in range(TILES + 1):
                if t < TILES and t % 2 == 1:
                    dve.wait_ge(uw_mm, t + 1)
                    dve.tensor_copy(sl(vk, 0, P, t * 512, (D, 2), (DV, H), (1, DV)), bank(1, 0, P, 0, (DV, 2), (P, H), (1, DV))).then_inc(uw_dve, 1)
                if t % 2 == 1:
                    dve.wait_ge(w_turned, t)
                    dve.tensor_copy(sl(wq, 0, P, (t - 1) * QC * 2 * C, (NCHUNK * 2 * C, CT), (2 * C, QC), (1, C)),
                                    bank(2, 0, P, 0, (P, CT), (C, QC), (1, C))).then_inc(w_dve, 1)

            for n in range(STEPS):
                g, q = divmod(n, QC)
                for s in range(SETS):
                    dve.wait_ge(wq_mm[s], n + 1)
                    dve.tensor_tensor(sl(u_new, C * q, C, (s * 2 + n % 2) * 512, (D, 2), (DV, H), (1, DV)),
                                      sl(vk, C * q, C, (s * TPS + g) * 512, (TPB * 512, 2), (DV, H), (1, DV)),
                                      bank(2 * s + n % 2, 0, C, 0, (D, 2), (DV, H), (1, DV)), ALU.subtract
                                      ).then_inc(u_ready[s], 1)
                if n == STEPS - 1:
                    continue
                for s in range(SETS):
                    dve.wait_ge(s_mm[s], n + 1)
                    dve.tensor_tensor(sl(state, 0, P, s * 512, (P, 4), (1, P)), bank(4 + s, 0, P, 0, (P, 4), (1, P)),
                                      sl(mask_heads, 0, P, 0, (0, 4), (1, P)), ALU.mult).then_inc(state_ready[s], 1)

            for n in range(1, 32, 2):
                dve.wait_ge(win_mm, n + 1)
                dve.tensor_copy(win_dst(n), bank(n % 4, 0, WIN, 0, (1, P), (P, 4))).then_inc(win_dve, 1)
            for n in range(1, 24, 2):
                dve.wait_ge(blk_mm, n + 1)
                dve.tensor_copy(blk_dst(n), blk_src(n)).then_inc(blk_dve, 1)
            dve.wait_ge(blk_act, 12)
            dve.wait_ge(blk_dve, 12)
            for j, (p, h) in enumerate(STATS):
                if p < NF:
                    dve.wait_ge(fir_act, 16 * (h + 1))
                x = sl(PATHS[p], 0, P, h * DV, (P, C), (1, DV))
                to = p * 8 + h * 4
                dve.tensor_reduce(sl(st, 0, P, to, (40, C)), x, AX.X, ALU.add)
                dve.tensor_reduce(sl(st, 0, P, to + 2, (40, C)), x, AX.X, ALU.add,
                                  apply_absolute_value=True).then_inc(stat_abs, 1)
                dve.wait_ge(sq_ready, j + 1)
                dve.tensor_reduce(sl(st, 0, P, to + 1, (40, C)), sl(sqt, 0, P, (j % 2) * C * DV, (DV, C), (1, DV)),
                                  AX.X, ALU.add).then_inc(stat_sq, 1)
            dve.wait_ge(st_norm, 1)
            dve.wait_ge(stat_sq, 2 * NPATH)
            dve.wait_ge(stat_abs, 2 * NPATH)
            dve.tensor_scalar(sl(st, 0, P, 0, (4, 320), (1, 3)), sl(st, 0, P, 0, (4, 320), (1, 3)), 1.0 / DV, None,
                              ALU.mult).then_inc(st_ready, 1)
            dve.wait_ge(s_par, 16 * 8)
            dve.tensor_scalar(tau_t[:, 0:2], tau_in, -1.0, None, ALU.mult).then_inc(par_dve, 1)
            dve.wait_ge(par_dve, 1)
            dve.tensor_tensor(tau_t[:, 0:2], tau_t[:, 0:2], tau_in, ALU.max).then_inc(par_dve, 1)
            dve.wait_ge(par_act, 2)
            dve.tensor_scalar(tau_in, tau_in, 0.0, 0.5, ALU.max, ALU.add).then_inc(par_dve, 1)
            dve.wait_ge(par_dve, 3)
            dve.tensor_tensor(tau_in, tau_in, tau_t[:, 2:4], ALU.add).then_inc(par_dve, 1)
            dve.wait_ge(par_dve, 4)
            dve.reciprocal(tau_inv, tau_in).then_inc(par_dve, 1)

            dve.wait_ge(w1s_mm, 1)
            dve.tensor_copy(w1_s, bank(4, 0, P, 0, (1, HF))).then_inc(w1s_ready, 1)
            dve.wait_ge(statsT_zero, 1)
            for n in range(1, 8, 2):
                dve.wait_ge(st_mm, n + 1)
                for ct in range(CT):
                    last = dve.tensor_copy(stats_dst(n, ct), bank(4 + n % 4, 0, 40, ct * DV, (P, 4), (1, DV)))
                last.then_inc(st_dve, 1)
            dve.wait_ge(par_act, 3)
            dve.tensor_scalar(eps_row, eps_row, 0.2, None, ALU.mult).then_inc(par_dve, 1)
            dve.wait_ge(par_dve, 6)
            dve.tensor_reduce(eps_keep, sl(eps_row, 0, P, 0, (NPATH, 2), (1, NPATH)), AX.X, ALU.add).then_inc(par_dve, 1)
            dve.wait_ge(par_dve, 7)
            dve.tensor_scalar(eps_keep, eps_keep, -1.0, 1.0, ALU.mult, ALU.add).then_inc(par_dve, 1)

            for b in range(NB):
                dve.wait_ge(lT_mm, b + 1)
                dve.tensor_copy(sl(lT, 0, 20, b * L, (1, L)), bank(6 + b % 2, 0, 20, 0, (1, L))).then_inc(lT_dve, 1)
            dve.wait_ge(lg_mm, 1)
            dve.tensor_tensor(sl(lg, 0, P, 0, (10, C), (1, 10)), bank(5, 0, P, 0, (10, C), (1, 10)),
                              sl(gb2_row, 0, P, 0, (0, C), (1, 10)), ALU.add).then_inc(gate_step, 1)
            dve.wait_ge(gate_step, 1)
            dve.wait_ge(par_dve, 8)
            lg3 = sl(lg, 0, P, 0, (10, C), (NPATH, 2), (1, NPATH))
            dve.tensor_tensor(lg3, lg3, sl(tau_inv, 0, P, 0, (0, C), (1, 2), (0, NPATH)), ALU.mult).then_inc(gate_step, 1)
            dve.wait_ge(gate_step, 2)
            lg2 = sl(lg, 0, P, 0, (NPATH, 2 * C), (1, NPATH))
            dve.tensor_reduce(mx, lg2, AX.X, ALU.max).then_inc(mix_step, 1)
            dve.wait_ge(mix_step, 1)
            dve.tensor_tensor(lg2, lg2, sl(mx, 0, P, 0, (1, 2 * C), (0, NPATH)), ALU.subtract).then_inc(gate_step, 1)
            dve.wait_ge(exp_done, 1)
            pr2 = sl(pr, 0, P, 0, (NPATH, 2 * C), (1, NPATH))
            dve.tensor_reduce(sm, pr2, AX.X, ALU.add).then_inc(mix_step, 1)
            dve.wait_ge(mix_step, 2)
            dve.reciprocal(rs, sm).then_inc(mix_step, 1)
            dve.wait_ge(mix_step, 3)
            dve.tensor_tensor(sl(rs, 0, P, 0, (2, C), (1, 2)), sl(rs, 0, P, 0, (2, C), (1, 2)),
                              sl(eps_keep, 0, P, 0, (0, C), (1, 2)), ALU.mult).then_inc(mix_step, 1)
            dve.wait_ge(mix_step, 4)
            dve.tensor_tensor(pr2, pr2, sl(rs, 0, P, 0, (1, 2 * C), (0, NPATH)), ALU.mult).then_inc(mix_step, 1)
            dve.wait_ge(mix_step, 5)
            dve.tensor_tensor(sl(pr, 0, P, 0, (10, C), (1, 10)), sl(pr, 0, P, 0, (10, C), (1, 10)),
                              sl(eps_row, 0, P, 0, (0, C), (1, 10)), ALU.add).then_inc(pr_ready, 1)
            dve.wait_ge(pr_ready, 1)
            for p in range(2, NPATH):
                x = sl(PATHS[p], 0, P, 0, (DV, 2 * C), (1, DV))
                dve.tensor_tensor(x, x, sl(pr, 0, P, p, (NPATH, 2 * C), (0, DV)), ALU.mult).then_inc(mix_dve, 1)
            for i, x in enumerate((o_blk, v_blk, PATHS[0])):
                dve.wait_ge(mix_dve, 3 + i)
                if i == 2:
                    dve.wait_ge(mix_pool, 3)
                dve.tensor_tensor(mix, mix, x, ALU.add).then_inc(mix_dve, 1)
            dve.wait_ge(mix_sq, 1)
            dve.tensor_reduce(r64, sl(sqt, 0, P, 0, (DV, 2 * C), (1, DV)), AX.X, ALU.add).then_inc(mix_sum, 1)
            dve.wait_ge(mix_sqrt, 1)
            dve.reciprocal(r64, rs).then_inc(mix_step, 1)
            dve.wait_ge(mix_step, 6)
            x = sl(mix, 0, P, 0, (DV, 2 * C), (1, DV))
            dve.tensor_tensor(x, x, sl(r64, 0, P, 0, (1, 2 * C), (0, DV)), ALU.mult).then_inc(on_ready, 1)
            for n in range(1, 8, 2):
                dve.wait_ge(on_mm, n + 1)
                dve.tensor_copy(on_dst(n), on_src(n)).then_inc(on_dve, 1)
            dve.wait_ge(wts_in, 16 * 7)
            dve.tensor_copy(sl(bv_rep, 0, P, 0, (P, CT), (1, P)), sl(bv_col, 0, P, 0, (1, CT), (0, P))
                            ).then_inc(bv_ready, 1)

            for t in range(TILES):
                dve.wait_ge(wo_mm, t + 1)
                dve.wait_ge(x_in[t // TPB], 16)
                x = sl(x1, 0, P, t * D, (1, D))
                dve.tensor_tensor(x, x, bank(t % 4, 0, P, 0, (1, D)), ALU.add).then_inc(res1, 1)
                dve.wait_ge(res1, t + 1)
                if t:
                    dve.wait_ge(agg, t)
                dve.bn_stats(bn6, x).then_inc(bn, 1)
                dve.wait_ge(bn, t + 1)
                dve.bn_aggr(mv[:, 2 * t:2 * t + 2], bn6).then_inc(agg, 1)
                if t % TPB == TPB - 1:
                    b = t // TPB
                    dve.wait_ge(sqrt1, b + 1)
                    rb = rstd[:, TPB * b:TPB * b + TPB]
                    dve.reciprocal(rb, rb).then_inc(rstd1, 1)
                    dve.wait_ge(rstd1, b + 1)
                    for i in range(TPB * b, TPB * b + TPB):
                        x = sl(x1, 0, P, i * D, (1, D))
                        dve.tensor_scalar(x, x, mv[:, 2 * i:2 * i + 1], rstd[:, i:i + 1], ALU.subtract, ALU.mult
                                          ).then_inc(x1_ready, 1)

            dve.wait_ge(fold_mm, 4)
            dve.tensor_tensor(b_vo, bank(5, 0, P, 0, (1, D)), bo_row, ALU.add).then_inc(bvo_ready, 1)

            def filled(*step):
                bk, i = misc(*step)
                dve.wait_ge(full[bk - 6], i + 1)
                return bk, free[bk - 6]

            def statistics(k, i, x):
                n = TPB * k + i
                dve.wait_ge(res2, n + 1)
                dve.wait_ge(agg, TILES + n)
                if i == 0 and k:
                    dve.wait_ge(x2_ready if k % 2 else y_ready, TPB * ((k + 1) // 2))
                dve.bn_stats(bn6, x).then_inc(bn, 1)
                dve.wait_ge(bn, TILES + n + 1)
                dve.bn_aggr(mv2[:, 2 * i:2 * i + 2], bn6).then_inc(agg, 1)

            def centre(k, src, dst, done):
                dve.wait_ge(sqrt2, k + 1)
                dve.reciprocal(rstd2, rstd2).then_inc(rstd2_ready, 1)
                dve.wait_ge(rstd2_ready, k + 1)
                for i in range(TPB):
                    dve.tensor_scalar(sl(dst, 0, P, i * D, (1, D)), sl(src, 0, P, i * D, (1, D)),
                                      mv2[:, 2 * i:2 * i + 1], rstd2[:, i:i + 1], ALU.subtract, ALU.mult
                                      ).then_inc(done, 1)

            for kind, b, i in TAIL:
                n = TPB * b + i
                if kind == "scores":
                    for c in range(4):
                        dve.wait_ge(scored, 4 * n + c + 1)
                        last = dve.tensor_reduce(sl(sm_part, 0, P, c, (1, 1)), bank(c, 0, P, 0, (1, min(512, S_CTX - 512 * c))),
                                                 AX.X, ALU.max)
                    last.then_inc(maxed, 1)
                    dve.wait_ge(maxed, 2 * n + 1)
                    dve.tensor_reduce(sl(sm_max, 0, P, n % 8, (1, 1)), sm_part, AX.X, ALU.max).then_inc(maxed, 1)
                    dve.wait_ge(maxed, 2 * n + 2)
                    dve.tensor_scalar(sl(sm_neg, 0, P, n % 8, (1, 1)), sl(sm_max, 0, P, n % 8, (1, 1)), -1.0 / 16.0,
                                      None, ALU.mult).then_inc(neg_ready, 1)
                elif kind == "turn_p":
                    for g in (1, 3):
                        dve.wait_ge(p_mm[1], 2 * n + g // 2 + 1)
                        if g == 1:
                            dve.tensor_copy(p_dst(i, g), bank(5, 0, P, 0, (P, 4), (1, P))).then_inc(p_kept[1], 1)
                        else:
                            dve.tensor_copy(sl(pT, 0, KV[12], 12 * L + i * P, (1, P)),
                                            bank(5, 0, KV[12], 0, (1, P))).then_inc(p_kept[1], 1)
                elif kind == "post":
                    if i == 0:
                        dve.reciprocal(sl(sm_inv, 0, P, (b % 2) * TPB, (1, TPB)),
                                       sl(sm_sum, 0, P, (b % 2) * TPB, (1, TPB))).then_inc(inv_ready, 1)
                        dve.wait_ge(inv_ready, b + 1)
                        dve.wait_ge(x1_bias, b + 1)
                    bk, done = filled(kind, b, i)
                    x = sl(x1, 0, P, n * D, (1, D))
                    dve.scalar_tensor_tensor(out=x, in0=bank(bk, 0, P, 0, (1, D)),
                                             scalar=sl(sm_inv, 0, P, n % 8, (1, 1)), in1=x,
                                             op0=ALU.mult, op1=ALU.add).then_inc(res2, 1)
                    statistics(2 * b, i, x)
                    dve.sem_inc(done, 1)
                    if i == TPB - 1:
                        centre(2 * b, sl(x1, 0, P, b * TPB * D, (1, TPB * D)), x2, x2_ready)
                elif kind == "up":
                    bk, done = filled(kind, b, i)
                    m = FT * b + i
                    dve.wait_ge(silu_g, m + 1)
                    dve.tensor_tensor(sl(hF, 0, P, i * L, (1, L)), sg, bank(bk, 0, P, 0, (1, L)), ALU.mult
                                      ).then_inc(h_ready, 1)
                    dve.wait_ge(h_ready, m + 1)
                    dve.sem_inc(done, 1)
                elif kind == "down":
                    bk, done = filled(kind, b, i)
                    x = sl(x2, 0, P, i * D, (1, D))
                    dve.tensor_tensor(x, x, bank(bk, 0, P, 0, (1, D)), ALU.add).then_inc(res2, 1)
                    statistics(2 * b + 1, i, x)
                    dve.sem_inc(done, 1)
                    if i == TPB - 1:
                        if b:
                            dve.wait_ge(stored, 16 * b)
                        centre(2 * b + 1, x2, y_out, y_ready)



def constants():
    import numpy as np

    row = np.arange(P)
    gram = np.zeros((P, 4, C), np.float32)
    behind = np.arange(C)[None, :] - (row % C)[:, None]
    gram[:, 0:2, :] = -(behind > 0).astype(np.float32)[:, None, :]
    gram[:, 2:4, :] = (behind >= 0).astype(np.float32)[:, None, :]
    heads = (row[:, None] // DV == row[None, :] // DV).astype(np.float32)
    h, kind = row // 32, row // 8 % 4
    expand = np.zeros((P, NPATH, P), np.float32)
    for p in range(NPATH):
        expand[row, p, 64 * (h // 2) + 8 * p + 4 * (h % 2) + kind] = 1.0
    eps = np.zeros((P, 4), np.float32)
    eps[:, 0], eps[:, 1] = 1e-6, LN_EPS
    return {"ident": np.eye(P, dtype=np.float32), "mask_gram": gram.reshape(P, -1), "mask_heads": heads,
            "expand": expand.reshape(P, -1), "eps": eps}


def laid_out(inputs):
    import numpy as np

    a, x, f = "L0_attn_", "L0_xattn_", "L0_ffn_"
    get = {k: np.asarray(v) for k, v in inputs.items()}
    own = {"xT": get["x"].reshape(TOK, D).T, "x": get["x"].reshape(TOK, D),
           "ctx": get["ctx_1024"].reshape(-1, D), "ctxT": get["ctx_1024"].transpose(0, 2, 1).reshape(NB * D, S_CTX)}
    for k in ("Wq", "Wk", "Wv", "Wb", "Wo", "conv_q", "conv_k", "conv_v", "gW1", "gW2", "gb2", "log_tau", "norm_w"):
        own[k] = get[a + k]
    own["gb1"] = get[a + "gb1"].reshape(-1, P).T
    own["eps_logit"] = get[a + "eps_logit"].reshape(-1)
    taps = np.zeros((D, WIN + C - 1, NF), np.float32)
    for i, k in enumerate(("fir_s", "fir_m", "fir_l")):
        taps[:, WIN - FIRS[i]:WIN, i] = get[a + k]
    own["taps"] = taps.reshape(D, -1)
    own.update({"xWq": get[x + "Wq"], "xWk": get[x + "Wk"], "xWv": get[x + "Wv"], "xWoT": get[x + "Wo"].T,
                "xbq": get[x + "bq"].reshape(CT, P).T, "xbv": get[x + "bv"].reshape(CT, P).T, "xbo": get[x + "bo"],
                "wgT": get[f + "w_gate"].T, "wuT": get[f + "w_up"].T, "wdT": get[f + "w_down"].T})
    own.update(constants())
    return {k: np.ascontiguousarray(v) for k, v in own.items()}


def kernel(**inputs):
    import concourse.bacc as bacc
    from concourse.bass_utils import run_bass_kernel_spmd

    nc = bacc.Bacc("TRN2", target_bir_lowering=False, num_devices=1)
    arrays = {f"in_{k}_dram": v for k, v in laid_out(inputs).items()}
    a = {k[3:-5]: nc.dram_tensor(k, list(v.shape), mybir.dt.from_np(v.dtype), kind="ExternalInput").ap()
         for k, v in arrays.items()}
    for k in ("scr_a", "scr_u"):
        a[k] = nc.dram_tensor(k, [2, P, C * C], F32, kind="Internal").ap()
    out = nc.dram_tensor("out_0_dram", [TOK, D], F32, kind="ExternalOutput").ap()
    build(nc, a, out)
    r = run_bass_kernel_spmd(nc, [arrays], core_ids=[0])
    return r.results[0]["out_0_dram"].reshape(NB, L, D)
```

```python
from contextlib import ExitStack

import concourse.bass as bass
from concourse import mybir

F32 = mybir.dt.float32
F32R = mybir.dt.float32r
I32 = mybir.dt.int32
ALU = mybir.AluOpType
ACT = mybir.ActivationFunctionType
AX = mybir.AxisListType

P = 128
NB, L, D, H = 4, 512, 256, 4
DV = D // H
CT = D // P
TOK = NB * L
TILES = TOK // P
TPB = L // P
C = 32
QC = P // C
NCHUNK = TOK // C
BLK = TOK // C
CONV_K = 4
FIRS = (3, 15, 64)
NF = len(FIRS)
HALO = 64
WIN = HALO + C
NPATH = 5
NKIND = 4
HF = 2 * D
S_CTX = 1601
KV = [min(P, S_CTX - P * i) for i in range(-(-S_CTX // P))]
S_PAD = S_CTX + 1
HID = 768
FT = HID // P
LN_EPS = 1e-5


def sl(buf, p0, n, off, *dims):
    pitch = buf.ap[0][0]
    return bass.AP(buf.tensor, buf.offset + p0 * pitch + off, [[pitch, n]] + [[s, c] for s, c in dims])


def dr(x, off, *dims):
    return bass.AP(x.tensor, off, [[s, c] for s, c in dims])


def phase_one_order():
    steps = [(n, 0, "project", n) for n in range(6 * NB + 1)]
    for b in range(NB):
        t0 = 6 * (b + 1)
        for r in range(TPB):
            steps += [(t0 + 2 + r, 1, "turn", TPB * b + r), (t0 + 7 + r, 3, "turn_back", TPB * b + r),
                      (t0 + 8 + r, 4, "gram", TPB * b + r)]
        steps.append((t0 + 6, 2, "normalise", b))
    return [(kind, n) for _, _, kind, n in sorted(steps)]


def build(nc, a, out):
    with ExitStack() as ctx:
        WORDS = 53200
        with nc.sbuf_tensor("arena", [P, WORDS], F32) as arena:
            pass
        ps = ctx.enter_context(nc.psum_tensor("ps", [P, 8, 512], F32))
        psv = ps[:, :, :].rearrange("p b n -> p (b n)")

        def sem(name):
            return ctx.enter_context(nc.semaphore(name))

        def at(start, n):
            assert start + n <= WORDS
            return arena[:, start:start + n]

        def named(name, start, n, dtype):
            with nc.sbuf_tensor(f"below_{name}", [P, start], F32):
                with nc.sbuf_tensor(name, [P, n], dtype) as words:
                    return start, n, words[:, :]

        def within(views, x):
            p0, off = divmod(x.offset, WORDS)
            for start, n, words in views:
                if start <= off < start + n:
                    return bass.AP(words.tensor, p0 * n + off - start, [[n, x.ap[0][1]]] + [list(d) for d in x.ap[1:]])

        def r32(x):
            return within(OPERANDS, x)

        def high_of(x):
            return r32(x).bitcast(F32)

        def loaded(x):
            return within(LOADED, x)

        def bank(i, p0, n, off, *dims):
            return sl(psv, p0, n, 512 * i + off, *dims)

        ident = at(0, 128)
        mask_gram = at(128, 128)
        mask_heads = at(256, 128)
        eps_col = at(384, 4)
        conv_w = at(388, CT * 3 * CONV_K)
        beta = at(416, TILES * H)
        ss = at(480, TPB * 8)
        nrm = at(512, TPB * 8)
        rn = at(544, TPB * 8)
        vT = at(2048 + HALO, CT * TOK)
        kn = at(6656, TILES * D)
        vk = at(10752, TILES * H * 2 * DV)
        al = at(18944, TILES * CT * 4 * C)
        wq = at(23040, CT * NCHUNK * 2 * C)
        xT = at(31232, CT * TOK)
        o_tok = xT
        w_in = at(35328, CT * 3 * D)
        w_beta = at(36864, CT * H)
        y_buf = at(36880, 2 * L)
        qkT = at(37904, 2 * 2 * CT * L)
        raw = at(42000, TPB * 2 * D)
        sq = at(44048, 2 * D)
        qn = at(44688, TPB * D)
        knT = at(45712, 2 * CT * P)
        bd = at(46224, 2 * CT * 4 * P)
        a_row = at(48384, C * C)
        u_row = at(49408, C * C)
        u_tmp = at(50432, C * C)
        ubd = at(35328, 2 * 8 * H * P)
        state = at(43520, 2 * 4 * P)
        u_new = at(44544, 2 * 2 * 4 * P)

        SETS = 2
        s_const = sem("s_const")
        s_par = sem("s_par")
        s_x = [sem(f"s_x{b}") for b in range(NB)]
        s_win = sem("s_win")
        zeroed = sem("zeroed")
        beta_mm, beta_ready = sem("beta_mm"), sem("beta_ready")
        projected, tap_first, tap_step, conv_done, silu_done = (
            sem("projected"), sem("tap_first"), sem("tap_step"), sem("conv_done"), sem("silu_done"))
        kq_turned, v_turned = sem("kq_turned"), sem("v_turned")
        raw_done, ss_done, vb_done = sem("raw_done"), sem("ss_done"), sem("vb_done")
        sqrt_done, rn_done, kn_done, kb_done, qn_done = (
            sem("sqrt_done"), sem("rn_done"), sem("kn_done"), sem("kb_done"), sem("qn_done"))
        back_turned, back_act, back_dve, wq_q = sem("back_turned"), sem("back_act"), sem("back_dve"), sem("wq_q")
        gram_done, gram_masked = sem("gram_done"), sem("gram_masked")
        a_out, a_in, u_out, u_in = sem("a_out"), sem("a_in"), sem("u_out"), [sem(f"u_in{s}") for s in range(SETS)]
        u_init, solve_step, solved = sem("u_init"), sem("solve_step"), sem("solved")
        zero_words = sem("zero_words")
        uw_mm, uw_act, uw_dve = sem("uw_mm"), sem("uw_act"), sem("uw_dve")
        w_turned, w_act, w_dve = sem("w_turned"), sem("w_act"), sem("w_dve")
        wq_mm = [sem(f"wq_mm{g}") for g in range(2)]
        u_ready = [sem(f"u_ready{g}") for g in range(2)]
        o_mm = [sem(f"o_mm{g}") for g in range(2)]
        s_mm = [sem(f"s_mm{g}") for g in range(2)]
        state_ready = [sem(f"state_ready{g}") for g in range(2)]
        o_kept = [sem(f"o_kept{g}") for g in range(2)]

        win = at(6656, CT * P * BLK)
        fir = at(35328, NF * C * P)
        taps_ring = at(47616, 3 * CT * 4 * C * NF)
        expand = at(49920, NPATH * P)
        w1_part = at(50560, NPATH * HF)
        w1_raw = at(35328, 2 * 8 * HF)
        v_blk = at(23040, C * P)
        oT = at(2112, CT * TOK)
        o_blk = at(31232, C * P)
        xT2 = at(27136, CT * TOK)
        st = at(640, C * 40)
        w2_sb = at(1920, 4 * 20)
        b1_col, gb2_row, tau_in, tau_inv = at(2000, 4), at(2004, 10), at(2014, 2), at(2016, 2)
        eps_row, eps_keep, tau_t, nw_col = at(2018, 10), at(2028, 2), at(2030, 4), at(2034, 1)
        sqt = at(2112, C * P)
        hT = at(6656, 4 * TOK)
        statsT = at(14848, TOK)
        w1_s = at(16896, HF)
        w1_x = at(17408, CT * HF)
        lT = at(18432, TOK)
        pr, lg, mx, sm, rs, r64 = at(640, 320), at(960, 320), at(1280, 64), at(1344, 64), at(1408, 64), at(1472, 64)
        mix = sl(fir, 0, P, 2 * C * P, (1, C * P))
        onT = xT2
        x1 = at(31232, TILES * D)
        w_o = at(20480, 512)
        stage_i = at(20992, 1536)
        w_qk, w_vo, b_vo = at(35328, 512), at(35840, 512), at(36352, 256)
        x_q, x_k, x_v, x_oT = (at(36608 + 512 * i, 512) for i in range(4))
        bv_rep = at(38656, CT * P)
        p_sb = at(36608, 2 * 1664)
        qk_h, qk_l = at(640, CT * L), at(1664, CT * L)
        ctx_t = at(6656, 2 * CT * S_PAD)
        ctxt_h = at(13064, CT * S_PAD)
        ctx_n, ctxn_h = at(16272, 13 * D), at(19600, 13 * D)
        pT_h, pT_l = at(22928, 13 * 2 * P), at(26256, 13 * 2 * P)
        x2T_h, x2T_l = at(44032, CT * 2 * P), at(44544, CT * 2 * P)
        hF_l, hF_h = at(40960, FT * 2 * P), at(42496, FT * 2 * P)
        w_g, w_u, w_d = at(47616, 1536), at(49152, 1536), at(50688, 1536)
        wg_h, wu_h = at(45056, 1536), at(5120, 1536)
        wd_h = [at(46592 + D * m if m < 4 else 52224 + D * (m - 4), D) for m in range(FT)]
        x1T = at(29584, CT * L)
        sg = at(30608, 2 * 2 * P)
        x2 = at(39936, TPB * D)
        pcT = at(2688, CT * L)
        y_out = at(3712, TPB * D)
        OPERANDS = [named(f"{name}_operand", start, n, F32R) for name, start, n in (
            ("qk_high", 640, CT * L), ("qk_low", 1664, CT * L), ("wu_high", 5120, 1536),
            ("ctxt_low", 6656, 2 * CT * S_PAD), ("ctxt_high", 13064, CT * S_PAD),
            ("ctxn_low", 16272, 13 * D), ("ctxn_high", 19600, 13 * D),
            ("pT_high", 22928, 26 * P), ("pT_low", 26256, 26 * P),
            ("hF_low", 40960, FT * 2 * P), ("hF_high", 42496, FT * 2 * P),
            ("x2T_high", 44032, CT * 2 * P), ("x2T_low", 44544, CT * 2 * P), ("wg_high", 45056, 1536),
            ("wd_high_first", 46592, 4 * D), ("wg_low", 47616, 1536), ("wu_low", 49152, 1536), ("wd_low", 50688, 1536),
            ("wd_high_last", 52224, 2 * D))]
        LOADED = [named("ctxt_loaded", 6656, 2 * CT * S_PAD, F32), named("ctxn_loaded", 16272, 13 * D, F32)]
        bn6, mv, rstd = at(388, 6), at(400, 32), at(432, 16)
        bqk, bq_col, bo_row = at(448, 2), at(450, 2), at(4736, 256)
        sm_max, sm_neg, sm_sum, sm_inv = at(456, 8), at(464, 8), at(472, 8), at(480, 8)
        mv2, rstd2 = at(488, 8), at(496, 4)
        bv_col = at(500, 2)
        sm_part = at(502, 4)

        win_mm, win_act, win_dve, win_fixed = sem("win_mm"), sem("win_act"), sem("win_dve"), sem("win_fixed")
        blk_mm, blk_act, blk_dve = sem("blk_mm"), sem("blk_act"), sem("blk_dve")
        fir_mm, fir_act = sem("fir_mm"), sem("fir_act")
        taps_in = [sem(f"taps_in{i}") for i in range(3)]
        w1_in = [sem(f"w1_in{i}") for i in range(2)]
        w1_add, w1x_in, xT2_in, gate_in = sem("w1_add"), sem("w1x_in"), sem("xT2_in"), sem("gate_in")
        par_act, par_dve = sem("par_act"), sem("par_dve")
        sq_ready, stat_abs, stat_sq, st_norm, st_ready = (
            sem("sq_ready"), sem("stat_abs"), sem("stat_sq"), sem("st_norm"), sem("st_ready"))
        statsT_zero, st_mm, st_act, st_dve = sem("statsT_zero"), sem("st_mm"), sem("st_act"), sem("st_dve")
        w1s_mm, w1s_ready, hid_mm, hid_act = sem("w1s_mm"), sem("w1s_ready"), sem("hid_mm"), sem("hid_act")
        lT_mm, lT_dve, lg_mm, gate_step, exp_done, pr_ready = (
            sem("lT_mm"), sem("lT_dve"), sem("lg_mm"), sem("gate_step"), sem("exp_done"), sem("pr_ready"))
        mix_pool, mix_dve, mix_sq, mix_sum = (
            sem("mix_pool"), sem("mix_dve"), sem("mix_sq"), sem("mix_sum"))
        on_mm, on_act, on_dve = sem("on_mm"), sem("on_act"), sem("on_dve")
        x_in = [sem(f"x_in{b}") for b in range(NB)]
        wts_in, wo_in, int_in, int_done = sem("wts_in"), sem("wo_in"), sem("int_in"), sem("int_done")
        wo_scaled, wo_mm, res1, bn, agg, sqrt1, rstd1, x1_ready = (
            sem("wo_scaled"), sem("wo_mm"), sem("res1"), sem("bn"), sem("agg"), sem("sqrt1"), sem("rstd1"), sem("x1_ready"))
        x1_bias = sem("x1_bias")
        fold_mm, fold_done, bvo_ready = sem("fold_mm"), sem("fold_done"), sem("bvo_ready")
        ctx_in = [sem(f"ctx_in{i}") for i in range(2)]
        ctxt_high, ctxt_ready, ctxn_in, ctxn_ready, w_split = (
            sem("ctxt_high"), sem("ctxt_ready"), sem("ctxn_in"), sem("ctxn_ready"), sem("w_split"))
        x2_high = sem("x2_high")
        scored, maxed, neg_ready, exped = sem("scored"), sem("maxed"), sem("neg_ready"), sem("exped")
        p_mm, p_high, p_kept, high_kept = sem("p_mm"), sem("p_high"), sem("p_kept"), sem("high_kept")
        full, free = [sem(f"bank_full{i}") for i in range(2)], [sem(f"bank_free{i}") for i in range(2)]
        inv_ready, res2, sqrt2, rstd2_ready, x2_ready = (
            sem("inv_ready"), sem("res2"), sem("sqrt2"), sem("rstd2_ready"), sem("x2_ready"))
        mix_step, bv_ready = sem("mix_step"), sem("bv_ready")
        silu_g, h_product, h_high, h_ready = sem("silu_g"), sem("h_product"), sem("h_high"), sem("h_ready")
        y_ready, stored = sem("y_ready"), sem("stored")

        PATHS = [sl(fir, 0, P, i * C * P, (1, C * P)) for i in range(NF)] + [o_blk, v_blk]
        STATS = [(4, 0), (4, 1), (3, 0), (3, 1)] + [(p, h) for h in range(2) for p in range(NF)]

        def fir_between(j):
            ends = (0, 2, 6, 10, 16, 20, 24, 32)
            return (ends[j - 1], ends[j]) if 0 < j < 8 else (0, 0)


        def tail_order():
            def begin(b):
                return [[("turn_x1", b, 0), ("turn_x1", b, 1)], [("qk", b, 0), ("qk", b, 1)],
                        [("split_ctx", b, c) for c in range(4)]] if b < NB else [[], [], []]

            turns, qks, split = begin(0)
            steps = split + turns + qks
            for b in range(NB + 1):
                turns, qks, split = begin(b + 1)
                if b < NB:
                    steps.append(("scores", b, 0))
                else:
                    steps.append(("turn_last", b - 1, TPB - 1))
                if b:
                    steps += [("pv", b - 1, 1)] + [("post", b - 1, i) for i in range(TPB)]
                if b < NB:
                    steps.append(("scores", b, 1))
                if b:
                    steps += [("turn_x2", b - 1, 0)] + [("ffn", b - 1, m) for m in range(FT)]
                if b < NB:
                    steps.append(("scores", b, 2))
                if b:
                    steps += [("down", b - 1, 0), ("down", b - 1, 1), ("turn_x2", b - 1, 1)]
                if b < NB:
                    steps += [("pv", b, 0), ("scores", b, 3)]
                if b:
                    for m in range(FT):
                        steps.append(("ffn", b - 1, FT + m))
                        steps += split[m - 1:m] if m else []
                    steps += turns + [("down", b - 1, 2)] + qks + [("down", b - 1, 3)]
                else:
                    steps += split + turns + qks
            return steps

        TAIL = tail_order()
        MISC = {step: i for i, step in enumerate(x for x in TAIL if x[0] not in ("scores", "turn_last", "split_ctx"))}

        def misc(*step):
            i = MISC[step]
            return 6 + i % 2, i // 2

        def ctx_cols(c):
            return 512 * c, min(512, S_CTX - 512 * c)

        COLS = (3, 0, 1, 2)
        TURNS = {3: (0,), 0: (1,), 1: (2, 3), 2: ()}

        def group(g):
            return (4 * g, 4, P) if g < 3 else (12, 1, KV[12])

        ORDER = phase_one_order()
        NPROJ = 6 * NB
        PROJ_V, PROJ_K, PROJ_Q = 0, 1, 2
        TPS = TILES // SETS
        STEPS = L // C

        def y_of(n):
            return sl(y_buf, 0, P, (n % 2) * L, (1, L))

        def silu_dst(n):
            b, j = divmod(n, 6)
            proj, ct = divmod(j, 2)
            if proj == PROJ_V:
                return sl(vT, 0, P, ct * TOK + b * L, (1, L))
            return sl(qkT, 0, P, ((b % 2) * 2 + proj - 1) * CT * L + ct * L, (1, L))

        def win_dst(n):
            ct, g = divmod(n, 16)
            return sl(win, 0, WIN, ct * P * BLK + 4 * g, (BLK, P), (1, 4))

        def blk_dst(n):
            k, i = divmod(n, 8)
            if k == 1:
                return sl(oT, 0, P, i * 2 * P, (P, 2), (TOK, CT), (1, P))
            return sl((v_blk, None, o_blk)[k], 0, P, i * 512, (1, 512))

        def blk_src(n):
            if n // 8 == 1:
                return bank(n % 4, 0, P, 0, (256, 2), (P, CT), (1, P))
            return bank(n % 4, 0, P, 0, (1, 512))

        def fir_dst(n):
            return sl(fir, 0, P, 4 * n, (P, C), (C * P, NF), (1, 4))

        def fir_src(n):
            return bank(6 + n % 2, 0, P, (C - 1) * NF, (-NF, C), (1, NF), (C * NF, 4))

        def stats_dst(n, ct):
            return sl(statsT, DV * ct, 40, 4 * n, (1, 4), (C, BLK))

        def on_dst(n):
            return sl(onT, 0, P, 4 * n, (1, 4), (TOK, CT), (C, BLK))

        def on_src(n):
            return bank(n % 4, 0, P, 0, (P, 4), (DV, CT), (1, DV))

        def p_dst(buf, r, g):
            g0, count, rows = group(g)
            return sl(buf, 0, rows, g0 * 2 * P + (r % 2) * P, (2 * P, count), (1, P))

        block = ctx.enter_context(nc.Block())

        @block.sync
        def _(sp):
            sp.dma_start(sl(xT, 0, P, 0, (TOK, CT), (1, L)),
                         dr(a["xT"], 0, (TOK, P), (P * TOK, CT), (1, L))).then_inc(s_x[0], 16)
            for i, w in enumerate((a["Wv"], a["Wk"], a["Wq"])):
                sp.dma_start(sl(w_in, 0, P, i * D, (3 * D, CT), (1, D)),
                             w.rearrange("(c p) n -> p c n", p=P)).then_inc(s_win, 16)
            sp.dma_start(sl(w_beta, 0, P, 0, (H, CT), (1, H)),
                         a["Wb"].rearrange("(c p) n -> p c n", p=P)).then_inc(s_win, 16)
            for i, w in enumerate((a["conv_v"], a["conv_k"], a["conv_q"])):
                sp.dma_start(sl(conv_w, 0, P, i * CONV_K, (3 * CONV_K, CT), (1, CONV_K)),
                             w.rearrange("(c p) k -> p c k", p=P)).then_inc(s_const, 16)
            sp.dma_start(ident, a["ident"]).then_inc(s_const, 16)
            sp.dma_start(mask_gram, a["mask_gram"]).then_inc(s_const, 16)
            sp.dma_start(mask_heads, a["mask_heads"]).then_inc(s_const, 16)
            sp.dma_start(eps_col, a["eps"]).then_inc(s_const, 16)
            for b in range(1, NB):
                sp.dma_start(sl(xT, 0, P, b * L, (TOK, CT), (1, L)),
                             dr(a["xT"], b * L, (TOK, P), (P * TOK, CT), (1, L))).then_inc(s_x[b], 16)
            for ct in range(CT):
                half = (DV * ct, DV)
                sp.dma_start(sl(gb2_row, *half, 0, (1, 10)), dr(a["gb2"], 10 * ct, (0, DV), (1, 10))).then_inc(s_par, 16)
                sp.dma_start(sl(tau_in, *half, 0, (1, 2)), dr(a["log_tau"], 2 * ct, (0, DV), (1, 2))).then_inc(s_par, 16)
                sp.dma_start(sl(eps_row, *half, 0, (1, 10)), dr(a["eps_logit"], 10 * ct, (0, DV), (1, 10))
                             ).then_inc(s_par, 16)
                sp.dma_start(sl(nw_col, *half, 0, (1, 1)), a["norm_w"].rearrange("(a b) -> a b", b=1)).then_inc(s_par, 16)

            for s in range(SETS):
                sp.wait_ge(gram_masked, QC * TPS * (s + 1))
                for q in range(QC):
                    for h in range(2):
                        sp.dma_start(dr(a["scr_a"], s * P * C * C + (h * QC + q) * C * C,
                                        (C, C), (2 * QC * C * C, CT * TPS), (1, C)),
                                     sl(al, C * q, C, s * TPS * 256 + h * C, (P, CT * TPS), (1, C))).then_inc(a_out, 16)
                sp.wait_ge(a_out, 16 * 2 * QC * (s + 1))
                if s:
                    sp.wait_ge(solved, s)
                sp.dma_start(a_row, dr(a["scr_a"], s * P * C * C, (C * C, P), (1, C * C))).then_inc(a_in, 16)
                sp.wait_ge(solved, s + 1)
                sp.dma_start(dr(a["scr_u"], s * P * C * C, (C * C, P), (1, C * C)), u_row).then_inc(u_out, 16)
                sp.wait_ge(u_out, 16 * (s + 1))
                sp.wait_ge(zero_words, 1)
                for q in range(QC):
                    sp.dma_start(sl(ubd, C * q, C, s * TPS * H * P + C * q, (P, H * TPS), (1, C)),
                                 dr(a["scr_u"], s * P * C * C + q * C * C, (C, C), (QC * C * C, 4 * TPS), (1, C)),
                                 ).then_inc(u_in[s], 16)
            for s in range(SETS):
                sp.wait_ge(u_in[s], 16 * QC)
            sp.dma_start(sl(w2_sb, 0, P, 0, (20, 4), (1, 20)), a["gW2"].rearrange("(m p) n -> p m n", p=P)).then_inc(gate_in, 16)
            sp.dma_start(b1_col, a["gb1"]).then_inc(gate_in, 16)
            sp.dma_start(expand, a["expand"]).then_inc(gate_in, 16)

            def load_taps(n):
                if n >= 3:
                    sp.wait_ge(fir_mm, n - 2)
                for ct in range(CT):
                    sp.dma_start(sl(taps_ring, 0, WIN, (n % 3) * 768 + ct * 384, (96, 4), (1, 96)),
                                 dr(a["taps"], (ct * P + 4 * n) * NF * (WIN + C - 1),
                                    (NF, WIN), (NF * (WIN + C - 1), 4), (1, C * NF))).then_inc(taps_in[n % 3], 16)

            for n in range(3):
                load_taps(n)
            for n in range(3, 32):
                load_taps(n)
            sp.wait_ge(win_mm, 1)
            sp.dma_start(sl(xT2, 0, P, 0, (TOK, CT), (1, TOK)), a["xT"].rearrange("(c p) n -> p c n", p=P)).then_inc(xT2_in, 16)
            sp.wait_ge(fir_mm, 32)
            sp.dma_start(sl(w1_x, 0, P, 0, (HF, CT), (1, HF)), a["gW1"][0:D, :].rearrange("(c p) n -> p c n", p=P)).then_inc(w1x_in, 16)
            sp.dma_start(sl(w_o, 0, P, 0, (D, CT), (1, D)), a["Wo"].rearrange("(c p) n -> p c n", p=P)).then_inc(wo_in, 16)
            sp.wait_ge(w1s_mm, 1)
            for i, (name, w) in enumerate((("wgT", w_g), ("wuT", w_u), ("wdT", w_d))):
                if i:
                    sp.wait_ge(int_done, i)
                n = a[name].shape[1]
                sp.dma_start(sl(stage_i, 0, P, 0, (n, 1536 // n), (1, n)).bitcast(I32),
                             a[name].rearrange("(c p) n -> p c n", p=P)).then_inc(int_in, 16)
            sp.wait_ge(mix_dve, 6)
            for w, name in ((x_q, "xWq"), (x_k, "xWk"), (x_v, "xWv"), (x_oT, "xWoT")):
                sp.dma_start(sl(w, 0, P, 0, (D, CT), (1, D)), a[name].rearrange("(c p) n -> p c n", p=P)).then_inc(wts_in, 16)
            sp.dma_start(bq_col, a["xbq"]).then_inc(wts_in, 16)
            sp.dma_start(bv_col, a["xbv"]).then_inc(wts_in, 16)
            sp.wait_ge(mix_sum, 1)
            sp.dma_start(bo_row, dr(a["xbo"], 0, (0, P), (1, D))).then_inc(wts_in, 16)
            for t in range(0, TILES, TPB):
                sp.dma_start(sl(x1, 0, P, t * D, (D, TPB), (1, D)),
                             dr(a["x"], t * P * D, (D, P), (P * D, TPB), (1, D))).then_inc(x_in[t // TPB], 16)

            def load_ctx_t(b):
                if b == 0:
                    sp.wait_ge(lg_mm, 1)
                if b >= 2:
                    sp.wait_ge(scored, 4 * TPB * (b - 1))
                sp.dma_start(loaded(sl(ctx_t, 0, P, (b % 2) * CT * S_PAD, (S_PAD, CT), (1, S_CTX))),
                             dr(a["ctxT"], b * D * S_CTX, (S_CTX, P), (P * S_CTX, CT), (1, S_CTX))
                             ).then_inc(ctx_in[b % 2], 16)

            def load_ctx_n(b):
                n = S_CTX // P
                if b:
                    bk, i = misc("pv", b - 1, 1)
                    sp.wait_ge(full[bk - 6], i + 1)
                sp.dma_start(loaded(sl(ctx_n, 0, P, 0, (D, n), (1, D))),
                             dr(a["ctx"], b * S_CTX * D, (D, P), (P * D, n), (1, D))).then_inc(ctxn_in, 16)
                sp.dma_start(loaded(sl(ctx_n, 0, S_CTX - n * P, n * D, (1, D))),
                             dr(a["ctx"], (b * S_CTX + n * P) * D, (D, S_CTX - n * P), (1, D))).then_inc(ctxn_in, 16)

            def store(b):
                sp.wait_ge(y_ready, TPB * (b + 1))
                sp.dma_start(dr(out, b * L * D, (D, P), (P * D, TPB), (1, D)),
                             sl(y_out, 0, P, 0, (D, TPB), (1, D))).then_inc(stored, 16)

            load_ctx_t(0)
            load_ctx_t(1)
            load_ctx_n(0)
            for b in range(NB):
                if b + 2 < NB:
                    load_ctx_t(b + 2)
                if b:
                    store(b - 1)
                if b + 1 < NB:
                    load_ctx_n(b + 1)
            store(NB - 1)
            sp.wait_ge(stored, 16 * NB)

        @block.gpsimd
        def _(pool):
            pool.memset(sl(vT, 0, P, -HALO, (1, HALO)), 0.0).then_inc(zeroed, 1)
            pool.memset(bd, 0.0).then_inc(zeroed, 1)

            def normalise(b):
                pool.wait_ge(rn_done, b + 1)
                pool.wait_ge(zeroed, 2)
                pool.wait_ge(u_init, 2)
                if b:
                    pool.wait_ge(back_turned, TPB * b)
                    pool.wait_ge(wq_q, 2 * TPB * b)
                pool.tensor_tensor(sl(qn, 0, P, 0, (D, TPB), (DV, H), (1, DV)),
                                   sl(raw, 0, P, D, (2 * D, TPB), (DV, H), (1, DV)),
                                   sl(rn, 0, P, H, (8, TPB), (1, H), (0, DV)), ALU.mult).then_inc(qn_done, 1)

            def turn_back(t):
                pool.wait_ge(back_act, t + 1)
                pool.wait_ge(back_dve, t + 1)
                for h in range(2):
                    pool.wait_ge(qn_done, (t // TPB) + 1)
                    if t or h:
                        pool.wait_ge(wq_q, 2 * t + h)
                    pool.tensor_copy(
                        sl(wq, DV * h, DV, t * QC * 2 * C + C, (NCHUNK * 2 * C, CT), (2 * C, QC), (1, C)),
                        sl(bd, DV * h, DV, (t % 2) * CT * 512 + 256 + h * P, (512, CT), (C, QC), (1, C))
                        ).then_inc(wq_q, 1)

            def start_solver():
                pool.memset(u_row, 0.0).then_inc(u_init, 1)
                pool.wait_ge(u_init, 1)
                pool.memset(sl(u_row, 0, P, 0, (C + 1, C)), 1.0).then_inc(u_init, 1)

            start_solver()
            for kind, n in ORDER:
                if kind == "normalise":
                    normalise(n)
                elif kind == "turn_back":
                    turn_back(n)
            pool.wait_ge(gram_done, TILES)
            pool.wait_ge(silu_done, NPROJ)
            pool.wait_ge(wq_q, 2 * TILES)
            pool.memset(ubd, 0.0).then_inc(zero_words, 1)
            pool.memset(state, 0.0).then_inc(zero_words, 1)
            pool.wait_ge(u_out, 16)
            pool.memset(u_row, 0.0).then_inc(u_init, 1)
            pool.wait_ge(u_init, 3)
            pool.memset(sl(u_row, 0, P, 0, (C + 1, C)), 1.0).then_inc(u_init, 1)

            pool.wait_ge(w_turned, TILES)
            pool.wait_ge(solved, SETS)
            pool.wait_ge(u_out, 16 * SETS)

            def load_w1(p):
                pool.dma_start(sl(w1_raw, 0, P, (p % 2) * 8 * HF, (1, 8 * HF)),
                               dr(a["gW1"], (D + p * 1024) * HF, (8 * HF, P), (1, 8 * HF))).then_inc(w1_in[p % 2], 16)

            load_w1(0)
            load_w1(1)
            adds = 0
            for p in range(NPATH):
                pool.wait_ge(w1_in[p % 2], 16 * (p // 2 + 1))
                r0 = (p % 2) * 8 * HF
                for n in (4, 2, 1):
                    if adds:
                        pool.wait_ge(w1_add, adds)
                    x = sl(w1_raw, 0, P, r0, (1, n * HF))
                    y = x if n > 1 else sl(w1_part, 0, P, p * HF, (1, HF))
                    pool.tensor_tensor(y, x, sl(w1_raw, 0, P, r0 + n * HF, (1, n * HF)), ALU.add).then_inc(w1_add, 1)
                    adds += 1
                if p + 2 < NPATH:
                    pool.wait_ge(w1_add, adds)
                    load_w1(p + 2)

            pool.wait_ge(w1_add, adds)
            pool.wait_ge(win_act, 16)
            pool.wait_ge(win_dve, 16)
            pool.memset(sl(win, 0, HALO, 0, (BLK, CT * P), (BLK // NB, NB)), 0.0).then_inc(win_fixed, 1)
            pool.wait_ge(win_fixed, 1)
            pool.memset(sl(win, 0, C, 1, (BLK, CT * P), (BLK // NB, NB)), 0.0).then_inc(win_fixed, 1)
            pool.wait_ge(win_fixed, 2)
            pool.wait_ge(fir_mm, 32)
            pool.memset(statsT, 0.0).then_inc(statsT_zero, 1)

            pool.wait_ge(statsT_zero, 1)
            pool.wait_ge(wo_in, 16)
            pool.wait_ge(s_par, 16 * 8)
            pool.tensor_scalar(w_o, w_o, nw_col, None, ALU.mult).then_inc(wo_scaled, 1)
            pool.wait_ge(wo_scaled, 1)
            for i, w in enumerate((w_g, w_u, w_d)):
                pool.wait_ge(int_in, 16 * (i + 1))
                if i:
                    pool.wait_ge(int_done, i)
                pool.tensor_scalar(w, stage_i.bitcast(I32), 1.0 / 127.0, None, ALU.mult).then_inc(int_done, 1)
            pool.wait_ge(int_done, 3)

            pool.wait_ge(pr_ready, 1)
            pool.wait_ge(statsT_zero, 1)
            for p in range(2):
                if p:
                    pool.wait_ge(mix_pool, p)
                x = sl(PATHS[p], 0, P, 0, (DV, 2 * C), (1, DV))
                pool.tensor_tensor(x, x, sl(pr, 0, P, p, (NPATH, 2 * C), (0, DV)), ALU.mult).then_inc(mix_pool, 1)
            pool.wait_ge(mix_pool, 2)
            pool.tensor_tensor(PATHS[0], PATHS[0], PATHS[1], ALU.add).then_inc(mix_pool, 1)
            pool.wait_ge(mix_pool, 3)

            parts = [(wg_h, w_g), (wu_h, w_u)] + [(wd_h[m], w_d[:, D * m:D * (m + 1)]) for m in range(FT)]
            pool.wait_ge(on_mm, 8)
            pool.wait_ge(mix_sum, 1)
            for buf, n in ((ctxt_h, CT), (ctx_t, 2 * CT)):
                pool.tensor_scalar(r32(sl(buf, 0, P, S_CTX, (S_PAD, n))), ident[:, 0:n], 0.0, None, ALU.mult
                                   ).then_inc(zero_words, 1)
            for i, (high, w) in enumerate(parts):
                if i:
                    pool.wait_ge(w_split, 2 * i)
                pool.tensor_copy(r32(high), w).then_inc(w_split, 1)
                pool.wait_ge(w_split, 2 * i + 1)
                pool.tensor_tensor(r32(w), w, high_of(high), ALU.subtract).then_inc(w_split, 1)
            pool.wait_ge(w_split, 2 * len(parts))

            pool.wait_ge(wo_mm, TILES)
            pool.wait_ge(bvo_ready, 1)
            done = 0
            for b in range(NB):
                pool.wait_ge(ctxn_in, 32 * (b + 1))
                for g in range(5):
                    rows, off, n = (P, 3 * g * D, 3 * D) if g < 4 else (KV[12], 12 * D, D)
                    raw_n, high = sl(ctx_n, 0, rows, off, (1, n)), sl(ctxn_h, 0, rows, off, (1, n))
                    if done:
                        pool.wait_ge(ctxn_ready, done)
                    pool.tensor_copy(r32(high), loaded(raw_n)).then_inc(ctxn_ready, 1)
                    pool.wait_ge(ctxn_ready, done + 1)
                    pool.tensor_tensor(r32(raw_n), loaded(raw_n), high_of(high), ALU.subtract).then_inc(ctxn_ready, 1)
                    done += 2
                pool.wait_ge(ctxn_ready, done)
                for i in range(2):
                    bk, j = misc("turn_x1", b, i)
                    pool.wait_ge(full[bk - 6], j + 1)
                x = sl(x1, 0, P, b * TPB * D, (D, TPB), (1, D))
                pool.tensor_tensor(x, x, sl(b_vo, 0, P, 0, (0, TPB), (1, D)), ALU.add).then_inc(x1_bias, 1)
                pool.wait_ge(x1_bias, b + 1)

        @block.scalar
        def _(act):
            def silu(n):
                act.wait_ge(conv_done, n + 1)
                b, j = divmod(n, 6)
                if j >= 2 and b >= 2:
                    act.wait_ge(kq_turned, TPB * (b - 1))
                if n == 0:
                    act.wait_ge(zeroed, 1)
                act.activation(silu_dst(n), y_of(n), ACT.Silu).then_inc(silu_done, 1)

            def project(n):
                if n < NPROJ:
                    b, j = divmod(n, 6)
                    proj, ct = divmod(j, 2)
                    act.wait_ge(projected, n + 1)
                    if n >= 2:
                        act.wait_ge(silu_done, n - 1)
                    act.activation(y_of(n), bank(n % 2, 0, P, 0, (1, L)), ACT.Copy,
                                   scale=sl(conv_w, 0, P, ct * 12 + proj * CONV_K + CONV_K - 1, (1, 1))
                                   ).then_inc(tap_first, 1)
                if n:
                    silu(n - 1)

            def turn(t):
                b, r = divmod(t, TPB)
                if t == 0:
                    act.wait_ge(beta_mm, 1)
                    act.activation(beta, bank(7, 0, P, 0, (1, TILES * H)), ACT.Sigmoid).then_inc(beta_ready, 1)
                act.wait_ge(kq_turned, t + 1)
                if b and r == 0:
                    act.wait_ge(kn_done, b)
                    act.wait_ge(qn_done, b)
                act.activation(sl(raw, 0, P, r * 2 * D, (1, 2 * D)), bank(2, 0, P, 0, (1, 512)), ACT.Copy)
                if t:
                    act.wait_ge(ss_done, t)
                act.activation(sq, bank(2, 0, P, 0, (1, 512)), ACT.Square).then_inc(raw_done, 1)

            def normalise(b):
                act.wait_ge(ss_done, TPB * (b + 1))
                if b:
                    act.wait_ge(rn_done, b)
                act.activation(nrm, ss, ACT.Sqrt, bias=sl(eps_col, 0, P, 0, (1, 1))).then_inc(sqrt_done, 1)

            def turn_back(t):
                act.wait_ge(back_turned, t + 1)
                if t >= 2:
                    act.wait_ge(gram_done, t - 1)
                    act.wait_ge(wq_q, 2 * (t - 1))
                if t == 0:
                    act.wait_ge(zeroed, 2)
                act.activation(sl(knT, 0, P, (t % 2) * CT * P, (1, CT * P)), bank(4, 0, P, 0, (1, CT * P)), ACT.Copy)
                act.activation(sl(bd, 0, DV, (t % 2) * CT * 512, (256, 2 * CT), (1, P)),
                               bank(5, 0, DV, 0, (P, 2 * CT), (1, P)), ACT.Copy).then_inc(back_act, 1)

            act.wait_ge(s_const, 16 * 7)
            for kind, n in ORDER:
                if kind == "project":
                    project(n)
                elif kind == "turn":
                    turn(n)
                elif kind == "normalise":
                    normalise(n)
                elif kind == "turn_back":
                    turn_back(n)

            for t in range(TILES + 1):
                if t < TILES and t % 2 == 0:
                    act.wait_ge(uw_mm, t + 1)
                    act.activation(sl(vk, 0, P, t * 512, (D, 2), (DV, H), (1, DV)), bank(0, 0, P, 0, (DV, 2), (P, H), (1, DV)), ACT.Copy
                                   ).then_inc(uw_act, 1)
                if t and t % 2 == 0:
                    act.wait_ge(w_turned, t)
                    act.activation(sl(wq, 0, P, (t - 1) * QC * 2 * C, (NCHUNK * 2 * C, CT), (2 * C, QC), (1, C)),
                                   bank(3, 0, P, 0, (P, CT), (C, QC), (1, C)), ACT.Copy).then_inc(w_act, 1)
            for n in range(STEPS):
                g, q = divmod(n, QC)
                for s in range(SETS):
                    act.wait_ge(o_mm[s], n + 1)
                    act.activation(sl(o_tok, C * q, C, (s * TPS + g) * D, (TPB * D, 2), (1, D)),
                                   bank(2 * s + n % 2, C, C, 0, (D, 2), (1, D)), ACT.Copy).then_inc(o_kept[s], 1)

            for n in range(0, 32, 2):
                act.wait_ge(win_mm, n + 1)
                act.activation(win_dst(n), bank(n % 4, 0, WIN, 0, (1, P), (P, 4)), ACT.Copy).then_inc(win_act, 1)
            for n in range(0, 24, 2):
                act.wait_ge(blk_mm, n + 1)
                act.activation(blk_dst(n), blk_src(n), ACT.Copy).then_inc(blk_act, 1)
            act.wait_ge(blk_act, 12)
            act.wait_ge(blk_dve, 12)
            for j, (p, h) in enumerate(STATS):
                if j < 2:
                    pass
                else:
                    act.wait_ge(stat_sq, j - 1)
                for n in range(*fir_between(j)):
                    act.wait_ge(fir_mm, n + 1)
                    act.activation(fir_dst(n), fir_src(n), ACT.Copy).then_inc(fir_act, 1)
                if p < NF:
                    act.wait_ge(fir_act, 16 * (h + 1))
                act.activation(sl(sqt, 0, P, (j % 2) * C * DV, (DV, C), (1, DV)), sl(PATHS[p], 0, P, h * DV, (P, C), (1, DV)),
                               ACT.Square).then_inc(sq_ready, 1)
            act.wait_ge(stat_sq, 2 * NPATH)
            act.activation(sl(st, 0, P, 3, (4, 320)), sl(st, 0, P, 1, (4, 320)), ACT.Sqrt).then_inc(st_norm, 1)
            act.wait_ge(par_dve, 2)
            act.activation(tau_inv, tau_t[:, 0:2], ACT.Exp, scale=-1.0).then_inc(par_act, 1)
            act.wait_ge(par_act, 1)
            act.activation(tau_t[:, 2:4], tau_inv, ACT.Ln, bias=1.0).then_inc(par_act, 1)
            act.activation(eps_row, eps_row, ACT.Sigmoid).then_inc(par_act, 1)
            act.wait_ge(statsT_zero, 1)
            for n in range(0, 8, 2):
                act.wait_ge(st_mm, n + 1)
                for ct in range(CT):
                    last = act.activation(stats_dst(n, ct), bank(4 + n % 4, 0, 40, ct * DV, (P, 4), (1, DV)), ACT.Copy)
                last.then_inc(st_act, 1)
            for n in range(16):
                b, m = divmod(n, 4)
                act.wait_ge(hid_mm, n + 1)
                act.activation(sl(hT, 0, P, m * TOK + b * L, (1, L)), bank(n % 4, 0, P, 0, (1, L)), ACT.Gelu,
                               bias=b1_col[:, m:m + 1]).then_inc(hid_act, 1)
            act.wait_ge(gate_step, 3)
            act.activation(pr, lg, ACT.Exp).then_inc(exp_done, 1)
            act.wait_ge(mix_dve, 6)
            act.activation(sqt, mix, ACT.Square).then_inc(mix_sq, 1)
            act.wait_ge(mix_sum, 1)
            act.activation(rs, r64, ACT.Sqrt, bias=eps_col[:, 1:2], scale=1.0 / DV).then_inc(mix_sq, 1)
            for n in range(0, 8, 2):
                act.wait_ge(on_mm, n + 1)
                act.activation(on_dst(n), on_src(n), ACT.Copy).then_inc(on_act, 1)

            for b in range(NB):
                act.wait_ge(agg, TPB * (b + 1))
                act.activation(rstd[:, TPB * b:TPB * b + TPB], sl(mv, 0, P, 2 * TPB * b + 1, (2, TPB)), ACT.Sqrt,
                               bias=eps_col[:, 1:2]).then_inc(sqrt1, 1)
            for i, w in enumerate((w_qk, w_vo)):
                act.wait_ge(fold_mm, i + 1)
                act.activation(w, bank(6 + i, 0, P, 0, (1, 512)), ACT.Copy).then_inc(fold_done, 1)
            act.wait_ge(fold_mm, 3)
            act.activation(bqk, bank(4, 0, P, 0, (1, 2)), ACT.Copy).then_inc(fold_done, 1)

            def filled(*step):
                bk, i = misc(*step)
                act.wait_ge(full[bk - 6], i + 1)
                return bk, free[bk - 6]

            def high_p(n):
                for g in range(4):
                    act.wait_ge(p_mm, 4 * n + g + 1)
                    g0, count, rows = group(g)
                    act.activation(r32(p_dst(pT_h, n, g)), bank(4 + g % 2, 0, rows, 0, (P, count), (1, P)),
                                   ACT.Copy).then_inc(p_high, 1)

            def high_h(k):
                act.wait_ge(h_product, k + 1)
                m = k % FT
                act.activation(r32(sl(hF_h, 0, P, m * 256, (1, 256))), sl(hF_l, 0, P, m * 256, (1, 256)),
                               ACT.Copy).then_inc(h_high, 1)

            for kind, b, i in TAIL:
                n = TPB * b + i
                if kind == "turn_x1":
                    bk, done = filled(kind, b, i)
                    act.activation(sl(x1T, 0, P, i * 256, (P, 2), (L, CT), (1, P)),
                                   bank(bk, 0, P, 0, (256, 2), (P, CT), (1, P)), ACT.Copy).then_inc(done, 1)
                elif kind == "qk":
                    bk, done = filled(kind, b, i)
                    act.activation(r32(sl(qk_h, 0, P, i * L, (1, L))), bank(bk, 0, P, 0, (1, L)), ACT.Identity,
                                   bias=bqk[:, i:i + 1]).then_inc(high_kept, 1)
                elif kind == "split_ctx":
                    act.wait_ge(ctx_in[b % 2], 16 * (b // 2 + 1))
                    if b:
                        act.wait_ge(scored, 4 * TPB * b)
                    off, w = ctx_cols(COLS[i])
                    act.activation(r32(sl(ctxt_h, 0, P, off, (S_PAD, CT), (1, w))),
                                   loaded(sl(ctx_t, 0, P, (b % 2) * CT * S_PAD + off, (S_PAD, CT), (1, w))), ACT.Copy
                                   ).then_inc(ctxt_high, 1)
                elif kind == "scores":
                    if n:
                        high_p(n - 1)
                    act.wait_ge(neg_ready, n + 1)
                    act.activation(sl(p_sb, 0, P, (n % 2) * 1664, (1, S_CTX)), bank(0, 0, P, 0, (1, S_CTX)), ACT.Exp,
                                   bias=sl(sm_neg, 0, P, n % 8, (1, 1)), scale=1.0 / 16.0,
                                   accum_out=sl(sm_sum, 0, P, n % 8, (1, 1))).then_inc(exped, 1)
                elif kind == "turn_last":
                    high_p(n)
                elif kind == "pv":
                    bk, done = filled(kind, b, i)
                    act.activation(sl(pcT, 0, P, i * 256, (L, CT), (1, 256)), bank(bk, 0, P, 0, (256, CT), (1, 256)),
                                   ACT.Copy).then_inc(done, 1)
                elif kind == "ffn":
                    bk, done = filled(kind, b, i)
                    k = 2 * FT * b + i
                    if k >= 2:
                        act.wait_ge(h_product, k - 1)
                    act.activation(sl(sg, 0, P, (k % 2) * 256, (1, 256)), bank(bk, 0, P, 0, (1, 256)), ACT.Silu
                                   ).then_inc(silu_g, 1)
                    if i % FT:
                        high_h(k - 1)
                    if i % FT == FT - 1:
                        high_h(k)
                if kind in ("post", "down") and i == TPB - 1:
                    k = 2 * b + (kind == "down")
                    act.wait_ge(agg, TILES + TPB * (k + 1))
                    act.activation(rstd2, sl(mv2, 0, P, 1, (2, TPB)), ACT.Sqrt, bias=eps_col[:, 1:2]).then_inc(sqrt2, 1)

        @block.tensor
        def _(pe):
            def betas():
                for b in range(NB):
                    pe.wait_ge(s_x[b], 16)
                for t in range(TILES):
                    for ct in range(CT):
                        last = pe.matmul(bank(7, 0, P, t * H, (1, H)), sl(xT, 0, P, ct * TOK + t * P, (1, P)),
                                         sl(w_beta, 0, P, ct * H, (1, H)), start=(ct == 0), stop=(ct == CT - 1))
                last.then_inc(beta_mm, 1)

            def project(n):
                if n >= NPROJ:
                    return
                b, j = divmod(n, 6)
                proj, ct = divmod(j, 2)
                if j == 0:
                    pe.wait_ge(s_x[b], 16)
                if n >= 2:
                    pe.wait_ge(conv_done, n - 1)
                for k in range(CT):
                    last = pe.matmul(bank(n % 2, 0, P, 0, (1, L)),
                                     sl(w_in, 0, P, k * 3 * D + proj * D + ct * P, (1, P)),
                                     sl(xT, 0, P, k * TOK + b * L, (1, L)), start=(k == 0), stop=(k == CT - 1))
                last.then_inc(projected, 1)

            def turn(t):
                b, r = divmod(t, TPB)
                if t == 0:
                    betas()
                    pe.wait_ge(s_const, 16 * 7)
                pe.wait_ge(silu_done, 6 * (b + 1))
                if t:
                    pe.wait_ge(raw_done, t)
                for kq in range(2):
                    for ct in range(CT):
                        last = pe.transpose(bank(2, 0, P, kq * D + ct * P, (1, P)),
                                            sl(qkT, 0, P, ((b % 2) * 2 + kq) * CT * L + ct * L + r * P, (1, P)), ident)
                last.then_inc(kq_turned, 1)
                if t:
                    pe.wait_ge(vb_done, t)
                for ct in range(CT):
                    last = pe.transpose(bank(3, 0, P, ct * P, (1, P)),
                                        sl(vT, 0, P, ct * TOK + t * P, (1, P)), ident)
                last.then_inc(v_turned, 1)

            def turn_back(t):
                b, r = divmod(t, TPB)
                pe.wait_ge(kb_done, b + 1)
                pe.wait_ge(qn_done, b + 1)
                if t:
                    pe.wait_ge(back_act, t)
                    pe.wait_ge(back_dve, t)
                for ct in range(CT):
                    pe.transpose(bank(4, 0, P, ct * P, (1, P)), sl(kn, 0, P, t * D + ct * P, (1, P)), ident)
                    pe.transpose(bank(5, 0, P, ct * 256, (1, P)),
                                 sl(vk, 0, P, t * 512 + D + ct * P, (1, P)), ident)
                    last = pe.transpose(bank(5, 0, P, ct * 256 + P, (1, P)),
                                        sl(qn, 0, P, r * D + ct * P, (1, P)), ident)
                last.then_inc(back_turned, 1)

            def gram(t):
                pe.wait_ge(back_act, t + 1)
                pe.wait_ge(back_dve, t + 1)
                if t:
                    pe.wait_ge(gram_masked, QC * t)
                for ct in range(CT):
                    last = pe.matmul(bank(6 + ct, 0, P, 0, (1, 512)), sl(knT, 0, P, ((t % 2) * CT + ct) * P, (1, P)),
                                     sl(bd, 0, P, ((t % 2) * CT + ct) * 512, (1, 512)), start=True, stop=True)
                last.then_inc(gram_done, 1)

            pe.wait_ge(s_win, 16 * 4)
            for kind, n in ORDER:
                if kind == "project":
                    project(n)
                elif kind == "turn":
                    turn(n)
                elif kind == "turn_back":
                    if n == 0:
                        pe.wait_ge(beta_ready, 1)
                    turn_back(n)
                elif kind == "gram":
                    gram(n)

            def make_uw(t):
                s = t // TPS
                pe.wait_ge(u_in[s], 16 * QC)
                if t == 0:
                    pe.wait_ge(conv_done, NPROJ)
                    pe.wait_ge(raw_done, TILES)
                    pe.wait_ge(vb_done, TILES)
                if t >= 2:
                    pe.wait_ge((uw_act, uw_dve)[t % 2], t // 2)
                for h in range(H):
                    last = pe.matmul(bank(t % 2, 0, P, h * P, (1, P)), sl(ubd, 0, P, (t * H + h) * P, (1, P)),
                                     sl(vk, 0, P, t * 512 + h * DV, (D, 2), (1, DV)), start=True, stop=True)
                last.then_inc(uw_mm, 1)

            def turn_w(t):
                pe.wait_ge((uw_act, uw_dve)[t % 2], t // 2 + 1)
                if t >= 2:
                    pe.wait_ge((w_dve, w_act)[t % 2], t // 2)
                for ct in range(CT):
                    last = pe.transpose(bank(2 + t % 2, 0, P, ct * P, (1, P)),
                                        sl(vk, 0, P, t * 512 + D + ct * P, (1, P)), ident)
                last.then_inc(w_turned, 1)

            for t in range(TILES + 1):
                if t < TILES:
                    make_uw(t)
                if t:
                    turn_w(t - 1)

            def scan_in(n, s):
                g, q = divmod(n, QC)
                if n == 0:
                    pe.wait_ge(w_act, TILES // 2)
                    pe.wait_ge(w_dve, TILES // 2)
                    pe.wait_ge(uw_act, TILES // 2)
                    pe.wait_ge(uw_dve, TILES // 2)
                    pe.wait_ge(wq_q, 2 * TILES)
                    pe.wait_ge(zero_words, 2)
                    pe.wait_ge(gram_masked, QC * TILES)
                else:
                    pe.wait_ge(state_ready[s], n)
                if n >= 2:
                    pe.wait_ge(o_kept[s], n - 1)
                for i in range(4):
                    b, ct = divmod(i, CT)
                    chunk = (s * TPS + b * TPB + g) * QC + q
                    last = pe.matmul(bank(2 * s + n % 2, 0, 2 * C, i * P, (1, P)),
                                     sl(wq, 0, P, (ct * NCHUNK + chunk) * 2 * C, (1, 2 * C)),
                                     sl(state, 0, P, (s * 4 + i) * P, (1, P)), start=(i == 0), stop=(i == 3),
                                     skip_group_check=True)
                last.then_inc(wq_mm[s], 1)

            def scan_out(n, s):
                g, q = divmod(n, QC)
                pe.wait_ge(u_ready[s], n + 1)
                for i in range(4):
                    b, ct = divmod(i, CT)
                    t = s * TPS + b * TPB + g
                    for h in range(2):
                        last = pe.matmul(bank(2 * s + n % 2, C, C, i * P + h * DV, (1, DV)),
                                         sl(al, C * q, C, ((t * CT + ct) * 4 + 2 + h) * C, (1, C)),
                                         sl(u_new, C * q, C, (s * 2 + n % 2) * 512 + i * P + h * DV, (1, DV)),
                                         start=False, stop=True, skip_group_check=True)
                last.then_inc(o_mm[s], 1)
                if n == STEPS - 1:
                    return
                for i in range(4):
                    b, ct = divmod(i, CT)
                    t = s * TPS + b * TPB + g
                    last = pe.matmul(bank(4 + s, 0, P, i * P, (1, P)), sl(kn, C * q, C, t * D + ct * P, (1, P)),
                                     sl(u_new, C * q, C, (s * 2 + n % 2) * 512 + i * P, (1, P)),
                                     start=(n == 0 and i == 0), stop=True, skip_group_check=True)
                last.then_inc(s_mm[s], 1)

            for n in range(STEPS):
                for s in range(SETS):
                    scan_in(n, s)
                for s in range(SETS):
                    scan_out(n, s)

            def ring(n, n_before, by_act, by_dve):
                if n >= 4:
                    pe.wait_ge((by_act, by_dve)[n % 2], (n - 4) // 2 + 1)

            for s in range(SETS):
                pe.wait_ge(o_kept[s], STEPS)
            for n in range(32):
                ct, g = divmod(n, 16)
                ring(n, 0, win_act, win_dve)
                for w in range(4):
                    last = pe.transpose(bank(n % 4, 0, WIN, w * P, (1, P)),
                                        sl(vT, 0, P, ct * TOK + (4 * g + w) * C - HALO, (1, WIN)), ident)
                last.then_inc(win_mm, 1)
            for n in range(24):
                k, i = divmod(n, 8)
                if n < 4:
                    pe.wait_ge((win_act, win_dve)[n % 2], 16)
                ring(n, 0, blk_act, blk_dve)
                if k == 1 and i == 0:
                    pass
                if k == 2:
                    pe.wait_ge(blk_act, 8)
                    pe.wait_ge(blk_dve, 8)
                for w in range(4):
                    if k == 1:
                        src = sl(o_tok, 0, P, i * 512 + w * P, (1, P))
                    else:
                        src = sl((vT, None, oT)[k], 0, P, 4 * i + w, (C, P))
                    last = pe.transpose(bank(n % 4, 0, P, w * P, (1, P)), src, ident)
                last.then_inc(blk_mm, 1)

            pe.wait_ge(win_fixed, 2)
            for n in range(32):
                pe.wait_ge(taps_in[n % 3], 32 * (n // 3 + 1))
                if n >= 2:
                    pe.wait_ge(fir_act, n - 1)
                for c in range(4):
                    for ct in range(CT):
                        last = pe.matmul(bank(6 + n % 2, DV * ct, DV, c * 96, (1, 96)),
                                         sl(win, 0, WIN, (ct * P + 4 * n + c) * BLK, (1, BLK)),
                                         sl(taps_ring, 0, WIN, (n % 3) * 768 + ct * 384 + c * 96, (1, 96)),
                                         start=True, stop=True, skip_group_check=True)
                last.then_inc(fir_mm, 1)

            pe.wait_ge(w1_add, 3 * NPATH)
            pe.wait_ge(gate_in, 48)
            for p in range(NPATH):
                last = pe.matmul(bank(4, 0, P, 0, (1, HF)), sl(expand, 0, P, p * P, (1, P)),
                                 sl(w1_part, 0, P, p * HF, (1, HF)), start=(p == 0), stop=(p == NPATH - 1))
            last.then_inc(w1s_mm, 1)
            def hidden_x(n):
                b, m = divmod(n, 4)
                for k in range(CT):
                    pe.matmul(bank(n % 4, 0, P, 0, (1, L)), sl(w1_x, 0, P, k * HF + m * P, (1, P)),
                              sl(xT2, 0, P, k * TOK + b * L, (1, L)), start=(k == 0), stop=False)

            pe.wait_ge(w1x_in, 16)
            pe.wait_ge(xT2_in, 16)
            for n in range(4):
                hidden_x(n)
            pe.wait_ge(st_ready, 1)
            pe.wait_ge(w1s_ready, 1)
            pe.wait_ge(fir_act, 32)
            for n in range(8):
                ring(n, 0, st_act, st_dve)
                for w in range(4):
                    last = pe.transpose(bank(4 + n % 4, 0, 40, w * P, (1, P)), sl(st, 0, P, (4 * n + w) * 40, (1, 40)), ident)
                last.then_inc(st_mm, 1)
            pe.wait_ge(st_act, 4)
            pe.wait_ge(st_dve, 4)
            for n in range(16):
                b, m = divmod(n, 4)
                if n >= 4:
                    pe.wait_ge(hid_act, n - 3)
                    hidden_x(n)
                pe.matmul(bank(n % 4, 0, P, 0, (1, L)), sl(w1_s, 0, P, m * P, (1, P)),
                          sl(statsT, 0, P, b * L, (1, L)), start=False, stop=True).then_inc(hid_mm, 1)
            for b in range(NB):
                pe.wait_ge(hid_act, 4 * (b + 1))
                if b >= 2:
                    pe.wait_ge(lT_dve, b - 1)
                for m in range(4):
                    last = pe.matmul(bank(6 + b % 2, 0, 20, 0, (1, L)), sl(w2_sb, 0, P, m * 20, (1, 20)),
                                     sl(hT, 0, P, m * TOK + b * L, (1, L)), start=(m == 0), stop=(m == 3))
                last.then_inc(lT_mm, 1)
            pe.wait_ge(lT_dve, NB)
            for j in range(C):
                for ct in range(CT):
                    last = pe.matmul(bank(5, DV * ct, DV, j * 10, (1, 10)), sl(lT, 0, 20, j, (C, BLK)),
                                     sl(ident, 0, 20, ct * 10, (1, 10)), start=True, stop=True, skip_group_check=True)
            last.then_inc(lg_mm, 1)

            pe.wait_ge(mix_step, 7)
            for n in range(8):
                ring(n, 0, on_act, on_dve)
                for w in range(4):
                    last = pe.transpose(bank(n % 4, 0, P, w * P, (1, P)), sl(mix, 0, P, (4 * n + w) * P, (1, P)), ident)
                last.then_inc(on_mm, 1)
            pe.wait_ge(on_act, 4)
            pe.wait_ge(on_dve, 4)
            pe.wait_ge(wo_scaled, 1)
            for t in range(TILES):
                if t >= 4:
                    pe.wait_ge(res1, t - 3)
                for k in range(CT):
                    last = pe.matmul(bank(t % 4, 0, P, 0, (1, D)), sl(onT, 0, P, k * TOK + t * P, (1, P)),
                                     sl(w_o, 0, P, k * D, (1, D)), start=(k == 0), stop=(k == CT - 1))
                last.then_inc(wo_mm, 1)
            pe.wait_ge(wts_in, 16 * 7)
            for i, (x, y) in enumerate(((x_q, x_k), (x_v, x_oT))):
                for m in range(CT):
                    for k in range(CT):
                        last = pe.matmul(bank(6 + i, 0, P, m * D, (1, D)), sl(x, 0, P, k * D + m * P, (1, P)),
                                         sl(y, 0, P, k * D, (1, D)), start=(k == 0), stop=(k == CT - 1),
                                         skip_group_check=True)
                last.then_inc(fold_mm, 1)
            for m in range(CT):
                for k in range(CT):
                    last = pe.matmul(bank(4, 0, P, m, (1, 1)), sl(x_k, 0, P, k * D + m * P, (1, P)),
                                     sl(bq_col, 0, P, k, (1, 1)), start=(k == 0), stop=(k == CT - 1))
            last.then_inc(fold_mm, 1)
            pe.wait_ge(bv_ready, 1)
            for k in range(CT):
                last = pe.matmul(bank(5, 0, P, 0, (1, D)), sl(bv_rep, 0, P, k * P, (1, P)), sl(x_oT, 0, P, k * D, (1, D)),
                                 start=(k == 0), stop=(k == CT - 1))
            last.then_inc(fold_mm, 1)

            pe.wait_ge(res1, TILES)

            def claim(*step):
                bk, i = misc(*step)
                if i:
                    pe.wait_ge(free[bk - 6], i)
                return bk, full[bk - 6]

            def freed(*step):
                bk, i = misc(*step)
                pe.wait_ge(free[bk - 6], i + 1)

            def product(dst, w_h, w_l, x_h, x_l, start, stop):
                w_h, w_l, x_h, x_l = (r32(x) for x in (w_h, w_l, x_h, x_l))
                pe.matmul(dst, w_h, x_h, start=start, stop=False)
                pe.matmul(dst, w_h, x_l, start=False, stop=False)
                return pe.matmul(dst, w_l, x_h, start=False, stop=stop)

            def turn_p(n, g):
                pe.wait_ge(exped, n + 1)
                if 4 * n + g >= 2:
                    pe.wait_ge(p_kept, 4 * n + g - 1)
                g0, count, rows = group(g)
                for w in range(count):
                    last = pe.transpose(bank(4 + g % 2, 0, rows, w * P, (1, P)),
                                        sl(p_sb, 0, P, (n % 2) * 1664 + (g0 + w) * P, (1, rows)), ident)
                last.then_inc(p_mm, 1)

            pe.wait_ge(fold_done, 3)
            pe.wait_ge(bvo_ready, 1)
            pe.wait_ge(zero_words, 4)
            for kind, b, i in TAIL:
                n = TPB * b + i
                if (kind, b, i) in MISC:
                    bk, done = claim(kind, b, i)
                if kind == "turn_x1":
                    pe.wait_ge(x1_ready, TPB * (b + 1))
                    for w in range(4):
                        t, ct = divmod(w, CT)
                        last = pe.transpose(bank(bk, 0, P, w * P, (1, P)),
                                            sl(x1, 0, P, (TPB * b + 2 * i + t) * D + ct * P, (1, P)), ident)
                    last.then_inc(done, 1)
                elif kind == "qk":
                    for k in range(2):
                        freed("turn_x1", b, k)
                    for k in range(CT):
                        last = pe.matmul(bank(bk, 0, P, 0, (1, L)), sl(w_qk, 0, P, k * D + i * P, (1, P)),
                                         sl(x1T, 0, P, k * L, (1, L)), start=(k == 0), stop=(k == CT - 1))
                    last.then_inc(done, 1)
                elif kind == "scores":
                    if i == 0:
                        for k in range(CT):
                            freed("qk", b, k)
                    if n:
                        pe.wait_ge(exped, n)
                    for j, c in enumerate(COLS):
                        off, w = ctx_cols(c)
                        w += w % 2
                        if i == 0:
                            pe.wait_ge(ctxt_ready, 4 * b + j + 1)
                        for k in range(CT):
                            last = product(bank(c, 0, P, 0, (1, w)),
                                           sl(qk_h, 0, P, k * L + i * P, (1, P)), sl(qk_l, 0, P, k * L + i * P, (1, P)),
                                           sl(ctxt_h, 0, P, k * S_PAD + off, (1, w)),
                                           sl(ctx_t, 0, P, ((b % 2) * CT + k) * S_PAD + off, (1, w)),
                                           k == 0, k == CT - 1)
                        last.then_inc(scored, 1)
                        if n:
                            for g in TURNS[c]:
                                turn_p(n - 1, g)
                elif kind == "turn_last":
                    for g in range(4):
                        turn_p(n, g)
                elif kind == "pv":
                    pe.wait_ge(p_kept, 4 * (TPB * b + 2 * i + 2))
                    pe.wait_ge(ctxn_ready, 10 * (b + 1))
                    for m in range(CT):
                        for g, kv in enumerate(KV):
                            at_c, at_p = g * D + m * P, g * 2 * P
                            last = product(bank(bk, 0, P, m * 256, (1, 256)),
                                           sl(ctxn_h, 0, kv, at_c, (1, P)), sl(ctx_n, 0, kv, at_c, (1, P)),
                                           sl(pT_h, 0, kv, at_p, (1, 256)), sl(pT_l, 0, kv, at_p, (1, 256)),
                                           g == 0, g == 12)
                    last.then_inc(done, 1)
                elif kind == "post":
                    for k in range(2):
                        freed("pv", b, k)
                    for k in range(CT):
                        last = pe.matmul(bank(bk, 0, P, 0, (1, D)), sl(pcT, 0, P, k * L + i * P, (1, P)),
                                         sl(w_vo, 0, P, k * D, (1, D)), start=(k == 0), stop=(k == CT - 1))
                    last.then_inc(done, 1)
                elif kind == "turn_x2":
                    pe.wait_ge(x2_ready, TPB * (b + 1))
                    for w in range(4):
                        t, ct = divmod(w, CT)
                        last = pe.transpose(bank(bk, 0, P, w * P, (1, P)),
                                            sl(x2, 0, P, (2 * i + t) * D + ct * P, (1, P)), ident)
                    last.then_inc(done, 1)
                elif kind == "ffn":
                    pair, m = divmod(i, FT)
                    freed("turn_x2", b, pair)
                    pe.wait_ge(w_split, 2 * (2 + FT))
                    for to, (w_h, w_l) in enumerate(((wg_h, w_g), (wu_h, w_u))):
                        for k in range(CT):
                            last = product(bank(bk, 0, P, to * 256, (1, 256)),
                                           sl(w_h, 0, P, k * HID + m * P, (1, P)), sl(w_l, 0, P, k * HID + m * P, (1, P)),
                                           sl(x2T_h, 0, P, k * 256, (1, 256)), sl(x2T_l, 0, P, k * 256, (1, 256)),
                                           k == 0, k == CT - 1)
                    last.then_inc(done, 1)
                elif kind == "down":
                    pe.wait_ge(h_ready, FT * (2 * b + i // 2 + 1))
                    for m in range(FT):
                        at_h = m * 256 + (i % 2) * P
                        last = product(bank(bk, 0, P, 0, (1, D)),
                                       sl(hF_h, 0, P, at_h, (1, P)), sl(hF_l, 0, P, at_h, (1, P)),
                                       wd_h[m], sl(w_d, 0, P, m * D, (1, D)), m == 0, m == FT - 1)
                    last.then_inc(done, 1)

        @block.vector
        def _(dve):
            def project(n):
                if n >= NPROJ:
                    return
                b, j = divmod(n, 6)
                proj, ct = divmod(j, 2)
                dve.wait_ge(tap_first, n + 1)
                for k in range(1, CONV_K):
                    if k > 1:
                        dve.wait_ge(tap_step, 2 * n + k - 1)
                    y = sl(y_buf, 0, P, (n % 2) * L + k, (1, L - k))
                    dve.scalar_tensor_tensor(
                        out=y, in0=bank(n % 2, 0, P, 0, (1, L - k)),
                        scalar=sl(conv_w, 0, P, ct * 12 + proj * CONV_K + CONV_K - 1 - k, (1, 1)), in1=y,
                        op0=ALU.mult, op1=ALU.add).then_inc(tap_step if k < CONV_K - 1 else conv_done, 1)

            def turn(t):
                b, r = divmod(t, TPB)
                dve.wait_ge(raw_done, t + 1)
                if b and r == 0:
                    dve.wait_ge(sqrt_done, b)
                dve.tensor_reduce(sl(ss, 0, P, r * 8, (1, 8)), sl(sq, 0, P, 0, (DV, 8), (1, DV)), AX.X, ALU.add
                                  ).then_inc(ss_done, 1)
                dve.wait_ge(v_turned, t + 1)
                if t == 0:
                    dve.wait_ge(beta_ready, 1)
                dve.tensor_tensor(sl(vk, 0, P, t * 512, (DV, H), (1, DV)), bank(3, 0, P, 0, (DV, H), (1, DV)),
                                  sl(beta, 0, P, t * H, (1, H), (0, DV)), ALU.mult).then_inc(vb_done, 1)

            def normalise(b):
                dve.wait_ge(sqrt_done, b + 1)
                if b:
                    dve.wait_ge(qn_done, b)
                dve.reciprocal(rn, nrm).then_inc(rn_done, 1)
                dve.wait_ge(rn_done, b + 1)
                knb = sl(kn, 0, P, b * TPB * D, (D, TPB), (DV, H), (1, DV))
                dve.tensor_tensor(knb, sl(raw, 0, P, 0, (2 * D, TPB), (DV, H), (1, DV)),
                                  sl(rn, 0, P, 0, (8, TPB), (1, H), (0, DV)), ALU.mult).then_inc(kn_done, 1)
                dve.wait_ge(kn_done, b + 1)
                dve.tensor_tensor(sl(vk, 0, P, b * TPB * 512 + D, (512, TPB), (DV, H), (1, DV)),
                                  sl(kn, 0, P, b * TPB * D, (D, TPB), (DV, H), (1, DV)),
                                  sl(beta, 0, P, b * TPB * H, (H, TPB), (1, H), (0, DV)), ALU.mult).then_inc(kb_done, 1)

            def turn_back(t):
                dve.wait_ge(back_turned, t + 1)
                if t >= 2:
                    dve.wait_ge(gram_done, t - 1)
                    dve.wait_ge(wq_q, 2 * (t - 1))
                if t == 0:
                    dve.wait_ge(zeroed, 2)
                dve.tensor_copy(sl(bd, DV, DV, (t % 2) * CT * 512 + P, (256, 2 * CT), (1, P)),
                                bank(5, DV, DV, 0, (P, 2 * CT), (1, P))).then_inc(back_dve, 1)

            def gram(t):
                dve.wait_ge(gram_done, t + 1)
                for q in range(QC):
                    dve.tensor_tensor(sl(al, C * q, C, t * 256, (P, CT), (C, 4), (1, C)),
                                      bank(6, C * q, C, C * q, (512, CT), (P, 4), (1, C)),
                                      sl(mask_gram, C * q, C, 0, (0, CT), (C, 4), (1, C)), ALU.mult
                                      ).then_inc(gram_masked, 1)

            steps_before = [0]

            def solve(s):
                dve.wait_ge(a_in, 16 * (s + 1))
                dve.wait_ge(u_init, 2 * (s + 1))
                for l in range(C - 1):
                    n = C - 1 - l
                    if l:
                        dve.wait_ge(solve_step, steps_before[0])
                    dve.tensor_tensor(sl(u_tmp, 0, P, 0, (n, l + 1), (1, n)),
                                      sl(u_row, 0, P, l, (C, l + 1), (0, n)),
                                      sl(a_row, 0, P, l * C + l + 1, (0, l + 1), (1, n)), ALU.mult
                                      ).then_inc(solve_step, 1)
                    steps_before[0] += 1
                    dve.wait_ge(solve_step, steps_before[0])
                    u = sl(u_row, 0, P, l + 1, (C, l + 1), (1, n))
                    last = dve.tensor_tensor(u, u, sl(u_tmp, 0, P, 0, (n, l + 1), (1, n)), ALU.add)
                    if l < C - 2:
                        last.then_inc(solve_step, 1)
                        steps_before[0] += 1
                last.then_inc(solved, 1)

            for kind, n in ORDER:
                if kind == "project":
                    project(n)
                elif kind == "turn":
                    turn(n)
                elif kind == "normalise":
                    normalise(n)
                elif kind == "turn_back":
                    turn_back(n)
                elif kind == "gram":
                    gram(n)
            for s in range(SETS):
                solve(s)
            dve.wait_ge(s_const, 16 * 7)
            for t in range(TILES + 1):
                if t < TILES and t % 2 == 1:
                    dve.wait_ge(uw_mm, t + 1)
                    dve.tensor_copy(sl(vk, 0, P, t * 512, (D, 2), (DV, H), (1, DV)), bank(1, 0, P, 0, (DV, 2), (P, H), (1, DV))).then_inc(uw_dve, 1)
                if t % 2 == 1:
                    dve.wait_ge(w_turned, t)
                    dve.tensor_copy(sl(wq, 0, P, (t - 1) * QC * 2 * C, (NCHUNK * 2 * C, CT), (2 * C, QC), (1, C)),
                                    bank(2, 0, P, 0, (P, CT), (C, QC), (1, C))).then_inc(w_dve, 1)

            for n in range(STEPS):
                g, q = divmod(n, QC)
                for s in range(SETS):
                    dve.wait_ge(wq_mm[s], n + 1)
                    dve.tensor_tensor(sl(u_new, C * q, C, (s * 2 + n % 2) * 512, (D, 2), (DV, H), (1, DV)),
                                      sl(vk, C * q, C, (s * TPS + g) * 512, (TPB * 512, 2), (DV, H), (1, DV)),
                                      bank(2 * s + n % 2, 0, C, 0, (D, 2), (DV, H), (1, DV)), ALU.subtract
                                      ).then_inc(u_ready[s], 1)
                if n == STEPS - 1:
                    continue
                for s in range(SETS):
                    dve.wait_ge(s_mm[s], n + 1)
                    dve.tensor_tensor(sl(state, 0, P, s * 512, (P, 4), (1, P)), bank(4 + s, 0, P, 0, (P, 4), (1, P)),
                                      sl(mask_heads, 0, P, 0, (0, 4), (1, P)), ALU.mult).then_inc(state_ready[s], 1)

            for n in range(1, 32, 2):
                dve.wait_ge(win_mm, n + 1)
                dve.tensor_copy(win_dst(n), bank(n % 4, 0, WIN, 0, (1, P), (P, 4))).then_inc(win_dve, 1)
            for n in range(1, 24, 2):
                dve.wait_ge(blk_mm, n + 1)
                dve.tensor_copy(blk_dst(n), blk_src(n)).then_inc(blk_dve, 1)
            dve.wait_ge(blk_act, 12)
            dve.wait_ge(blk_dve, 12)
            for j, (p, h) in enumerate(STATS):
                if p < NF:
                    dve.wait_ge(fir_act, 16 * (h + 1))
                x = sl(PATHS[p], 0, P, h * DV, (P, C), (1, DV))
                to = p * 8 + h * 4
                dve.tensor_reduce(sl(st, 0, P, to, (40, C)), x, AX.X, ALU.add)
                dve.tensor_reduce(sl(st, 0, P, to + 2, (40, C)), x, AX.X, ALU.add,
                                  apply_absolute_value=True).then_inc(stat_abs, 1)
                dve.wait_ge(sq_ready, j + 1)
                dve.tensor_reduce(sl(st, 0, P, to + 1, (40, C)), sl(sqt, 0, P, (j % 2) * C * DV, (DV, C), (1, DV)),
                                  AX.X, ALU.add).then_inc(stat_sq, 1)
            dve.wait_ge(st_norm, 1)
            dve.wait_ge(stat_sq, 2 * NPATH)
            dve.wait_ge(stat_abs, 2 * NPATH)
            dve.tensor_scalar(sl(st, 0, P, 0, (4, 320), (1, 3)), sl(st, 0, P, 0, (4, 320), (1, 3)), 1.0 / DV, None,
                              ALU.mult).then_inc(st_ready, 1)
            dve.wait_ge(s_par, 16 * 8)
            dve.tensor_scalar(tau_t[:, 0:2], tau_in, -1.0, None, ALU.mult).then_inc(par_dve, 1)
            dve.wait_ge(par_dve, 1)
            dve.tensor_tensor(tau_t[:, 0:2], tau_t[:, 0:2], tau_in, ALU.max).then_inc(par_dve, 1)
            dve.wait_ge(par_act, 2)
            dve.tensor_scalar(tau_in, tau_in, 0.0, 0.5, ALU.max, ALU.add).then_inc(par_dve, 1)
            dve.wait_ge(par_dve, 3)
            dve.tensor_tensor(tau_in, tau_in, tau_t[:, 2:4], ALU.add).then_inc(par_dve, 1)
            dve.wait_ge(par_dve, 4)
            dve.reciprocal(tau_inv, tau_in).then_inc(par_dve, 1)

            dve.wait_ge(w1s_mm, 1)
            dve.tensor_copy(w1_s, bank(4, 0, P, 0, (1, HF))).then_inc(w1s_ready, 1)
            dve.wait_ge(statsT_zero, 1)
            for n in range(1, 8, 2):
                dve.wait_ge(st_mm, n + 1)
                for ct in range(CT):
                    last = dve.tensor_copy(stats_dst(n, ct), bank(4 + n % 4, 0, 40, ct * DV, (P, 4), (1, DV)))
                last.then_inc(st_dve, 1)
            dve.wait_ge(par_act, 3)
            dve.tensor_scalar(eps_row, eps_row, 0.2, None, ALU.mult).then_inc(par_dve, 1)
            dve.wait_ge(par_dve, 6)
            dve.tensor_reduce(eps_keep, sl(eps_row, 0, P, 0, (NPATH, 2), (1, NPATH)), AX.X, ALU.add).then_inc(par_dve, 1)
            dve.wait_ge(par_dve, 7)
            dve.tensor_scalar(eps_keep, eps_keep, -1.0, 1.0, ALU.mult, ALU.add).then_inc(par_dve, 1)

            for b in range(NB):
                dve.wait_ge(lT_mm, b + 1)
                dve.tensor_copy(sl(lT, 0, 20, b * L, (1, L)), bank(6 + b % 2, 0, 20, 0, (1, L))).then_inc(lT_dve, 1)
            dve.wait_ge(lg_mm, 1)
            dve.tensor_tensor(sl(lg, 0, P, 0, (10, C), (1, 10)), bank(5, 0, P, 0, (10, C), (1, 10)),
                              sl(gb2_row, 0, P, 0, (0, C), (1, 10)), ALU.add).then_inc(gate_step, 1)
            dve.wait_ge(gate_step, 1)
            dve.wait_ge(par_dve, 8)
            lg3 = sl(lg, 0, P, 0, (10, C), (NPATH, 2), (1, NPATH))
            dve.tensor_tensor(lg3, lg3, sl(tau_inv, 0, P, 0, (0, C), (1, 2), (0, NPATH)), ALU.mult).then_inc(gate_step, 1)
            dve.wait_ge(gate_step, 2)
            lg2 = sl(lg, 0, P, 0, (NPATH, 2 * C), (1, NPATH))
            dve.tensor_reduce(mx, lg2, AX.X, ALU.max).then_inc(mix_step, 1)
            dve.wait_ge(mix_step, 1)
            dve.tensor_tensor(lg2, lg2, sl(mx, 0, P, 0, (1, 2 * C), (0, NPATH)), ALU.subtract).then_inc(gate_step, 1)
            dve.wait_ge(exp_done, 1)
            pr2 = sl(pr, 0, P, 0, (NPATH, 2 * C), (1, NPATH))
            dve.tensor_reduce(sm, pr2, AX.X, ALU.add).then_inc(mix_step, 1)
            dve.wait_ge(mix_step, 2)
            dve.reciprocal(rs, sm).then_inc(mix_step, 1)
            dve.wait_ge(mix_step, 3)
            dve.tensor_tensor(sl(rs, 0, P, 0, (2, C), (1, 2)), sl(rs, 0, P, 0, (2, C), (1, 2)),
                              sl(eps_keep, 0, P, 0, (0, C), (1, 2)), ALU.mult).then_inc(mix_step, 1)
            dve.wait_ge(mix_step, 4)
            dve.tensor_tensor(pr2, pr2, sl(rs, 0, P, 0, (1, 2 * C), (0, NPATH)), ALU.mult).then_inc(mix_step, 1)
            dve.wait_ge(mix_step, 5)
            dve.tensor_tensor(sl(pr, 0, P, 0, (10, C), (1, 10)), sl(pr, 0, P, 0, (10, C), (1, 10)),
                              sl(eps_row, 0, P, 0, (0, C), (1, 10)), ALU.add).then_inc(pr_ready, 1)
            dve.wait_ge(pr_ready, 1)
            for p in range(2, NPATH):
                x = sl(PATHS[p], 0, P, 0, (DV, 2 * C), (1, DV))
                dve.tensor_tensor(x, x, sl(pr, 0, P, p, (NPATH, 2 * C), (0, DV)), ALU.mult).then_inc(mix_dve, 1)
            for i, x in enumerate((o_blk, v_blk, PATHS[0])):
                dve.wait_ge(mix_dve, 3 + i)
                if i == 2:
                    dve.wait_ge(mix_pool, 3)
                dve.tensor_tensor(mix, mix, x, ALU.add).then_inc(mix_dve, 1)
            dve.wait_ge(mix_sq, 1)
            dve.tensor_reduce(r64, sl(sqt, 0, P, 0, (DV, 2 * C), (1, DV)), AX.X, ALU.add).then_inc(mix_sum, 1)
            dve.wait_ge(mix_sq, 2)
            dve.reciprocal(r64, rs).then_inc(mix_step, 1)
            dve.wait_ge(mix_step, 6)
            x = sl(mix, 0, P, 0, (DV, 2 * C), (1, DV))
            dve.tensor_tensor(x, x, sl(r64, 0, P, 0, (1, 2 * C), (0, DV)), ALU.mult).then_inc(mix_step, 1)
            for n in range(1, 8, 2):
                dve.wait_ge(on_mm, n + 1)
                dve.tensor_copy(on_dst(n), on_src(n)).then_inc(on_dve, 1)
            dve.wait_ge(wts_in, 16 * 7)
            dve.tensor_copy(sl(bv_rep, 0, P, 0, (P, CT), (1, P)), sl(bv_col, 0, P, 0, (1, CT), (0, P))
                            ).then_inc(bv_ready, 1)

            for t in range(TILES):
                dve.wait_ge(wo_mm, t + 1)
                dve.wait_ge(x_in[t // TPB], 16)
                x = sl(x1, 0, P, t * D, (1, D))
                dve.tensor_tensor(x, x, bank(t % 4, 0, P, 0, (1, D)), ALU.add).then_inc(res1, 1)
                dve.wait_ge(res1, t + 1)
                if t:
                    dve.wait_ge(agg, t)
                dve.bn_stats(bn6, x).then_inc(bn, 1)
                dve.wait_ge(bn, t + 1)
                dve.bn_aggr(mv[:, 2 * t:2 * t + 2], bn6).then_inc(agg, 1)
                if t % TPB == TPB - 1:
                    b = t // TPB
                    dve.wait_ge(sqrt1, b + 1)
                    rb = rstd[:, TPB * b:TPB * b + TPB]
                    dve.reciprocal(rb, rb).then_inc(rstd1, 1)
                    dve.wait_ge(rstd1, b + 1)
                    for i in range(TPB * b, TPB * b + TPB):
                        x = sl(x1, 0, P, i * D, (1, D))
                        dve.tensor_scalar(x, x, mv[:, 2 * i:2 * i + 1], rstd[:, i:i + 1], ALU.subtract, ALU.mult
                                          ).then_inc(x1_ready, 1)

            dve.wait_ge(fold_mm, 4)
            dve.tensor_tensor(b_vo, bank(5, 0, P, 0, (1, D)), bo_row, ALU.add).then_inc(bvo_ready, 1)

            def filled(*step):
                bk, i = misc(*step)
                dve.wait_ge(full[bk - 6], i + 1)
                return bk, free[bk - 6]

            def statistics(k, i, x):
                n = TPB * k + i
                dve.wait_ge(res2, n + 1)
                dve.wait_ge(agg, TILES + n)
                if i == 0 and k:
                    dve.wait_ge(x2_ready if k % 2 else y_ready, TPB * ((k + 1) // 2))
                dve.bn_stats(bn6, x).then_inc(bn, 1)
                dve.wait_ge(bn, TILES + n + 1)
                dve.bn_aggr(mv2[:, 2 * i:2 * i + 2], bn6).then_inc(agg, 1)

            def centre(k, src, dst, done):
                dve.wait_ge(sqrt2, k + 1)
                dve.reciprocal(rstd2, rstd2).then_inc(rstd2_ready, 1)
                dve.wait_ge(rstd2_ready, k + 1)
                for i in range(TPB):
                    dve.tensor_scalar(sl(dst, 0, P, i * D, (1, D)), sl(src, 0, P, i * D, (1, D)),
                                      mv2[:, 2 * i:2 * i + 1], rstd2[:, i:i + 1], ALU.subtract, ALU.mult
                                      ).then_inc(done, 1)

            def low_p(n, g):
                dve.wait_ge(p_high, 4 * n + g + 1)
                g0, count, rows = group(g)
                dve.tensor_tensor(r32(p_dst(pT_l, n, g)), bank(4 + g % 2, 0, rows, 0, (P, count), (1, P)),
                                  high_of(p_dst(pT_h, n, g)), ALU.subtract).then_inc(p_kept, 1)

            def low_h(k):
                dve.wait_ge(h_high, k + 1)
                x = sl(hF_l, 0, P, k % FT * 256, (1, 256))
                dve.tensor_tensor(r32(x), x, high_of(sl(hF_h, 0, P, k % FT * 256, (1, 256))), ALU.subtract
                                  ).then_inc(h_ready, 1)

            for kind, b, i in TAIL:
                n = TPB * b + i
                if kind == "split_ctx":
                    dve.wait_ge(ctxt_high, 4 * b + i + 1)
                    off, w = ctx_cols(COLS[i])
                    x = sl(ctx_t, 0, P, (b % 2) * CT * S_PAD + off, (S_PAD, CT), (1, w))
                    dve.tensor_tensor(r32(x), loaded(x), high_of(sl(ctxt_h, 0, P, off, (S_PAD, CT), (1, w))), ALU.subtract
                                      ).then_inc(ctxt_ready, 1)
                elif kind == "qk":
                    bk, done = filled(kind, b, i)
                    dve.wait_ge(high_kept, 2 * b + i + 1)
                    dve.scalar_tensor_tensor(out=r32(sl(qk_l, 0, P, i * L, (1, L))),
                                             in0=bank(bk, 0, P, 0, (1, L)), scalar=bqk[:, i:i + 1],
                                             in1=high_of(sl(qk_h, 0, P, i * L, (1, L))), op0=ALU.add, op1=ALU.subtract
                                             ).then_inc(done, 1)
                elif kind == "turn_x2":
                    bk, done = filled(kind, b, i)
                    dve.tensor_copy(r32(sl(x2T_h, 0, P, 0, (P, 2), (256, CT), (1, P))),
                                    bank(bk, 0, P, 0, (256, 2), (P, CT), (1, P))).then_inc(x2_high, 1)
                    dve.wait_ge(x2_high, 2 * b + i + 1)
                    dve.tensor_tensor(r32(sl(x2T_l, 0, P, 0, (P, 2), (256, CT), (1, P))),
                                      bank(bk, 0, P, 0, (256, 2), (P, CT), (1, P)),
                                      high_of(sl(x2T_h, 0, P, 0, (P, 2), (256, CT), (1, P))), ALU.subtract).then_inc(done, 1)
                elif kind == "scores":
                    for j, c in enumerate(COLS):
                        dve.wait_ge(scored, 4 * n + j + 1)
                        off, w = ctx_cols(c)
                        last = dve.tensor_reduce(sl(sm_part, 0, P, c, (1, 1)), bank(c, 0, P, 0, (1, w)), AX.X, ALU.max)
                        if n:
                            for g in TURNS[c]:
                                low_p(n - 1, g)
                    last.then_inc(maxed, 1)
                    dve.wait_ge(maxed, 2 * n + 1)
                    dve.tensor_reduce(sl(sm_max, 0, P, n % 8, (1, 1)), sm_part, AX.X, ALU.max).then_inc(maxed, 1)
                    dve.wait_ge(maxed, 2 * n + 2)
                    dve.tensor_scalar(sl(sm_neg, 0, P, n % 8, (1, 1)), sl(sm_max, 0, P, n % 8, (1, 1)), -1.0 / 16.0,
                                      None, ALU.mult).then_inc(neg_ready, 1)
                elif kind == "turn_last":
                    for g in range(4):
                        low_p(n, g)
                elif kind == "post":
                    if i == 0:
                        dve.reciprocal(sl(sm_inv, 0, P, (b % 2) * TPB, (1, TPB)),
                                       sl(sm_sum, 0, P, (b % 2) * TPB, (1, TPB))).then_inc(inv_ready, 1)
                        dve.wait_ge(inv_ready, b + 1)
                        dve.wait_ge(x1_bias, b + 1)
                    bk, done = filled(kind, b, i)
                    x = sl(x1, 0, P, n * D, (1, D))
                    dve.scalar_tensor_tensor(out=x, in0=bank(bk, 0, P, 0, (1, D)),
                                             scalar=sl(sm_inv, 0, P, n % 8, (1, 1)), in1=x,
                                             op0=ALU.mult, op1=ALU.add).then_inc(res2, 1)
                    statistics(2 * b, i, x)
                    dve.sem_inc(done, 1)
                    if i == TPB - 1:
                        centre(2 * b, sl(x1, 0, P, b * TPB * D, (1, TPB * D)), x2, x2_ready)
                elif kind == "ffn":
                    bk, done = filled(kind, b, i)
                    k = 2 * FT * b + i
                    dve.wait_ge(silu_g, k + 1)
                    dve.tensor_tensor(sl(hF_l, 0, P, k % FT * 256, (1, 256)), sl(sg, 0, P, (k % 2) * 256, (1, 256)),
                                      bank(bk, 0, P, 256, (1, 256)), ALU.mult).then_inc(h_product, 1)
                    dve.wait_ge(h_product, k + 1)
                    dve.sem_inc(done, 1)
                    if i % FT:
                        low_h(k - 1)
                    if i % FT == FT - 1:
                        low_h(k)
                elif kind == "down":
                    bk, done = filled(kind, b, i)
                    x = sl(x2, 0, P, i * D, (1, D))
                    dve.tensor_tensor(x, x, bank(bk, 0, P, 0, (1, D)), ALU.add).then_inc(res2, 1)
                    statistics(2 * b + 1, i, x)
                    dve.sem_inc(done, 1)
                    if i == TPB - 1:
                        if b:
                            dve.wait_ge(stored, 16 * b)
                        centre(2 * b + 1, x2, y_out, y_ready)



def constants():
    import numpy as np

    row = np.arange(P)
    gram = np.zeros((P, 4, C), np.float32)
    behind = np.arange(C)[None, :] - (row % C)[:, None]
    gram[:, 0:2, :] = -(behind > 0).astype(np.float32)[:, None, :]
    gram[:, 2:4, :] = (behind >= 0).astype(np.float32)[:, None, :]
    heads = (row[:, None] // DV == row[None, :] // DV).astype(np.float32)
    h, kind = row // 32, row // 8 % 4
    expand = np.zeros((P, NPATH, P), np.float32)
    for p in range(NPATH):
        expand[row, p, 64 * (h // 2) + 8 * p + 4 * (h % 2) + kind] = 1.0
    eps = np.zeros((P, 4), np.float32)
    eps[:, 0], eps[:, 1] = 1e-6, LN_EPS
    return {"ident": np.eye(P, dtype=np.float32), "mask_gram": gram.reshape(P, -1), "mask_heads": heads,
            "expand": expand.reshape(P, -1), "eps": eps}


def laid_out(inputs):
    import numpy as np

    a, x, f = "L0_attn_", "L0_xattn_", "L0_ffn_"
    get = {k: np.asarray(v) for k, v in inputs.items()}
    own = {"xT": get["x"].reshape(TOK, D).T, "x": get["x"].reshape(TOK, D),
           "ctx": get["ctx_1024"].reshape(-1, D), "ctxT": get["ctx_1024"].transpose(0, 2, 1).reshape(NB * D, S_CTX)}
    for k in ("Wq", "Wk", "Wv", "Wb", "Wo", "conv_q", "conv_k", "conv_v", "gW1", "gW2", "gb2", "log_tau", "norm_w"):
        own[k] = get[a + k]
    own["gb1"] = get[a + "gb1"].reshape(-1, P).T
    own["eps_logit"] = get[a + "eps_logit"].reshape(-1)
    taps = np.zeros((D, WIN + C - 1, NF), np.float32)
    for i, k in enumerate(("fir_s", "fir_m", "fir_l")):
        taps[:, WIN - FIRS[i]:WIN, i] = get[a + k]
    own["taps"] = taps.reshape(D, -1)
    own.update({"xWq": get[x + "Wq"], "xWk": get[x + "Wk"], "xWv": get[x + "Wv"], "xWoT": get[x + "Wo"].T,
                "xbq": get[x + "bq"].reshape(CT, P).T, "xbv": get[x + "bv"].reshape(CT, P).T, "xbo": get[x + "bo"],
                "wgT": get[f + "w_gate"].T, "wuT": get[f + "w_up"].T, "wdT": get[f + "w_down"].T})
    own.update(constants())
    return {k: np.ascontiguousarray(v) for k, v in own.items()}


def kernel(**inputs):
    import concourse.bacc as bacc
    from concourse.bass_utils import run_bass_kernel_spmd

    nc = bacc.Bacc("TRN2", target_bir_lowering=False, num_devices=1)
    arrays = {f"in_{k}_dram": v for k, v in laid_out(inputs).items()}
    a = {k[3:-5]: nc.dram_tensor(k, list(v.shape), mybir.dt.from_np(v.dtype), kind="ExternalInput").ap()
         for k, v in arrays.items()}
    for k in ("scr_a", "scr_u"):
        a[k] = nc.dram_tensor(k, [2, P, C * C], F32, kind="Internal").ap()
    out = nc.dram_tensor("out_0_dram", [TOK, D], F32, kind="ExternalOutput").ap()
    build(nc, a, out)
    r = run_bass_kernel_spmd(nc, [arrays], core_ids=[0])
    return r.results[0]["out_0_dram"].reshape(NB, L, D)
```

```python
from contextlib import ExitStack

import concourse.bass as bass
from concourse import mybir

F32 = mybir.dt.float32
F32R = mybir.dt.float32r
I32 = mybir.dt.int32
ALU = mybir.AluOpType
ACT = mybir.ActivationFunctionType
AX = mybir.AxisListType

P = 128
NB, L, D, H = 4, 512, 256, 4
DV = D // H
CT = D // P
TOK = NB * L
TILES = TOK // P
TPB = L // P
C = 32
QC = P // C
NCHUNK = TOK // C
BLK = TOK // C
CONV_K = 4
SOLVE_AFTER = 9
FIRS = (3, 15, 64)
NF = len(FIRS)
HALO = 64
WIN = HALO + C
NPATH = 5
GATED = 4
CG = C // GATED
GT = TOK // GATED
HF = 2 * D
S_CTX = 1601
KV = [min(P, S_CTX - P * i) for i in range(-(-S_CTX // P))]
S_PAD = S_CTX + 1
HID = 768
FT = HID // P
LN_EPS = 1e-5


def sl(buf, p0, n, off, *dims):
    pitch = buf.ap[0][0]
    return bass.AP(buf.tensor, buf.offset + p0 * pitch + off, [[pitch, n]] + [[s, c] for s, c in dims])


def dr(x, off, *dims):
    return bass.AP(x.tensor, off, [[s, c] for s, c in dims])


def phase_one_order():
    steps = [(n, 0, "project", n) for n in range(6 * NB + 1)]
    for b in range(NB):
        t0 = 6 * (b + 1)
        for r in range(TPB):
            steps += [(t0 + 2 + r, 1, "turn", TPB * b + r), (t0 + 8 + r, 3, "turn_back", TPB * b + r),
                      (t0 + 9 + r, 4, "gram", TPB * b + r)]
        steps.append((t0 + 6, 2, "normalise", b))
    return [(kind, n) for _, _, kind, n in sorted(steps)]


def build(nc, a, out):
    with ExitStack() as ctx:
        WORDS = 53200
        with nc.sbuf_tensor("arena", [P, WORDS], F32) as arena:
            pass
        ps = ctx.enter_context(nc.psum_tensor("ps", [P, 8, 512], F32))
        psv = ps[:, :, :].rearrange("p b n -> p (b n)")

        def sem(name):
            return ctx.enter_context(nc.semaphore(name))

        def at(start, n):
            assert start + n <= WORDS
            return arena[:, start:start + n]

        def named(name, start, n, dtype):
            with nc.sbuf_tensor(f"below_{name}", [P, start], F32):
                with nc.sbuf_tensor(name, [P, n], dtype) as words:
                    return start, n, words[:, :]

        def within(views, x):
            p0, off = divmod(x.offset, WORDS)
            for start, n, words in views:
                if start <= off < start + n:
                    return bass.AP(words.tensor, p0 * n + off - start, [[n, x.ap[0][1]]] + [list(d) for d in x.ap[1:]])

        def r32(x):
            return within(OPERANDS, x)

        def high_of(x):
            return r32(x).bitcast(F32)

        def loaded(x):
            return within(LOADED, x)

        def bank(i, p0, n, off, *dims):
            return sl(psv, p0, n, 512 * i + off, *dims)

        ident = at(0, 128)
        mask_gram = at(128, 128)
        mask_heads = at(256, 128)
        eps_col = at(384, 4)
        conv_w = at(388, CT * 3 * CONV_K)
        beta = at(416, TILES * H)
        ss = at(480, TPB * 8)
        nrm = at(512, TPB * 8)
        rn = at(544, TPB * 8)
        vT = at(2048 + HALO, CT * TOK)
        kn = at(6656, TILES * D)
        vk = at(10752, TILES * H * 2 * DV)
        al = at(18944, TILES * CT * 4 * C)
        wq = at(23040, CT * NCHUNK * 2 * C)
        xT = at(31232, CT * TOK)
        o_tok = xT
        w_in = at(35328, CT * 3 * D)
        w_beta = at(36864, CT * H)
        y_buf = at(36880, 2 * L)
        qkT = at(37904, 2 * 2 * CT * L)
        raw = at(42000, TPB * 2 * D)
        sq = at(44048, 2 * D)
        qn = at(44688, TPB * D)
        knT = at(45712, 2 * CT * P)
        bd = at(46224, 2 * CT * 4 * P)
        a_row = at(48384, C * C)
        u_row = at(49408, C * C)
        u_tmp = at(50432, C * C)
        ubd = at(35328, 2 * 8 * H * P)
        state = at(43520, 2 * 4 * P)
        u_new = at(44544, 2 * 2 * 4 * P)

        SETS = 2
        s_const = sem("s_const")
        s_par = sem("s_par")
        s_x = [sem(f"s_x{b}") for b in range(NB)]
        s_win = sem("s_win")
        zeroed = sem("zeroed")
        beta_mm, beta_ready = sem("beta_mm"), sem("beta_ready")
        projected, tap_first, tap_step, conv_done, silu_done = (
            sem("projected"), sem("tap_first"), sem("tap_step"), sem("conv_done"), sem("silu_done"))
        kq_turned, v_turned = sem("kq_turned"), sem("v_turned")
        raw_done, ss_done, vb_done = sem("raw_done"), sem("ss_done"), sem("vb_done")
        sqrt_done, rn_done, kn_done, kb_done, qn_done = (
            sem("sqrt_done"), sem("rn_done"), sem("kn_done"), sem("kb_done"), sem("qn_done"))
        back_turned, back_act, wq_q = sem("back_turned"), sem("back_act"), sem("wq_q")
        gram_done, gram_masked = sem("gram_done"), sem("gram_masked")
        a_out, a_in, u_out, u_in = sem("a_out"), sem("a_in"), sem("u_out"), [sem(f"u_in{s}") for s in range(SETS)]
        u_init, solve_step, solved = sem("u_init"), sem("solve_step"), sem("solved")
        zero_words = sem("zero_words")
        uw_mm, uw_act, uw_dve = sem("uw_mm"), sem("uw_act"), sem("uw_dve")
        w_turned, w_act, w_dve = sem("w_turned"), sem("w_act"), sem("w_dve")
        wq_mm = [sem(f"wq_mm{g}") for g in range(2)]
        u_ready = [sem(f"u_ready{g}") for g in range(2)]
        o_mm = [sem(f"o_mm{g}") for g in range(2)]
        s_mm = [sem(f"s_mm{g}") for g in range(2)]
        state_ready = [sem(f"state_ready{g}") for g in range(2)]
        o_kept = [sem(f"o_kept{g}") for g in range(2)]

        win = at(6656, CT * P * BLK)
        fir = at(35328, NF * C * P)
        taps_ring = at(47616, 3 * CT * 4 * C * NF)
        expand = at(49920, NPATH * P)
        w1_part = at(50560, NPATH * HF)
        w1_raw = at(35328, 2 * 8 * HF)
        v_blk = at(23040, C * P)
        oT = at(2112, CT * TOK)
        o_blk = at(31232, C * P)
        xT2 = at(27136, CT * TOK)
        st = at(640, C * 40)
        w2_sb = at(1920, 4 * 20)
        b1_col, gb2_row, tau_in, tau_inv = at(2000, 4), at(2004, 10), at(2014, 2), at(2016, 2)
        eps_row, eps_keep, tau_t, nw_col = at(2018, 10), at(2028, 2), at(2030, 4), at(2034, 1)
        sqt = at(2112, C * P)
        hT = at(6656, 4 * TOK)
        statsT = at(14848, TOK)
        w1_s = at(16896, HF)
        w1_x = at(17408, CT * HF)
        lT = at(18432, TOK)
        pr, lg, mx, sm, rs, r64 = at(640, 320), at(960, 320), at(1280, 64), at(1344, 64), at(1408, 64), at(1472, 64)
        mix = sl(fir, 0, P, 2 * C * P, (1, C * P))
        onT = at(39936, CT * TOK)
        x1 = at(31232, TILES * D)
        w_o_in, w_o = at(20480, 512), at(44032, 512)
        stage_i = at(20992, 1536)
        w_qk, w_vo, b_vo = at(35328, 512), at(35840, 512), at(36352, 256)
        x_q, x_k, x_v, x_oT = (at(36608 + 512 * i, 512) for i in range(4))
        bv_rep = at(38656, CT * P)
        p_sb = at(36608, 2 * 1664)
        qk_h, qk_l = at(640, CT * L), at(1664, CT * L)
        ctx_t = at(6656, 2 * CT * S_PAD)
        ctxt_h = at(13064, CT * S_PAD)
        ctx_n, ctxn_h = at(16272, 13 * D), at(19600, 13 * D)
        pT_h, pT_l = at(22928, 13 * 2 * P), at(26256, 13 * 2 * P)
        x2T_h, x2T_l = at(44032, CT * 2 * P), at(44544, CT * 2 * P)
        hF_l, hF_h = at(40960, FT * 2 * P), at(42496, FT * 2 * P)
        w_g, w_u, w_d = at(47616, 1536), at(49152, 1536), at(50688, 1536)
        wg_h, wu_h = at(45056, 1536), at(5120, 1536)
        wd_h = [at(46592 + D * m if m < 4 else 52224 + D * (m - 4), D) for m in range(FT)]
        x1T = at(29584, CT * L)
        sg = at(30608, 2 * 2 * P)
        x2 = at(39936, TPB * D)
        pcT = at(2688, CT * L)
        y_out = at(3712, TPB * D)
        OPERANDS = [named(f"{name}_operand", start, n, F32R) for name, start, n in (
            ("qk_high", 640, CT * L), ("qk_low", 1664, CT * L), ("wu_high", 5120, 1536),
            ("ctxt_low", 6656, 2 * CT * S_PAD), ("ctxt_high", 13064, CT * S_PAD),
            ("ctxn_low", 16272, 13 * D), ("ctxn_high", 19600, 13 * D),
            ("pT_high", 22928, 26 * P), ("pT_low", 26256, 26 * P),
            ("hF_low", 40960, FT * 2 * P), ("hF_high", 42496, FT * 2 * P),
            ("x2T_high", 44032, CT * 2 * P), ("x2T_low", 44544, CT * 2 * P), ("wg_high", 45056, 1536),
            ("wd_high_first", 46592, 4 * D), ("wg_low", 47616, 1536), ("wu_low", 49152, 1536), ("wd_low", 50688, 1536),
            ("wd_high_last", 52224, 2 * D))]
        LOADED = [named("ctxt_loaded", 6656, 2 * CT * S_PAD, F32), named("ctxn_loaded", 16272, 13 * D, F32)]
        bn6, mv, rstd = at(388, 6), at(400, 32), at(432, 16)
        bqk, bq_col, bo_row = at(448, 2), at(450, 2), at(4736, 256)
        sm_max, sm_neg, sm_sum, sm_inv = at(456, 8), at(464, 8), at(472, 8), at(480, 8)
        mv2, rstd2 = at(488, 8), at(496, 4)
        bv_col = at(500, 2)
        sm_part = at(502, 4)

        win_mm, win_act, win_dve, win_fixed = sem("win_mm"), sem("win_act"), sem("win_dve"), sem("win_fixed")
        blk_mm, blk_act, blk_dve = sem("blk_mm"), sem("blk_act"), sem("blk_dve")
        fir_mm, fir_act = sem("fir_mm"), sem("fir_act")
        taps_in = [sem(f"taps_in{i}") for i in range(3)]
        w1_in = [sem(f"w1_in{i}") for i in range(2)]
        w1_add, w1x_in, xT2_in, gate_in = sem("w1_add"), sem("w1x_in"), sem("xT2_in"), sem("gate_in")
        par_act, par_dve = sem("par_act"), sem("par_dve")
        sq_ready, stat_abs, stat_sq, st_norm, st_ready = (
            sem("sq_ready"), sem("stat_abs"), sem("stat_sq"), sem("st_norm"), sem("st_ready"))
        statsT_zero, st_mm, st_act, st_dve = sem("statsT_zero"), sem("st_mm"), sem("st_act"), sem("st_dve")
        w1s_mm, w1s_ready, hid_mm, hid_act = sem("w1s_mm"), sem("w1s_ready"), sem("hid_mm"), sem("hid_act")
        lT_mm, lT_kept, lg_mm, gate_step, exp_done, pr_ready = (
            sem("lT_mm"), sem("lT_kept"), sem("lg_mm"), sem("gate_step"), sem("exp_done"), sem("pr_ready"))
        mix_pool, mix_dve, mix_sq, mix_sum = (
            sem("mix_pool"), sem("mix_dve"), sem("mix_sq"), sem("mix_sum"))
        on_mm, on_act, on_dve = sem("on_mm"), sem("on_act"), sem("on_dve")
        x_in = [sem(f"x_in{b}") for b in range(NB)]
        wts_in, wo_in, int_in, int_done = sem("wts_in"), sem("wo_in"), sem("int_in"), sem("int_done")
        wo_scaled, wo_mm, res1, bn, agg, sqrt1, rstd1, x1_ready = (
            sem("wo_scaled"), sem("wo_mm"), sem("res1"), sem("bn"), sem("agg"), sem("sqrt1"), sem("rstd1"), sem("x1_ready"))
        x1_bias = sem("x1_bias")
        fold_mm, fold_done, bvo_ready = sem("fold_mm"), sem("fold_done"), sem("bvo_ready")
        ctx_in = [sem(f"ctx_in{i}") for i in range(2)]
        ctxt_high, ctxt_ready, ctxn_in, ctxn_ready, w_split = (
            sem("ctxt_high"), sem("ctxt_ready"), sem("ctxn_in"), sem("ctxn_ready"), sem("w_split"))
        x2_high = sem("x2_high")
        scored, maxed, neg_ready, exped = sem("scored"), sem("maxed"), sem("neg_ready"), sem("exped")
        p_mm, p_high, p_kept, high_kept = sem("p_mm"), sem("p_high"), sem("p_kept"), sem("high_kept")
        full, free = [sem(f"bank_full{i}") for i in range(2)], [sem(f"bank_free{i}") for i in range(2)]
        inv_ready, res2, sqrt2, rstd2_ready, x2_ready = (
            sem("inv_ready"), sem("res2"), sem("sqrt2"), sem("rstd2_ready"), sem("x2_ready"))
        mix_step, bv_ready = sem("mix_step"), sem("bv_ready")
        silu_g, h_product, h_high, h_ready = sem("silu_g"), sem("h_product"), sem("h_high"), sem("h_ready")
        y_ready, stored = sem("y_ready"), sem("stored")

        PATHS = [sl(fir, 0, P, i * C * P, (1, C * P)) for i in range(NF)] + [o_blk, v_blk]
        STATS = [(4, 0), (4, 1), (3, 0), (3, 1)] + [(p, h) for h in range(2) for p in range(NF)]

        def fir_between(j):
            ends = (0, 2, 6, 10, 16, 20, 24, 32)
            return (ends[j - 1], ends[j]) if 0 < j < 8 else (0, 0)


        def tail_order():
            def begin(b):
                return [[("turn_x1", b, 0), ("turn_x1", b, 1)], [("qk", b, 0), ("qk", b, 1)],
                        [("split_ctx", b, c) for c in range(4)]] if b < NB else [[], [], []]

            turns, qks, split = begin(0)
            steps = turns + qks
            for b in range(NB + 1):
                turns, qks, split = begin(b + 1)
                if b < NB:
                    steps.append(("scores", b, 0))
                else:
                    steps.append(("turn_last", b - 1, TPB - 1))
                if b == 0:
                    steps += [("wo", 1, i) for i in range(TPB)]
                if b:
                    steps += [("post", b - 1, 0), ("post", b - 1, 1), ("pv", b - 1, 1), ("post", b - 1, 2), ("post", b - 1, 3)]
                if b < NB:
                    steps.append(("scores", b, 1))
                if b == 0:
                    steps += [("wo", 2, i) for i in range(TPB)]
                if b:
                    steps += [("turn_x2", b - 1, 0)] + [("ffn", b - 1, m) for m in range(FT)]
                if b < NB:
                    steps.append(("scores", b, 2))
                if b == 0:
                    steps += [("wo", 3, i) for i in range(TPB)]
                if b:
                    steps += [("turn_x2", b - 1, 1)]
                if b < NB:
                    steps += [("pv", b, 0)] + (turns if b == 0 else []) + [("scores", b, 3)]
                if b:
                    steps += [("down", b - 1, 0), ("down", b - 1, 1)]
                    for m in range(FT):
                        steps.append(("ffn", b - 1, FT + m))
                        steps += split[m - 1:m] if m else []
                    steps += turns + [("down", b - 1, 2)] + qks + [("down", b - 1, 3)]
                else:
                    steps += split[:1] + qks + split[1:]
            return steps

        TAIL = tail_order()
        MISC = {step: i for i, step in enumerate(x for x in TAIL if x[0] not in ("scores", "turn_last", "split_ctx"))}

        NORMS = [("wo", 0, i) for i in range(TPB)] + [x for x in TAIL if x[0] in ("wo", "post", "down")]

        def misc(*step):
            i = MISC[step]
            return 6 + i % 2, i // 2

        def ctx_cols(c):
            return 512 * c, min(512, S_CTX - 512 * c)

        COLS = (3, 0, 1, 2)
        TURNS = {3: (0,), 0: (1,), 1: (2, 3), 2: ()}

        def group(g):
            return (4 * g, 4, P) if g < 3 else (12, 1, KV[12])

        ORDER = phase_one_order()
        NPROJ = 6 * NB
        PROJ_V = 0
        TPS = TILES // SETS
        STEPS = L // C

        def y_of(n):
            return sl(y_buf, 0, P, (n % 2) * L, (1, L))

        def silu_dst(n):
            b, j = divmod(n, 6)
            proj, ct = divmod(j, 2)
            if proj == PROJ_V:
                return sl(vT, 0, P, ct * TOK + b * L, (1, L))
            return sl(qkT, 0, P, ((b % 2) * 2 + proj - 1) * CT * L + ct * L, (1, L))

        def win_dst(n):
            ct, g = divmod(n, 16)
            return sl(win, 0, WIN, ct * P * BLK + 4 * g, (BLK, P), (1, 4))

        def blk_dst(n):
            k, i = divmod(n, 8)
            if k == 1:
                return sl(oT, 0, P, i * 2 * P, (P, 2), (TOK, CT), (1, P))
            return sl((v_blk, None, o_blk)[k], 0, P, i * 512, (1, 512))

        def blk_src(n):
            if n // 8 == 1:
                return bank(n % 4, 0, P, 0, (256, 2), (P, CT), (1, P))
            return bank(n % 4, 0, P, 0, (1, 512))

        def fir_dst(n):
            return sl(fir, 0, P, 4 * n, (P, C), (C * P, NF), (1, 4))

        def fir_src(n):
            return bank(6 + n % 2, 0, P, (C - 1) * NF, (-NF, C), (1, NF), (C * NF, 4))

        def stats_dst(n, ct):
            return sl(statsT, DV * ct, 40, 4 * n, (1, 4), (C, BLK))

        def on_dst(n):
            return sl(onT, 0, P, 4 * n, (1, 4), (TOK, CT), (C, BLK))

        def on_src(n):
            return bank(n % 4, 0, P, 0, (P, 4), (DV, CT), (1, DV))

        def p_dst(buf, r, g):
            g0, count, rows = group(g)
            return sl(buf, 0, rows, g0 * 2 * P + (r % 2) * P, (2 * P, count), (1, P))

        def uw_kept(t):
            if t < TPS:
                return uw_act, t + 1
            return (uw_dve, (t - TPS) // 2 + 1) if t % 2 else (uw_act, TPS + (t - TPS) // 2 + 1)

        def w_kept(t):
            if t < TPS:
                return w_act, t + 1
            return (w_act, TPS + (t - TPS) // 2 + 1) if t % 2 else (w_dve, (t - TPS) // 2 + 1)

        def uw_dst(t):
            return sl(vk, 0, P, t * 512, (D, 2), (DV, H), (1, DV))

        def uw_src(t):
            return bank(t % 2, 0, P, 0, (DV, 2), (P, H), (1, DV))

        def w_dst(t):
            return sl(wq, 0, P, t * QC * 2 * C, (NCHUNK * 2 * C, CT), (2 * C, QC), (1, C))

        def w_src(t):
            return bank(2 + t % 2, 0, P, 0, (P, CT), (C, QC), (1, C))

        block = ctx.enter_context(nc.Block())

        @block.sync
        def _(sp):
            sp.dma_start(sl(xT, 0, P, 0, (TOK, CT), (1, L)),
                         dr(a["xT"], 0, (TOK, P), (P * TOK, CT), (1, L))).then_inc(s_x[0], 16)
            for i, w in enumerate((a["Wv"], a["Wk"], a["Wq"])):
                sp.dma_start(sl(w_in, 0, P, i * D, (3 * D, CT), (1, D)),
                             w.rearrange("(c p) n -> p c n", p=P)).then_inc(s_win, 16)
            sp.dma_start(sl(w_beta, 0, P, 0, (H, CT), (1, H)),
                         a["Wb"].rearrange("(c p) n -> p c n", p=P)).then_inc(s_win, 16)
            for i, w in enumerate((a["conv_v"], a["conv_k"], a["conv_q"])):
                sp.dma_start(sl(conv_w, 0, P, i * CONV_K, (3 * CONV_K, CT), (1, CONV_K)),
                             w.rearrange("(c p) k -> p c k", p=P)).then_inc(s_const, 16)
            sp.dma_start(ident, a["ident"]).then_inc(s_const, 16)
            sp.dma_start(mask_gram, a["mask_gram"]).then_inc(s_const, 16)
            sp.dma_start(mask_heads, a["mask_heads"]).then_inc(s_const, 16)
            sp.dma_start(eps_col, a["eps"]).then_inc(s_const, 16)
            for b in range(1, NB):
                sp.dma_start(sl(xT, 0, P, b * L, (TOK, CT), (1, L)),
                             dr(a["xT"], b * L, (TOK, P), (P * TOK, CT), (1, L))).then_inc(s_x[b], 16)
            for ct in range(CT):
                half = (DV * ct, DV)
                sp.dma_start(sl(gb2_row, *half, 0, (1, 10)), dr(a["gb2"], 10 * ct, (0, DV), (1, 10))).then_inc(s_par, 16)
                sp.dma_start(sl(tau_in, *half, 0, (1, 2)), dr(a["log_tau"], 2 * ct, (0, DV), (1, 2))).then_inc(s_par, 16)
                sp.dma_start(sl(eps_row, *half, 0, (1, 10)), dr(a["eps_logit"], 10 * ct, (0, DV), (1, 10))
                             ).then_inc(s_par, 16)
                sp.dma_start(sl(nw_col, *half, 0, (1, 1)), a["norm_w"].rearrange("(a b) -> a b", b=1)).then_inc(s_par, 16)

            def lower_to_rows(s):
                sp.wait_ge(gram_masked, QC * TPS * (s + 1))
                for q in range(QC):
                    for h in range(2):
                        sp.dma_start(dr(a["scr_a"], s * P * C * C + (h * QC + q) * C * C,
                                        (C, C), (2 * QC * C * C, CT * TPS), (1, C)),
                                     sl(al, C * q, C, s * TPS * 256 + h * C, (P, CT * TPS), (1, C))).then_inc(a_out, 16)

            def rows_in(s):
                sp.wait_ge(a_out, 16 * 2 * QC * (s + 1))
                if s:
                    sp.wait_ge(solved, s)
                sp.dma_start(a_row, dr(a["scr_a"], s * P * C * C, (C * C, P), (1, C * C))).then_inc(a_in, 16)

            def rows_out(s):
                sp.wait_ge(solved, s + 1)
                sp.dma_start(dr(a["scr_u"], s * P * C * C, (C * C, P), (1, C * C)), u_row).then_inc(u_out, 16)

            def inverses_in(s):
                sp.wait_ge(u_out, 16 * (s + 1))
                sp.wait_ge(zero_words, s + 1)
                for q in range(QC):
                    sp.dma_start(sl(ubd, C * q, C, s * TPS * H * P + C * q, (P, H * TPS), (1, C)),
                                 dr(a["scr_u"], s * P * C * C + q * C * C, (C, C), (QC * C * C, 4 * TPS), (1, C)),
                                 ).then_inc(u_in[s], 16)

            lower_to_rows(0)
            rows_in(0)
            lower_to_rows(1)
            rows_out(0)
            rows_in(1)
            inverses_in(0)
            rows_out(1)
            inverses_in(1)
            for s in range(SETS):
                sp.wait_ge(u_in[s], 16 * QC)
            sp.dma_start(sl(w2_sb, 0, P, 0, (20, 4), (1, 20)), a["gW2"].rearrange("(m p) n -> p m n", p=P)).then_inc(gate_in, 16)
            sp.dma_start(b1_col, a["gb1"]).then_inc(gate_in, 16)
            sp.dma_start(expand, a["expand"]).then_inc(gate_in, 16)

            def load_taps(n):
                if n >= 3:
                    sp.wait_ge(fir_mm, n - 2)
                for ct in range(CT):
                    sp.dma_start(sl(taps_ring, 0, WIN, (n % 3) * 768 + ct * 384, (96, 4), (1, 96)),
                                 dr(a["taps"], (ct * P + 4 * n) * NF * (WIN + C - 1),
                                    (NF, WIN), (NF * (WIN + C - 1), 4), (1, C * NF))).then_inc(taps_in[n % 3], 16)

            for n in range(3):
                load_taps(n)
            for n in range(3, 32):
                load_taps(n)
            sp.wait_ge(win_mm, 1)
            sp.dma_start(sl(xT2, 0, P, 0, (TOK, CT), (1, TOK)), a["xT"].rearrange("(c p) n -> p c n", p=P)).then_inc(xT2_in, 16)
            sp.wait_ge(fir_mm, 32)
            sp.dma_start(sl(w1_x, 0, P, 0, (HF, CT), (1, HF)), a["gW1"][0:D, :].rearrange("(c p) n -> p c n", p=P)).then_inc(w1x_in, 16)
            sp.dma_start(sl(w_o_in, 0, P, 0, (D, CT), (1, D)), a["Wo"].rearrange("(c p) n -> p c n", p=P)).then_inc(wo_in, 16)
            sp.wait_ge(w1s_mm, 1)
            for i, (name, w) in enumerate((("wgT", w_g), ("wuT", w_u), ("wdT", w_d))):
                if i:
                    sp.wait_ge(int_done, i)
                n = a[name].shape[1]
                sp.dma_start(sl(stage_i, 0, P, 0, (n, 1536 // n), (1, n)).bitcast(I32),
                             a[name].rearrange("(c p) n -> p c n", p=P)).then_inc(int_in, 16)
            sp.wait_ge(mix_dve, 6 * GATED)
            for w, name in ((x_q, "xWq"), (x_k, "xWk"), (x_v, "xWv"), (x_oT, "xWoT")):
                sp.dma_start(sl(w, 0, P, 0, (D, CT), (1, D)), a[name].rearrange("(c p) n -> p c n", p=P)).then_inc(wts_in, 16)
            sp.dma_start(bq_col, a["xbq"]).then_inc(wts_in, 16)
            sp.dma_start(bv_col, a["xbv"]).then_inc(wts_in, 16)
            sp.wait_ge(mix_sum, GATED)
            sp.dma_start(bo_row, dr(a["xbo"], 0, (0, P), (1, D))).then_inc(wts_in, 16)
            for t in range(0, TILES, TPB):
                sp.dma_start(sl(x1, 0, P, t * D, (D, TPB), (1, D)),
                             dr(a["x"], t * P * D, (D, P), (P * D, TPB), (1, D))).then_inc(x_in[t // TPB], 16)

            def load_ctx_t(b):
                if b == 0:
                    sp.wait_ge(lg_mm, GATED)
                if b >= 2:
                    sp.wait_ge(scored, 4 * TPB * (b - 1))
                sp.dma_start(loaded(sl(ctx_t, 0, P, (b % 2) * CT * S_PAD, (S_PAD, CT), (1, S_CTX))),
                             dr(a["ctxT"], b * D * S_CTX, (S_CTX, P), (P * S_CTX, CT), (1, S_CTX))
                             ).then_inc(ctx_in[b % 2], 16)

            def load_ctx_n(b):
                n = S_CTX // P
                if b:
                    bk, i = misc("pv", b - 1, 1)
                    sp.wait_ge(full[bk - 6], i + 1)
                sp.dma_start(loaded(sl(ctx_n, 0, P, 0, (D, n), (1, D))),
                             dr(a["ctx"], b * S_CTX * D, (D, P), (P * D, n), (1, D))).then_inc(ctxn_in, 16)
                sp.dma_start(loaded(sl(ctx_n, 0, S_CTX - n * P, n * D, (1, D))),
                             dr(a["ctx"], (b * S_CTX + n * P) * D, (D, S_CTX - n * P), (1, D))).then_inc(ctxn_in, 16)

            def store(b):
                sp.wait_ge(y_ready, TPB * (b + 1))
                sp.dma_start(dr(out, b * L * D, (D, P), (P * D, TPB), (1, D)),
                             sl(y_out, 0, P, 0, (D, TPB), (1, D))).then_inc(stored, 16)

            load_ctx_t(0)
            load_ctx_t(1)
            load_ctx_n(0)
            for b in range(NB):
                if b + 2 < NB:
                    load_ctx_t(b + 2)
                if b:
                    store(b - 1)
                if b + 1 < NB:
                    load_ctx_n(b + 1)
            store(NB - 1)
            sp.wait_ge(stored, 16 * NB)

        @block.gpsimd
        def _(pool):
            pool.memset(sl(vT, 0, P, -HALO, (1, HALO)), 0.0).then_inc(zeroed, 1)
            pool.memset(bd, 0.0).then_inc(zeroed, 1)

            def normalise(b):
                pool.wait_ge(rn_done, b + 1)
                pool.wait_ge(zeroed, 2)
                pool.wait_ge(u_init, 2)
                if b:
                    pool.wait_ge(back_turned, TPB * b)
                    pool.wait_ge(wq_q, 2 * TPB * b)
                pool.tensor_tensor(sl(qn, 0, P, 0, (D, TPB), (DV, H), (1, DV)),
                                   sl(raw, 0, P, D, (2 * D, TPB), (DV, H), (1, DV)),
                                   sl(rn, 0, P, H, (8, TPB), (1, H), (0, DV)), ALU.mult).then_inc(qn_done, 1)

            def turn_back(t):
                pool.wait_ge(back_act, t + 1)
                for h in range(2):
                    pool.wait_ge(qn_done, (t // TPB) + 1)
                    if t or h:
                        pool.wait_ge(wq_q, 2 * t + h)
                    pool.tensor_copy(
                        sl(wq, DV * h, DV, t * QC * 2 * C + C, (NCHUNK * 2 * C, CT), (2 * C, QC), (1, C)),
                        sl(bd, DV * h, DV, (t % 2) * CT * 512 + 256 + h * P, (512, CT), (C, QC), (1, C))
                        ).then_inc(wq_q, 1)

            def start_solver():
                pool.memset(u_row, 0.0).then_inc(u_init, 1)
                pool.wait_ge(u_init, 1)
                pool.memset(sl(u_row, 0, P, 0, (C + 1, C)), 1.0).then_inc(u_init, 1)

            start_solver()
            for kind, n in ORDER:
                if kind == "normalise":
                    normalise(n)
                elif kind == "turn_back":
                    turn_back(n)
            pool.wait_ge(gram_done, TILES)
            pool.wait_ge(silu_done, NPROJ)
            pool.wait_ge(wq_q, 2 * TILES)
            for s in range(SETS):
                pool.memset(ubd[:, s * TPS * H * P:(s + 1) * TPS * H * P], 0.0).then_inc(zero_words, 1)
            pool.memset(state, 0.0).then_inc(zero_words, 1)
            pool.wait_ge(u_out, 16)
            pool.memset(u_row, 0.0).then_inc(u_init, 1)
            pool.wait_ge(u_init, 3)
            pool.memset(sl(u_row, 0, P, 0, (C + 1, C)), 1.0).then_inc(u_init, 1)

            pool.wait_ge(w_turned, TILES)
            pool.wait_ge(solved, SETS)
            pool.wait_ge(u_out, 16 * SETS)

            def load_w1(p):
                pool.dma_start(sl(w1_raw, 0, P, (p % 2) * 8 * HF, (1, 8 * HF)),
                               dr(a["gW1"], (D + p * 1024) * HF, (8 * HF, P), (1, 8 * HF))).then_inc(w1_in[p % 2], 16)

            load_w1(0)
            load_w1(1)
            adds = 0
            for p in range(NPATH):
                pool.wait_ge(w1_in[p % 2], 16 * (p // 2 + 1))
                r0 = (p % 2) * 8 * HF
                for n in (4, 2, 1):
                    if adds:
                        pool.wait_ge(w1_add, adds)
                    x = sl(w1_raw, 0, P, r0, (1, n * HF))
                    y = x if n > 1 else sl(w1_part, 0, P, p * HF, (1, HF))
                    pool.tensor_tensor(y, x, sl(w1_raw, 0, P, r0 + n * HF, (1, n * HF)), ALU.add).then_inc(w1_add, 1)
                    adds += 1
                if p + 2 < NPATH:
                    pool.wait_ge(w1_add, adds)
                    load_w1(p + 2)

            pool.wait_ge(w1_add, adds)
            pool.wait_ge(win_act, 16)
            pool.wait_ge(win_dve, 16)
            pool.memset(sl(win, 0, HALO, 0, (BLK, CT * P), (BLK // NB, NB)), 0.0).then_inc(win_fixed, 1)
            pool.wait_ge(win_fixed, 1)
            pool.memset(sl(win, 0, C, 1, (BLK, CT * P), (BLK // NB, NB)), 0.0).then_inc(win_fixed, 1)
            pool.wait_ge(win_fixed, 2)
            pool.wait_ge(fir_mm, 32)
            pool.memset(statsT, 0.0).then_inc(statsT_zero, 1)

            pool.wait_ge(statsT_zero, 1)
            for i, w in enumerate((w_g, w_u, w_d)):
                pool.wait_ge(int_in, 16 * (i + 1))
                if i:
                    pool.wait_ge(int_done, i)
                pool.tensor_scalar(w, stage_i.bitcast(I32), 1.0 / 127.0, None, ALU.mult).then_inc(int_done, 1)
            pool.wait_ge(int_done, 3)

            for g in range(GATED):
                pool.wait_ge(pr_ready, g + 1)
                xs = [sl(PATHS[p], 0, P, g * CG * P, (DV, 2 * CG), (1, DV)) for p in range(2)]
                for p in range(2):
                    if g or p:
                        pool.wait_ge(mix_pool, 3 * g + p)
                    pool.tensor_tensor(xs[p], xs[p], sl(pr, 0, P, g * 10 * CG + p, (NPATH, 2 * CG), (0, DV)), ALU.mult
                                       ).then_inc(mix_pool, 1)
                pool.wait_ge(mix_pool, 3 * g + 2)
                pool.tensor_tensor(xs[0], xs[0], xs[1], ALU.add).then_inc(mix_pool, 1)
            pool.wait_ge(mix_pool, 3 * GATED)

            pool.wait_ge(wo_in, 16)
            pool.wait_ge(s_par, 16 * 8)
            pool.wait_ge(on_mm, 2)
            pool.tensor_scalar(w_o, w_o_in, nw_col, None, ALU.mult).then_inc(wo_scaled, 1)
            pool.wait_ge(wo_scaled, 1)

            parts = [(wg_h, w_g), (wu_h, w_u)] + [(wd_h[m], w_d[:, D * m:D * (m + 1)]) for m in range(FT)]
            pool.wait_ge(on_mm, 8)
            pool.wait_ge(mix_sum, GATED)
            for buf, n in ((ctxt_h, CT), (ctx_t, 2 * CT)):
                pool.tensor_scalar(r32(sl(buf, 0, P, S_CTX, (S_PAD, n))), ident[:, 0:n], 0.0, None, ALU.mult
                                   ).then_inc(zero_words, 1)
            for i, (high, w) in enumerate(parts):
                if i:
                    pool.wait_ge(w_split, 2 * i)
                pool.tensor_copy(r32(high), w).then_inc(w_split, 1)
                pool.wait_ge(w_split, 2 * i + 1)
                pool.tensor_tensor(r32(w), w, high_of(high), ALU.subtract).then_inc(w_split, 1)
            pool.wait_ge(w_split, 2 * len(parts))

            pool.wait_ge(bvo_ready, 1)
            done = 0
            for b in range(NB):
                pool.wait_ge(ctxn_in, 32 * (b + 1))
                for g in range(5):
                    rows, off, n = (P, 3 * g * D, 3 * D) if g < 4 else (KV[12], 12 * D, D)
                    raw_n, high = sl(ctx_n, 0, rows, off, (1, n)), sl(ctxn_h, 0, rows, off, (1, n))
                    if done:
                        pool.wait_ge(ctxn_ready, done)
                    pool.tensor_copy(r32(high), loaded(raw_n)).then_inc(ctxn_ready, 1)
                    pool.wait_ge(ctxn_ready, done + 1)
                    pool.tensor_tensor(r32(raw_n), loaded(raw_n), high_of(high), ALU.subtract).then_inc(ctxn_ready, 1)
                    done += 2
                pool.wait_ge(ctxn_ready, done)
                for i in range(2):
                    bk, j = misc("turn_x1", b, i)
                    pool.wait_ge(full[bk - 6], j + 1)
                x = sl(x1, 0, P, b * TPB * D, (D, TPB), (1, D))
                pool.tensor_tensor(x, x, sl(b_vo, 0, P, 0, (0, TPB), (1, D)), ALU.add).then_inc(x1_bias, 1)
                pool.wait_ge(x1_bias, b + 1)

        @block.scalar
        def _(act):
            def silu(n):
                act.wait_ge(conv_done, n + 1)
                b, j = divmod(n, 6)
                if j >= 2 and b >= 2:
                    act.wait_ge(kq_turned, TPB * (b - 1))
                if n == 0:
                    act.wait_ge(zeroed, 1)
                act.activation(silu_dst(n), y_of(n), ACT.Silu).then_inc(silu_done, 1)

            def project(n):
                if n < NPROJ:
                    b, j = divmod(n, 6)
                    proj, ct = divmod(j, 2)
                    act.wait_ge(projected, n + 1)
                    if n >= 2:
                        act.wait_ge(silu_done, n - 1)
                    act.activation(y_of(n), bank(n % 2, 0, P, 0, (1, L)), ACT.Copy,
                                   scale=sl(conv_w, 0, P, ct * 12 + proj * CONV_K + CONV_K - 1, (1, 1))
                                   ).then_inc(tap_first, 1)
                if n:
                    silu(n - 1)

            def turn(t):
                b, r = divmod(t, TPB)
                if t == 0:
                    act.wait_ge(beta_mm, 1)
                    act.activation(beta, bank(7, 0, P, 0, (1, TILES * H)), ACT.Sigmoid).then_inc(beta_ready, 1)
                act.wait_ge(kq_turned, t + 1)
                if b and r == 0:
                    act.wait_ge(kn_done, b)
                    act.wait_ge(qn_done, b)
                act.activation(sl(raw, 0, P, r * 2 * D, (1, 2 * D)), bank(2, 0, P, 0, (1, 512)), ACT.Copy)
                if t:
                    act.wait_ge(ss_done, t)
                act.activation(sq, bank(2, 0, P, 0, (1, 512)), ACT.Square).then_inc(raw_done, 1)

            def normalise(b):
                act.wait_ge(ss_done, TPB * (b + 1))
                if b:
                    act.wait_ge(rn_done, b)
                act.activation(nrm, ss, ACT.Sqrt, bias=sl(eps_col, 0, P, 0, (1, 1))).then_inc(sqrt_done, 1)

            def turn_back(t):
                act.wait_ge(back_turned, t + 1)
                if t >= 2:
                    act.wait_ge(gram_done, t - 1)
                    act.wait_ge(wq_q, 2 * (t - 1))
                if t == 0:
                    act.wait_ge(zeroed, 2)
                act.activation(sl(knT, 0, P, (t % 2) * CT * P, (1, CT * P)), bank(4, 0, P, 0, (1, CT * P)), ACT.Copy)
                for h in range(2):
                    last = act.activation(sl(bd, DV * h, DV, (t % 2) * CT * 512 + h * P, (256, 2 * CT), (1, P)),
                                          bank(5, DV * h, DV, 0, (P, 2 * CT), (1, P)), ACT.Copy)
                last.then_inc(back_act, 1)

            act.wait_ge(s_const, 16 * 7)
            for kind, n in ORDER:
                if kind == "project":
                    project(n)
                elif kind == "turn":
                    turn(n)
                elif kind == "normalise":
                    normalise(n)
                elif kind == "turn_back":
                    turn_back(n)

            for t in range(TILES + 1):
                if t < TILES and uw_kept(t)[0] is uw_act:
                    act.wait_ge(uw_mm, t + 1)
                    act.activation(uw_dst(t), uw_src(t), ACT.Copy).then_inc(uw_act, 1)
                if t and w_kept(t - 1)[0] is w_act:
                    act.wait_ge(w_turned, t)
                    act.activation(w_dst(t - 1), w_src(t - 1), ACT.Copy).then_inc(w_act, 1)
            for n in range(STEPS):
                g, q = divmod(n, QC)
                for s in range(SETS):
                    act.wait_ge(o_mm[s], n + 1)
                    act.activation(sl(o_tok, C * q, C, (s * TPS + g) * D, (TPB * D, 2), (1, D)),
                                   bank(2 * s + n % 2, C, C, 0, (D, 2), (1, D)), ACT.Copy).then_inc(o_kept[s], 1)

            for n in range(0, 32, 2):
                act.wait_ge(win_mm, n + 1)
                act.activation(win_dst(n), bank(n % 4, 0, WIN, 0, (1, P), (P, 4)), ACT.Copy).then_inc(win_act, 1)
            for n in range(0, 24, 2):
                act.wait_ge(blk_mm, n + 1)
                act.activation(blk_dst(n), blk_src(n), ACT.Copy).then_inc(blk_act, 1)
            act.wait_ge(blk_act, 12)
            act.wait_ge(blk_dve, 12)
            for j, (p, h) in enumerate(STATS):
                if j >= 2:
                    act.wait_ge(stat_sq, j - 1)
                for n in range(*fir_between(j)):
                    act.wait_ge(fir_mm, n + 1)
                    act.activation(fir_dst(n), fir_src(n), ACT.Copy).then_inc(fir_act, 1)
                if p < NF:
                    act.wait_ge(fir_act, 16 * (h + 1))
                act.activation(sl(sqt, 0, P, (j % 2) * C * DV, (DV, C), (1, DV)), sl(PATHS[p], 0, P, h * DV, (P, C), (1, DV)),
                               ACT.Square).then_inc(sq_ready, 1)
            act.wait_ge(stat_sq, 2 * NPATH)
            act.activation(sl(st, 0, P, 3, (4, 320)), sl(st, 0, P, 1, (4, 320)), ACT.Sqrt).then_inc(st_norm, 1)
            act.wait_ge(par_dve, 2)
            act.activation(tau_inv, tau_t[:, 0:2], ACT.Exp, scale=-1.0).then_inc(par_act, 1)
            act.wait_ge(par_act, 1)
            act.activation(tau_t[:, 2:4], tau_inv, ACT.Ln, bias=1.0).then_inc(par_act, 1)
            act.activation(eps_row, eps_row, ACT.Sigmoid).then_inc(par_act, 1)
            act.wait_ge(statsT_zero, 1)
            for n in range(0, 8, 2):
                act.wait_ge(st_mm, n + 1)
                for ct in range(CT):
                    last = act.activation(stats_dst(n, ct), bank(4 + n % 4, 0, 40, ct * DV, (P, 4), (1, DV)), ACT.Copy)
                last.then_inc(st_act, 1)
            def hidden(g, m):
                act.wait_ge(hid_mm, 4 * g + m + 1)
                act.activation(sl(hT, 0, P, m * TOK + g * GT, (1, GT)), bank(m, 0, P, 0, (1, GT)), ACT.Gelu,
                               bias=b1_col[:, m:m + 1]).then_inc(hid_act, 1)

            def keep_lT(g):
                act.wait_ge(lT_mm, g + 1)
                act.activation(sl(lT, 0, 20, g * GT, (1, GT)), bank(6 + g % 2, 0, 20, 0, (1, GT)), ACT.Copy
                               ).then_inc(lT_kept, 1)

            def exponentials(g):
                act.wait_ge(gate_step, 3 * (g + 1))
                act.activation(pr[:, g * 10 * CG:(g + 1) * 10 * CG], lg[:, g * 10 * CG:(g + 1) * 10 * CG], ACT.Exp
                               ).then_inc(exp_done, 1)

            def squares(g):
                act.wait_ge(mix_dve, 6 * (g + 1))
                act.activation(sl(sqt, 0, P, g * CG * P, (1, CG * P)), sl(mix, 0, P, g * CG * P, (1, CG * P)), ACT.Square
                               ).then_inc(mix_sq, 1)

            def root(g):
                act.wait_ge(mix_sum, g + 1)
                act.activation(rs[:, 2 * CG * g:2 * CG * (g + 1)], r64[:, 2 * CG * g:2 * CG * (g + 1)], ACT.Sqrt,
                               bias=eps_col[:, 1:2], scale=1.0 / DV).then_inc(mix_sq, 1)

            for g in range(GATED + 1):
                if g < GATED:
                    hidden(g, 0)
                if g:
                    keep_lT(g - 1)
                if g >= 2:
                    squares(g - 2)
                    root(g - 2)
                if g < GATED:
                    hidden(g, 1)
                if g:
                    exponentials(g - 1)
                if g < GATED:
                    hidden(g, 2)
                    hidden(g, 3)
            squares(GATED - 1)
            root(GATED - 1)
            act.wait_ge(mix_pool, 3 * GATED)
            for n in range(0, 8, 2):
                act.wait_ge(on_mm, n + 1)
                act.activation(on_dst(n), on_src(n), ACT.Copy).then_inc(on_act, 1)

            def root1(b):
                act.wait_ge(agg, NORMS.index(("wo", b, TPB - 1)) + 1)
                act.activation(rstd[:, TPB * b:TPB * b + TPB], sl(mv, 0, P, 2 * TPB * b + 1, (2, TPB)), ACT.Sqrt,
                               bias=eps_col[:, 1:2]).then_inc(sqrt1, 1)

            def high_ctx(b, i):
                act.wait_ge(ctx_in[b % 2], 16 * (b // 2 + 1))
                if b:
                    act.wait_ge(scored, 4 * TPB * b)
                off, w = ctx_cols(COLS[i])
                act.activation(r32(sl(ctxt_h, 0, P, off, (S_PAD, CT), (1, w))),
                               loaded(sl(ctx_t, 0, P, (b % 2) * CT * S_PAD + off, (S_PAD, CT), (1, w))), ACT.Copy
                               ).then_inc(ctxt_high, 1)

            for i in range(4):
                high_ctx(0, i)
            root1(0)
            for i, w in enumerate((w_qk, w_vo)):
                act.wait_ge(fold_mm, i + 1)
                act.activation(w, bank(6 + i, 0, P, 0, (1, 512)), ACT.Copy).then_inc(fold_done, 1)
            act.wait_ge(fold_mm, 3)
            act.activation(bqk, bank(4, 0, P, 0, (1, 2)), ACT.Copy).then_inc(fold_done, 1)

            def filled(*step):
                bk, i = misc(*step)
                act.wait_ge(full[bk - 6], i + 1)
                return bk, free[bk - 6]

            def high_p(n):
                for g in range(4):
                    act.wait_ge(p_mm, 4 * n + g + 1)
                    g0, count, rows = group(g)
                    act.activation(r32(p_dst(pT_h, n, g)), bank(4 + g % 2, 0, rows, 0, (P, count), (1, P)),
                                   ACT.Copy).then_inc(p_high, 1)

            def high_h(k):
                act.wait_ge(h_product, k + 1)
                m = k % FT
                act.activation(r32(sl(hF_h, 0, P, m * 256, (1, 256))), sl(hF_l, 0, P, m * 256, (1, 256)),
                               ACT.Copy).then_inc(h_high, 1)

            for kind, b, i in TAIL:
                n = TPB * b + i
                if kind == "turn_x1":
                    bk, done = filled(kind, b, i)
                    act.activation(sl(x1T, 0, P, i * 256, (P, 2), (L, CT), (1, P)),
                                   bank(bk, 0, P, 0, (256, 2), (P, CT), (1, P)), ACT.Copy).then_inc(done, 1)
                elif kind == "qk":
                    bk, done = filled(kind, b, i)
                    act.activation(r32(sl(qk_h, 0, P, i * L, (1, L))), bank(bk, 0, P, 0, (1, L)), ACT.Identity,
                                   bias=bqk[:, i:i + 1]).then_inc(high_kept, 1)
                elif kind == "split_ctx":
                    high_ctx(b, i)
                elif kind == "scores":
                    if n:
                        high_p(n - 1)
                    act.wait_ge(neg_ready, n + 1)
                    act.activation(sl(p_sb, 0, P, (n % 2) * 1664, (1, S_CTX)), bank(0, 0, P, 0, (1, S_CTX)), ACT.Exp,
                                   bias=sl(sm_neg, 0, P, n % 8, (1, 1)), scale=1.0 / 16.0,
                                   accum_out=sl(sm_sum, 0, P, n % 8, (1, 1))).then_inc(exped, 1)
                elif kind == "turn_last":
                    high_p(n)
                elif kind == "pv":
                    bk, done = filled(kind, b, i)
                    act.activation(sl(pcT, 0, P, i * 256, (L, CT), (1, 256)), bank(bk, 0, P, 0, (256, CT), (1, 256)),
                                   ACT.Copy).then_inc(done, 1)
                elif kind == "ffn":
                    bk, done = filled(kind, b, i)
                    k = 2 * FT * b + i
                    if k >= 2:
                        act.wait_ge(h_product, k - 1)
                    act.activation(sl(sg, 0, P, (k % 2) * 256, (1, 256)), bank(bk, 0, P, 0, (1, 256)), ACT.Silu
                                   ).then_inc(silu_g, 1)
                    if i % FT:
                        high_h(k - 1)
                    if i % FT == FT - 1:
                        high_h(k)
                if kind == "wo" and i == TPB - 1:
                    root1(b)
                if kind in ("post", "down") and i == TPB - 1:
                    act.wait_ge(agg, NORMS.index((kind, b, i)) + 1)
                    act.activation(rstd2, sl(mv2, 0, P, 1, (2, TPB)), ACT.Sqrt, bias=eps_col[:, 1:2]).then_inc(sqrt2, 1)

        @block.tensor
        def _(pe):
            def betas():
                for b in range(NB):
                    pe.wait_ge(s_x[b], 16)
                for t in range(TILES):
                    for ct in range(CT):
                        last = pe.matmul(bank(7, 0, P, t * H, (1, H)), sl(xT, 0, P, ct * TOK + t * P, (1, P)),
                                         sl(w_beta, 0, P, ct * H, (1, H)), start=(ct == 0), stop=(ct == CT - 1))
                last.then_inc(beta_mm, 1)

            def project(n):
                if n >= NPROJ:
                    return
                b, j = divmod(n, 6)
                proj, ct = divmod(j, 2)
                if j == 0:
                    pe.wait_ge(s_x[b], 16)
                if n >= 2:
                    pe.wait_ge(conv_done, n - 1)
                for k in range(CT):
                    last = pe.matmul(bank(n % 2, 0, P, 0, (1, L)),
                                     sl(w_in, 0, P, k * 3 * D + proj * D + ct * P, (1, P)),
                                     sl(xT, 0, P, k * TOK + b * L, (1, L)), start=(k == 0), stop=(k == CT - 1))
                last.then_inc(projected, 1)

            def turn(t):
                b, r = divmod(t, TPB)
                if t == 0:
                    betas()
                    pe.wait_ge(s_const, 16 * 7)
                pe.wait_ge(silu_done, 6 * (b + 1))
                if t:
                    pe.wait_ge(raw_done, t)
                for kq in range(2):
                    for ct in range(CT):
                        last = pe.transpose(bank(2, 0, P, kq * D + ct * P, (1, P)),
                                            sl(qkT, 0, P, ((b % 2) * 2 + kq) * CT * L + ct * L + r * P, (1, P)), ident)
                last.then_inc(kq_turned, 1)
                if t:
                    pe.wait_ge(vb_done, t)
                for ct in range(CT):
                    last = pe.transpose(bank(3, 0, P, ct * P, (1, P)),
                                        sl(vT, 0, P, ct * TOK + t * P, (1, P)), ident)
                last.then_inc(v_turned, 1)

            def turn_back(t):
                b, r = divmod(t, TPB)
                pe.wait_ge(kb_done, b + 1)
                pe.wait_ge(qn_done, b + 1)
                if t:
                    pe.wait_ge(back_act, t)
                for ct in range(CT):
                    pe.transpose(bank(4, 0, P, ct * P, (1, P)), sl(kn, 0, P, t * D + ct * P, (1, P)), ident)
                    pe.transpose(bank(5, 0, P, ct * 256, (1, P)),
                                 sl(vk, 0, P, t * 512 + D + ct * P, (1, P)), ident)
                    last = pe.transpose(bank(5, 0, P, ct * 256 + P, (1, P)),
                                        sl(qn, 0, P, r * D + ct * P, (1, P)), ident)
                last.then_inc(back_turned, 1)

            def gram(t):
                pe.wait_ge(back_act, t + 1)
                if t:
                    pe.wait_ge(gram_masked, QC * t)
                for ct in range(CT):
                    last = pe.matmul(bank(6 + ct, 0, P, 0, (1, 512)), sl(knT, 0, P, ((t % 2) * CT + ct) * P, (1, P)),
                                     sl(bd, 0, P, ((t % 2) * CT + ct) * 512, (1, 512)), start=True, stop=True)
                last.then_inc(gram_done, 1)

            pe.wait_ge(s_win, 16 * 4)
            for kind, n in ORDER:
                if kind == "project":
                    project(n)
                elif kind == "turn":
                    turn(n)
                elif kind == "turn_back":
                    if n == 0:
                        pe.wait_ge(beta_ready, 1)
                    turn_back(n)
                elif kind == "gram":
                    gram(n)

            def make_uw(t):
                s = t // TPS
                pe.wait_ge(u_in[s], 16 * QC)
                if t == 0:
                    pe.wait_ge(conv_done, NPROJ)
                    pe.wait_ge(raw_done, TILES)
                    pe.wait_ge(vb_done, TILES)
                if t >= 2:
                    pe.wait_ge(*uw_kept(t - 2))
                for h in range(H):
                    last = pe.matmul(bank(t % 2, 0, P, h * P, (1, P)), sl(ubd, 0, P, (t * H + h) * P, (1, P)),
                                     sl(vk, 0, P, t * 512 + h * DV, (D, 2), (1, DV)), start=True, stop=True)
                last.then_inc(uw_mm, 1)

            def turn_w(t):
                pe.wait_ge(*uw_kept(t))
                if t >= 2:
                    pe.wait_ge(*w_kept(t - 2))
                for ct in range(CT):
                    last = pe.transpose(bank(2 + t % 2, 0, P, ct * P, (1, P)),
                                        sl(vk, 0, P, t * 512 + D + ct * P, (1, P)), ident)
                last.then_inc(w_turned, 1)

            for t in range(TILES + 1):
                if t < TILES:
                    make_uw(t)
                if t:
                    turn_w(t - 1)

            def scan_in(n, s):
                g, q = divmod(n, QC)
                if n == 0:
                    for t in (TILES - 2, TILES - 1):
                        pe.wait_ge(*uw_kept(t))
                        pe.wait_ge(*w_kept(t))
                    pe.wait_ge(wq_q, 2 * TILES)
                    pe.wait_ge(zero_words, SETS + 1)
                    pe.wait_ge(gram_masked, QC * TILES)
                else:
                    pe.wait_ge(state_ready[s], n)
                if n >= 2:
                    pe.wait_ge(o_kept[s], n - 1)
                for i in range(4):
                    b, ct = divmod(i, CT)
                    chunk = (s * TPS + b * TPB + g) * QC + q
                    last = pe.matmul(bank(2 * s + n % 2, 0, 2 * C, i * P, (1, P)),
                                     sl(wq, 0, P, (ct * NCHUNK + chunk) * 2 * C, (1, 2 * C)),
                                     sl(state, 0, P, (s * 4 + i) * P, (1, P)), start=(i == 0), stop=(i == 3),
                                     skip_group_check=True)
                last.then_inc(wq_mm[s], 1)

            def scan_out(n, s):
                g, q = divmod(n, QC)
                pe.wait_ge(u_ready[s], n + 1)
                for i in range(4):
                    b, ct = divmod(i, CT)
                    t = s * TPS + b * TPB + g
                    for h in range(2):
                        last = pe.matmul(bank(2 * s + n % 2, C, C, i * P + h * DV, (1, DV)),
                                         sl(al, C * q, C, ((t * CT + ct) * 4 + 2 + h) * C, (1, C)),
                                         sl(u_new, C * q, C, (s * 2 + n % 2) * 512 + i * P + h * DV, (1, DV)),
                                         start=False, stop=True, skip_group_check=True)
                last.then_inc(o_mm[s], 1)
                if n == STEPS - 1:
                    return
                for i in range(4):
                    b, ct = divmod(i, CT)
                    t = s * TPS + b * TPB + g
                    last = pe.matmul(bank(4 + s, 0, P, i * P, (1, P)), sl(kn, C * q, C, t * D + ct * P, (1, P)),
                                     sl(u_new, C * q, C, (s * 2 + n % 2) * 512 + i * P, (1, P)),
                                     start=(n == 0 and i == 0), stop=True, skip_group_check=True)
                last.then_inc(s_mm[s], 1)

            for n in range(STEPS):
                for s in range(SETS):
                    scan_in(n, s)
                for s in range(SETS):
                    scan_out(n, s)

            def ring(n, n_before, by_act, by_dve):
                if n >= 4:
                    pe.wait_ge((by_act, by_dve)[n % 2], (n - 4) // 2 + 1)

            for s in range(SETS):
                pe.wait_ge(o_kept[s], STEPS)
            for n in range(32):
                ct, g = divmod(n, 16)
                ring(n, 0, win_act, win_dve)
                for w in range(4):
                    last = pe.transpose(bank(n % 4, 0, WIN, w * P, (1, P)),
                                        sl(vT, 0, P, ct * TOK + (4 * g + w) * C - HALO, (1, WIN)), ident)
                last.then_inc(win_mm, 1)
            for n in range(24):
                k, i = divmod(n, 8)
                if n < 4:
                    pe.wait_ge((win_act, win_dve)[n % 2], 16)
                ring(n, 0, blk_act, blk_dve)
                if k == 2:
                    pe.wait_ge(blk_act, 8)
                    pe.wait_ge(blk_dve, 8)
                for w in range(4):
                    if k == 1:
                        src = sl(o_tok, 0, P, i * 512 + w * P, (1, P))
                    else:
                        src = sl((vT, None, oT)[k], 0, P, 4 * i + w, (C, P))
                    last = pe.transpose(bank(n % 4, 0, P, w * P, (1, P)), src, ident)
                last.then_inc(blk_mm, 1)

            pe.wait_ge(win_fixed, 2)
            for n in range(32):
                pe.wait_ge(taps_in[n % 3], 32 * (n // 3 + 1))
                if n >= 2:
                    pe.wait_ge(fir_act, n - 1)
                for c in range(4):
                    for ct in range(CT):
                        last = pe.matmul(bank(6 + n % 2, DV * ct, DV, c * 96, (1, 96)),
                                         sl(win, 0, WIN, (ct * P + 4 * n + c) * BLK, (1, BLK)),
                                         sl(taps_ring, 0, WIN, (n % 3) * 768 + ct * 384 + c * 96, (1, 96)),
                                         start=True, stop=True, skip_group_check=True)
                last.then_inc(fir_mm, 1)

            pe.wait_ge(w1_add, 3 * NPATH)
            pe.wait_ge(gate_in, 48)
            for p in range(NPATH):
                last = pe.matmul(bank(4, 0, P, 0, (1, HF)), sl(expand, 0, P, p * P, (1, P)),
                                 sl(w1_part, 0, P, p * HF, (1, HF)), start=(p == 0), stop=(p == NPATH - 1))
            last.then_inc(w1s_mm, 1)
            def hidden_x(g, m):
                for k in range(CT):
                    pe.matmul(bank(m, 0, P, 0, (1, GT)), sl(w1_x, 0, P, k * HF + m * P, (1, P)),
                              sl(xT2, 0, P, k * TOK + g * CG, (C, BLK), (1, CG)), start=(k == 0), stop=False)

            pe.wait_ge(w1x_in, 16)
            pe.wait_ge(xT2_in, 16)
            for m in range(4):
                hidden_x(0, m)
            pe.wait_ge(st_ready, 1)
            pe.wait_ge(w1s_ready, 1)
            pe.wait_ge(fir_act, 32)
            for n in range(8):
                ring(n, 0, st_act, st_dve)
                for w in range(4):
                    last = pe.transpose(bank(4 + n % 4, 0, 40, w * P, (1, P)), sl(st, 0, P, (4 * n + w) * 40, (1, 40)), ident)
                last.then_inc(st_mm, 1)
            pe.wait_ge(st_act, 4)
            pe.wait_ge(st_dve, 4)
            def logits(g):
                pe.wait_ge(hid_act, 4 * (g + 1))
                if g >= 2:
                    pe.wait_ge(lT_kept, g - 1)
                for m in range(4):
                    last = pe.matmul(bank(6 + g % 2, 0, 20, 0, (1, GT)), sl(w2_sb, 0, P, m * 20, (1, 20)),
                                     sl(hT, 0, P, m * TOK + g * GT, (1, GT)), start=(m == 0), stop=(m == 3))
                last.then_inc(lT_mm, 1)
                pe.wait_ge(lT_kept, g + 1)
                if g >= 2:
                    pe.wait_ge(gate_step, 3 * (g - 2) + 1)
                for j in range(CG):
                    for ct in range(CT):
                        last = pe.matmul(bank(5 - g % 2, DV * ct, DV, j * 10, (1, 10)),
                                         sl(lT, 0, 20, g * GT + j, (CG, BLK)),
                                         sl(ident, 0, 20, ct * 10, (1, 10)), start=True, stop=True, skip_group_check=True)
                last.then_inc(lg_mm, 1)

            for g in range(GATED):
                for m in range(4):
                    if g:
                        pe.wait_ge(hid_act, 4 * (g - 1) + m + 1)
                        hidden_x(g, m)
                    pe.matmul(bank(m, 0, P, 0, (1, GT)), sl(w1_s, 0, P, m * P, (1, P)),
                              sl(statsT, 0, P, g * CG, (C, BLK), (1, CG)), start=False, stop=True).then_inc(hid_mm, 1)
                    if g and m == 0:
                        logits(g - 1)
            logits(GATED - 1)

            for n in range(8):
                pe.wait_ge(mix_step, 7 * (4 * n // CG + 1))
                ring(n, 0, on_act, on_dve)
                for w in range(4):
                    last = pe.transpose(bank(n % 4, 0, P, w * P, (1, P)), sl(mix, 0, P, (4 * n + w) * P, (1, P)), ident)
                last.then_inc(on_mm, 1)
            pe.wait_ge(on_act, 4)
            pe.wait_ge(on_dve, 4)
            pe.wait_ge(wo_scaled, 1)
            def project_out(dst, t):
                for k in range(CT):
                    last = pe.matmul(dst, sl(onT, 0, P, k * TOK + t * P, (1, P)),
                                     sl(w_o, 0, P, k * D, (1, D)), start=(k == 0), stop=(k == CT - 1))
                return last

            for t in range(TPB):
                project_out(bank(t, 0, P, 0, (1, D)), t).then_inc(wo_mm, 1)
            pe.wait_ge(wts_in, 16 * 7)
            for i, (x, y) in enumerate(((x_q, x_k), (x_v, x_oT))):
                for m in range(CT):
                    for k in range(CT):
                        last = pe.matmul(bank(6 + i, 0, P, m * D, (1, D)), sl(x, 0, P, k * D + m * P, (1, P)),
                                         sl(y, 0, P, k * D, (1, D)), start=(k == 0), stop=(k == CT - 1),
                                         skip_group_check=True)
                last.then_inc(fold_mm, 1)
            for m in range(CT):
                for k in range(CT):
                    last = pe.matmul(bank(4, 0, P, m, (1, 1)), sl(x_k, 0, P, k * D + m * P, (1, P)),
                                     sl(bq_col, 0, P, k, (1, 1)), start=(k == 0), stop=(k == CT - 1))
            last.then_inc(fold_mm, 1)
            pe.wait_ge(bv_ready, 1)
            for k in range(CT):
                last = pe.matmul(bank(5, 0, P, 0, (1, D)), sl(bv_rep, 0, P, k * P, (1, P)), sl(x_oT, 0, P, k * D, (1, D)),
                                 start=(k == 0), stop=(k == CT - 1))
            last.then_inc(fold_mm, 1)

            pe.wait_ge(res1, TPB)

            def claim(*step):
                bk, i = misc(*step)
                if i:
                    pe.wait_ge(free[bk - 6], i)
                return bk, full[bk - 6]

            def freed(*step):
                bk, i = misc(*step)
                pe.wait_ge(free[bk - 6], i + 1)

            def product(dst, w_h, w_l, x_h, x_l, start, stop):
                w_h, w_l, x_h, x_l = (r32(x) for x in (w_h, w_l, x_h, x_l))
                pe.matmul(dst, w_h, x_h, start=start, stop=False)
                pe.matmul(dst, w_h, x_l, start=False, stop=False)
                return pe.matmul(dst, w_l, x_h, start=False, stop=stop)

            def turn_p(n, g):
                pe.wait_ge(exped, n + 1)
                if 4 * n + g >= 2:
                    pe.wait_ge(p_kept, 4 * n + g - 1)
                g0, count, rows = group(g)
                for w in range(count):
                    last = pe.transpose(bank(4 + g % 2, 0, rows, w * P, (1, P)),
                                        sl(p_sb, 0, P, (n % 2) * 1664 + (g0 + w) * P, (1, rows)), ident)
                last.then_inc(p_mm, 1)

            pe.wait_ge(fold_done, 3)
            pe.wait_ge(bvo_ready, 1)
            pe.wait_ge(zero_words, SETS + 3)
            for kind, b, i in TAIL:
                n = TPB * b + i
                if (kind, b, i) in MISC:
                    bk, done = claim(kind, b, i)
                if kind == "wo":
                    project_out(bank(bk, 0, P, 0, (1, D)), n).then_inc(done, 1)
                elif kind == "turn_x1":
                    pe.wait_ge(x1_ready, TPB * (b + 1))
                    for w in range(4):
                        t, ct = divmod(w, CT)
                        last = pe.transpose(bank(bk, 0, P, w * P, (1, P)),
                                            sl(x1, 0, P, (TPB * b + 2 * i + t) * D + ct * P, (1, P)), ident)
                    last.then_inc(done, 1)
                elif kind == "qk":
                    for k in range(2):
                        freed("turn_x1", b, k)
                    for k in range(CT):
                        last = pe.matmul(bank(bk, 0, P, 0, (1, L)), sl(w_qk, 0, P, k * D + i * P, (1, P)),
                                         sl(x1T, 0, P, k * L, (1, L)), start=(k == 0), stop=(k == CT - 1))
                    last.then_inc(done, 1)
                elif kind == "scores":
                    if i == 0:
                        for k in range(CT):
                            freed("qk", b, k)
                    if n:
                        pe.wait_ge(exped, n)
                    for j, c in enumerate(COLS):
                        off, w = ctx_cols(c)
                        w += w % 2
                        if i == 0:
                            pe.wait_ge(ctxt_ready, 4 * b + j + 1)
                        for k in range(CT):
                            last = product(bank(c, 0, P, 0, (1, w)),
                                           sl(qk_h, 0, P, k * L + i * P, (1, P)), sl(qk_l, 0, P, k * L + i * P, (1, P)),
                                           sl(ctxt_h, 0, P, k * S_PAD + off, (1, w)),
                                           sl(ctx_t, 0, P, ((b % 2) * CT + k) * S_PAD + off, (1, w)),
                                           k == 0, k == CT - 1)
                        last.then_inc(scored, 1)
                        if n:
                            for g in TURNS[c]:
                                turn_p(n - 1, g)
                elif kind == "turn_last":
                    for g in range(4):
                        turn_p(n, g)
                elif kind == "pv":
                    pe.wait_ge(p_kept, 4 * (TPB * b + 2 * i + 2))
                    pe.wait_ge(ctxn_ready, 10 * (b + 1))
                    for m in range(CT):
                        for g, kv in enumerate(KV):
                            at_c, at_p = g * D + m * P, g * 2 * P
                            last = product(bank(bk, 0, P, m * 256, (1, 256)),
                                           sl(ctxn_h, 0, kv, at_c, (1, P)), sl(ctx_n, 0, kv, at_c, (1, P)),
                                           sl(pT_h, 0, kv, at_p, (1, 256)), sl(pT_l, 0, kv, at_p, (1, 256)),
                                           g == 0, g == 12)
                    last.then_inc(done, 1)
                elif kind == "post":
                    freed("pv", b, i // 2)
                    for k in range(CT):
                        last = pe.matmul(bank(bk, 0, P, 0, (1, D)), sl(pcT, 0, P, k * L + i * P, (1, P)),
                                         sl(w_vo, 0, P, k * D, (1, D)), start=(k == 0), stop=(k == CT - 1))
                    last.then_inc(done, 1)
                elif kind == "turn_x2":
                    pe.wait_ge(x2_ready, TPB * (b + 1))
                    for w in range(4):
                        t, ct = divmod(w, CT)
                        last = pe.transpose(bank(bk, 0, P, w * P, (1, P)),
                                            sl(x2, 0, P, (2 * i + t) * D + ct * P, (1, P)), ident)
                    last.then_inc(done, 1)
                elif kind == "ffn":
                    pair, m = divmod(i, FT)
                    freed("turn_x2", b, pair)
                    pe.wait_ge(w_split, 2 * (2 + FT))
                    for to, (w_h, w_l) in enumerate(((wg_h, w_g), (wu_h, w_u))):
                        for k in range(CT):
                            last = product(bank(bk, 0, P, to * 256, (1, 256)),
                                           sl(w_h, 0, P, k * HID + m * P, (1, P)), sl(w_l, 0, P, k * HID + m * P, (1, P)),
                                           sl(x2T_h, 0, P, k * 256, (1, 256)), sl(x2T_l, 0, P, k * 256, (1, 256)),
                                           k == 0, k == CT - 1)
                    last.then_inc(done, 1)
                elif kind == "down":
                    pe.wait_ge(h_ready, FT * (2 * b + i // 2 + 1))
                    for m in range(FT):
                        at_h = m * 256 + (i % 2) * P
                        last = product(bank(bk, 0, P, 0, (1, D)),
                                       sl(hF_h, 0, P, at_h, (1, P)), sl(hF_l, 0, P, at_h, (1, P)),
                                       wd_h[m], sl(w_d, 0, P, m * D, (1, D)), m == 0, m == FT - 1)
                    last.then_inc(done, 1)

        @block.vector
        def _(dve):
            def project(n):
                if n >= NPROJ:
                    return
                b, j = divmod(n, 6)
                proj, ct = divmod(j, 2)
                dve.wait_ge(tap_first, n + 1)
                for k in range(1, CONV_K):
                    if k > 1:
                        dve.wait_ge(tap_step, 2 * n + k - 1)
                    y = sl(y_buf, 0, P, (n % 2) * L + k, (1, L - k))
                    dve.scalar_tensor_tensor(
                        out=y, in0=bank(n % 2, 0, P, 0, (1, L - k)),
                        scalar=sl(conv_w, 0, P, ct * 12 + proj * CONV_K + CONV_K - 1 - k, (1, 1)), in1=y,
                        op0=ALU.mult, op1=ALU.add).then_inc(tap_step if k < CONV_K - 1 else conv_done, 1)

            def turn(t):
                b, r = divmod(t, TPB)
                dve.wait_ge(raw_done, t + 1)
                if b and r == 0:
                    dve.wait_ge(sqrt_done, b)
                dve.tensor_reduce(sl(ss, 0, P, r * 8, (1, 8)), sl(sq, 0, P, 0, (DV, 8), (1, DV)), AX.X, ALU.add
                                  ).then_inc(ss_done, 1)
                dve.wait_ge(v_turned, t + 1)
                if t == 0:
                    dve.wait_ge(beta_ready, 1)
                dve.tensor_tensor(sl(vk, 0, P, t * 512, (DV, H), (1, DV)), bank(3, 0, P, 0, (DV, H), (1, DV)),
                                  sl(beta, 0, P, t * H, (1, H), (0, DV)), ALU.mult).then_inc(vb_done, 1)

            def normalise(b):
                dve.wait_ge(sqrt_done, b + 1)
                if b:
                    dve.wait_ge(qn_done, b)
                dve.reciprocal(rn, nrm).then_inc(rn_done, 1)
                dve.wait_ge(rn_done, b + 1)
                knb = sl(kn, 0, P, b * TPB * D, (D, TPB), (DV, H), (1, DV))
                dve.tensor_tensor(knb, sl(raw, 0, P, 0, (2 * D, TPB), (DV, H), (1, DV)),
                                  sl(rn, 0, P, 0, (8, TPB), (1, H), (0, DV)), ALU.mult).then_inc(kn_done, 1)
                dve.wait_ge(kn_done, b + 1)
                dve.tensor_tensor(sl(vk, 0, P, b * TPB * 512 + D, (512, TPB), (DV, H), (1, DV)),
                                  sl(kn, 0, P, b * TPB * D, (D, TPB), (DV, H), (1, DV)),
                                  sl(beta, 0, P, b * TPB * H, (H, TPB), (1, H), (0, DV)), ALU.mult).then_inc(kb_done, 1)

            def gram(t):
                dve.wait_ge(gram_done, t + 1)
                for q in range(QC):
                    dve.tensor_tensor(sl(al, C * q, C, t * 256, (P, CT), (C, 4), (1, C)),
                                      bank(6, C * q, C, C * q, (512, CT), (P, 4), (1, C)),
                                      sl(mask_gram, C * q, C, 0, (0, CT), (C, 4), (1, C)), ALU.mult
                                      ).then_inc(gram_masked, 1)

            steps_before = [0]

            def solve(s, l):
                if l == 0:
                    dve.wait_ge(a_in, 16 * (s + 1))
                    dve.wait_ge(u_init, 2 * (s + 1))
                n = C - 1 - l
                if l:
                    dve.wait_ge(solve_step, steps_before[0])
                dve.tensor_tensor(sl(u_tmp, 0, P, 0, (n, l + 1), (1, n)),
                                  sl(u_row, 0, P, l, (C, l + 1), (0, n)),
                                  sl(a_row, 0, P, l * C + l + 1, (0, l + 1), (1, n)), ALU.mult
                                  ).then_inc(solve_step, 1)
                steps_before[0] += 1
                dve.wait_ge(solve_step, steps_before[0])
                u = sl(u_row, 0, P, l + 1, (C, l + 1), (1, n))
                last = dve.tensor_tensor(u, u, sl(u_tmp, 0, P, 0, (n, l + 1), (1, n)), ALU.add)
                if l < C - 2:
                    last.then_inc(solve_step, 1)
                    steps_before[0] += 1
                else:
                    last.then_inc(solved, 1)

            solve_from = ORDER.index(("gram", TPS - 1)) + SOLVE_AFTER
            l = 0
            for kind, n in ORDER:
                if kind == "project":
                    project(n)
                elif kind == "turn":
                    turn(n)
                elif kind == "normalise":
                    normalise(n)
                elif kind == "gram":
                    gram(n)
                for _ in range(2):
                    if ORDER.index((kind, n)) >= solve_from and l < C - 1:
                        solve(0, l)
                        l += 1
            for l in range(l, C - 1):
                solve(0, l)
            dve.wait_ge(s_const, 16 * 7)

            for l in range(C - 1):
                solve(1, l)
            for t in range(TPS, TILES + 1):
                if t < TILES and uw_kept(t)[0] is uw_dve:
                    dve.wait_ge(uw_mm, t + 1)
                    dve.tensor_copy(uw_dst(t), uw_src(t)).then_inc(uw_dve, 1)
                if w_kept(t - 1)[0] is w_dve:
                    dve.wait_ge(w_turned, t)
                    dve.tensor_copy(w_dst(t - 1), w_src(t - 1)).then_inc(w_dve, 1)

            for n in range(STEPS):
                g, q = divmod(n, QC)
                for s in range(SETS):
                    dve.wait_ge(wq_mm[s], n + 1)
                    dve.tensor_tensor(sl(u_new, C * q, C, (s * 2 + n % 2) * 512, (D, 2), (DV, H), (1, DV)),
                                      sl(vk, C * q, C, (s * TPS + g) * 512, (TPB * 512, 2), (DV, H), (1, DV)),
                                      bank(2 * s + n % 2, 0, C, 0, (D, 2), (DV, H), (1, DV)), ALU.subtract
                                      ).then_inc(u_ready[s], 1)
                if n == STEPS - 1:
                    continue
                for s in range(SETS):
                    dve.wait_ge(s_mm[s], n + 1)
                    dve.tensor_tensor(sl(state, 0, P, s * 512, (P, 4), (1, P)), bank(4 + s, 0, P, 0, (P, 4), (1, P)),
                                      sl(mask_heads, 0, P, 0, (0, 4), (1, P)), ALU.mult).then_inc(state_ready[s], 1)

            for n in range(1, 32, 2):
                dve.wait_ge(win_mm, n + 1)
                dve.tensor_copy(win_dst(n), bank(n % 4, 0, WIN, 0, (1, P), (P, 4))).then_inc(win_dve, 1)
            for n in range(1, 24, 2):
                dve.wait_ge(blk_mm, n + 1)
                dve.tensor_copy(blk_dst(n), blk_src(n)).then_inc(blk_dve, 1)
            dve.wait_ge(blk_act, 12)
            dve.wait_ge(blk_dve, 12)
            for j, (p, h) in enumerate(STATS):
                if p < NF:
                    dve.wait_ge(fir_act, 16 * (h + 1))
                x = sl(PATHS[p], 0, P, h * DV, (P, C), (1, DV))
                to = p * 8 + h * 4
                dve.tensor_reduce(sl(st, 0, P, to, (40, C)), x, AX.X, ALU.add)
                dve.tensor_reduce(sl(st, 0, P, to + 2, (40, C)), x, AX.X, ALU.add,
                                  apply_absolute_value=True).then_inc(stat_abs, 1)
                dve.wait_ge(sq_ready, j + 1)
                dve.tensor_reduce(sl(st, 0, P, to + 1, (40, C)), sl(sqt, 0, P, (j % 2) * C * DV, (DV, C), (1, DV)),
                                  AX.X, ALU.add).then_inc(stat_sq, 1)
            dve.wait_ge(st_norm, 1)
            dve.wait_ge(stat_sq, 2 * NPATH)
            dve.wait_ge(stat_abs, 2 * NPATH)
            dve.tensor_scalar(sl(st, 0, P, 0, (4, 320), (1, 3)), sl(st, 0, P, 0, (4, 320), (1, 3)), 1.0 / DV, None,
                              ALU.mult).then_inc(st_ready, 1)
            dve.wait_ge(s_par, 16 * 8)
            dve.tensor_scalar(tau_t[:, 0:2], tau_in, -1.0, None, ALU.mult).then_inc(par_dve, 1)
            dve.wait_ge(par_dve, 1)
            dve.tensor_tensor(tau_t[:, 0:2], tau_t[:, 0:2], tau_in, ALU.max).then_inc(par_dve, 1)
            dve.wait_ge(par_act, 2)
            dve.tensor_scalar(tau_in, tau_in, 0.0, 0.5, ALU.max, ALU.add).then_inc(par_dve, 1)
            dve.wait_ge(par_dve, 3)
            dve.tensor_tensor(tau_in, tau_in, tau_t[:, 2:4], ALU.add).then_inc(par_dve, 1)
            dve.wait_ge(par_dve, 4)
            dve.reciprocal(tau_inv, tau_in).then_inc(par_dve, 1)

            dve.wait_ge(w1s_mm, 1)
            dve.tensor_copy(w1_s, bank(4, 0, P, 0, (1, HF))).then_inc(w1s_ready, 1)
            dve.wait_ge(statsT_zero, 1)
            for n in range(1, 8, 2):
                dve.wait_ge(st_mm, n + 1)
                for ct in range(CT):
                    last = dve.tensor_copy(stats_dst(n, ct), bank(4 + n % 4, 0, 40, ct * DV, (P, 4), (1, DV)))
                last.then_inc(st_dve, 1)
            dve.wait_ge(par_act, 3)
            dve.tensor_scalar(eps_row, eps_row, 0.2, None, ALU.mult).then_inc(par_dve, 1)
            dve.wait_ge(par_dve, 6)
            dve.tensor_reduce(eps_keep, sl(eps_row, 0, P, 0, (NPATH, 2), (1, NPATH)), AX.X, ALU.add).then_inc(par_dve, 1)
            dve.wait_ge(par_dve, 7)
            dve.tensor_scalar(eps_keep, eps_keep, -1.0, 1.0, ALU.mult, ALU.add).then_inc(par_dve, 1)

            for g in range(GATED):
                lgg, prg = sl(lg, 0, P, g * 10 * CG, (1, 10 * CG)), sl(pr, 0, P, g * 10 * CG, (1, 10 * CG))
                mxg, smg, rsg, r64g = (sl(x, 0, P, g * 2 * CG, (1, 2 * CG)) for x in (mx, sm, rs, r64))
                step = 7 * g
                dve.wait_ge(lg_mm, g + 1)
                dve.tensor_tensor(sl(lgg, 0, P, 0, (10, CG), (1, 10)), bank(5 - g % 2, 0, P, 0, (10, CG), (1, 10)),
                                  sl(gb2_row, 0, P, 0, (0, CG), (1, 10)), ALU.add).then_inc(gate_step, 1)
                dve.wait_ge(gate_step, 3 * g + 1)
                dve.wait_ge(par_dve, 8)
                lg3 = sl(lgg, 0, P, 0, (10, CG), (NPATH, 2), (1, NPATH))
                dve.tensor_tensor(lg3, lg3, sl(tau_inv, 0, P, 0, (0, CG), (1, 2), (0, NPATH)), ALU.mult
                                  ).then_inc(gate_step, 1)
                dve.wait_ge(gate_step, 3 * g + 2)
                lg2 = sl(lgg, 0, P, 0, (NPATH, 2 * CG), (1, NPATH))
                dve.tensor_reduce(mxg, lg2, AX.X, ALU.max).then_inc(mix_step, 1)
                dve.wait_ge(mix_step, step + 1)
                dve.tensor_tensor(lg2, lg2, sl(mxg, 0, P, 0, (1, 2 * CG), (0, NPATH)), ALU.subtract).then_inc(gate_step, 1)
                dve.wait_ge(exp_done, g + 1)
                pr2 = sl(prg, 0, P, 0, (NPATH, 2 * CG), (1, NPATH))
                dve.tensor_reduce(smg, pr2, AX.X, ALU.add).then_inc(mix_step, 1)
                dve.wait_ge(mix_step, step + 2)
                dve.reciprocal(rsg, smg).then_inc(mix_step, 1)
                dve.wait_ge(mix_step, step + 3)
                keep = sl(rsg, 0, P, 0, (2, CG), (1, 2))
                dve.tensor_tensor(keep, keep, sl(eps_keep, 0, P, 0, (0, CG), (1, 2)), ALU.mult).then_inc(mix_step, 1)
                dve.wait_ge(mix_step, step + 4)
                dve.tensor_tensor(pr2, pr2, sl(rsg, 0, P, 0, (1, 2 * CG), (0, NPATH)), ALU.mult).then_inc(mix_step, 1)
                dve.wait_ge(mix_step, step + 5)
                pr10 = sl(prg, 0, P, 0, (10, CG), (1, 10))
                dve.tensor_tensor(pr10, pr10, sl(eps_row, 0, P, 0, (0, CG), (1, 10)), ALU.add).then_inc(pr_ready, 1)
                dve.wait_ge(pr_ready, g + 1)

                def part(x):
                    return sl(x, 0, P, g * CG * P, (DV, 2 * CG), (1, DV))

                for p in range(2, NPATH):
                    x = part(PATHS[p])
                    dve.tensor_tensor(x, x, sl(prg, 0, P, p, (NPATH, 2 * CG), (0, DV)), ALU.mult).then_inc(mix_dve, 1)
                for i, x in enumerate((o_blk, v_blk, PATHS[0])):
                    dve.wait_ge(mix_dve, 6 * g + 3 + i)
                    if i == 2:
                        dve.wait_ge(mix_pool, 3 * (g + 1))
                    dve.tensor_tensor(part(mix), part(mix), part(x), ALU.add).then_inc(mix_dve, 1)
                dve.wait_ge(mix_sq, 2 * g + 1)
                dve.tensor_reduce(r64g, part(sqt), AX.X, ALU.add).then_inc(mix_sum, 1)
                dve.wait_ge(mix_sq, 2 * g + 2)
                dve.reciprocal(r64g, rsg).then_inc(mix_step, 1)
                dve.wait_ge(mix_step, step + 6)
                dve.tensor_tensor(part(mix), part(mix), sl(r64g, 0, P, 0, (1, 2 * CG), (0, DV)), ALU.mult
                                  ).then_inc(mix_step, 1)
            dve.wait_ge(mix_pool, 3 * GATED)
            for n in range(1, 8, 2):
                dve.wait_ge(on_mm, n + 1)
                dve.tensor_copy(on_dst(n), on_src(n)).then_inc(on_dve, 1)
            dve.wait_ge(wts_in, 16 * 7)
            dve.tensor_copy(sl(bv_rep, 0, P, 0, (P, CT), (1, P)), sl(bv_col, 0, P, 0, (1, CT), (0, P))
                            ).then_inc(bv_ready, 1)

            def residual1(t, y):
                b, i = divmod(t, TPB)
                n = NORMS.index(("wo", b, i))
                dve.wait_ge(x_in[b], 16)
                x = sl(x1, 0, P, t * D, (1, D))
                dve.tensor_tensor(x, x, y, ALU.add).then_inc(res1, 1)
                dve.wait_ge(res1, t + 1)
                if n:
                    dve.wait_ge(agg, n)
                dve.bn_stats(bn6, x).then_inc(bn, 1)
                dve.wait_ge(bn, n + 1)
                dve.bn_aggr(mv[:, 2 * t:2 * t + 2], bn6).then_inc(agg, 1)

            def norm1(b):
                dve.wait_ge(sqrt1, b + 1)
                rb = rstd[:, TPB * b:TPB * b + TPB]
                dve.reciprocal(rb, rb).then_inc(rstd1, 1)
                dve.wait_ge(rstd1, b + 1)
                for i in range(TPB * b, TPB * b + TPB):
                    x = sl(x1, 0, P, i * D, (1, D))
                    dve.tensor_scalar(x, x, mv[:, 2 * i:2 * i + 1], rstd[:, i:i + 1], ALU.subtract, ALU.mult
                                      ).then_inc(x1_ready, 1)

            for t in range(TPB):
                dve.wait_ge(wo_mm, t + 1)
                residual1(t, bank(t, 0, P, 0, (1, D)))

            def low_ctx(b, i):
                dve.wait_ge(ctxt_high, 4 * b + i + 1)
                off, w = ctx_cols(COLS[i])
                x = sl(ctx_t, 0, P, (b % 2) * CT * S_PAD + off, (S_PAD, CT), (1, w))
                dve.tensor_tensor(r32(x), loaded(x), high_of(sl(ctxt_h, 0, P, off, (S_PAD, CT), (1, w))), ALU.subtract
                                  ).then_inc(ctxt_ready, 1)

            for i in range(4):
                low_ctx(0, i)
            norm1(0)

            dve.wait_ge(fold_mm, 4)
            dve.tensor_tensor(b_vo, bank(5, 0, P, 0, (1, D)), bo_row, ALU.add).then_inc(bvo_ready, 1)

            def filled(*step):
                bk, i = misc(*step)
                dve.wait_ge(full[bk - 6], i + 1)
                return bk, free[bk - 6]

            def statistics(kind, b, i, x):
                k = 2 * b + (kind == "down")
                n = NORMS.index((kind, b, i))
                dve.wait_ge(res2, TPB * k + i + 1)
                dve.wait_ge(agg, n)
                if i == 0 and k:
                    dve.wait_ge(x2_ready if k % 2 else y_ready, TPB * ((k + 1) // 2))
                dve.bn_stats(bn6, x).then_inc(bn, 1)
                dve.wait_ge(bn, n + 1)
                dve.bn_aggr(mv2[:, 2 * i:2 * i + 2], bn6).then_inc(agg, 1)

            def centre(k, src, dst, done):
                dve.wait_ge(sqrt2, k + 1)
                dve.reciprocal(rstd2, rstd2).then_inc(rstd2_ready, 1)
                dve.wait_ge(rstd2_ready, k + 1)
                for i in range(TPB):
                    dve.tensor_scalar(sl(dst, 0, P, i * D, (1, D)), sl(src, 0, P, i * D, (1, D)),
                                      mv2[:, 2 * i:2 * i + 1], rstd2[:, i:i + 1], ALU.subtract, ALU.mult
                                      ).then_inc(done, 1)

            def low_p(n, g):
                dve.wait_ge(p_high, 4 * n + g + 1)
                g0, count, rows = group(g)
                dve.tensor_tensor(r32(p_dst(pT_l, n, g)), bank(4 + g % 2, 0, rows, 0, (P, count), (1, P)),
                                  high_of(p_dst(pT_h, n, g)), ALU.subtract).then_inc(p_kept, 1)

            def low_h(k):
                dve.wait_ge(h_high, k + 1)
                x = sl(hF_l, 0, P, k % FT * 256, (1, 256))
                dve.tensor_tensor(r32(x), x, high_of(sl(hF_h, 0, P, k % FT * 256, (1, 256))), ALU.subtract
                                  ).then_inc(h_ready, 1)

            for kind, b, i in TAIL:
                n = TPB * b + i
                if kind == "split_ctx":
                    low_ctx(b, i)
                elif kind == "qk":
                    bk, done = filled(kind, b, i)
                    dve.wait_ge(high_kept, 2 * b + i + 1)
                    dve.scalar_tensor_tensor(out=r32(sl(qk_l, 0, P, i * L, (1, L))),
                                             in0=bank(bk, 0, P, 0, (1, L)), scalar=bqk[:, i:i + 1],
                                             in1=high_of(sl(qk_h, 0, P, i * L, (1, L))), op0=ALU.add, op1=ALU.subtract
                                             ).then_inc(done, 1)
                elif kind == "turn_x2":
                    bk, done = filled(kind, b, i)
                    dve.tensor_copy(r32(sl(x2T_h, 0, P, 0, (P, 2), (256, CT), (1, P))),
                                    bank(bk, 0, P, 0, (256, 2), (P, CT), (1, P))).then_inc(x2_high, 1)
                    dve.wait_ge(x2_high, 2 * b + i + 1)
                    dve.tensor_tensor(r32(sl(x2T_l, 0, P, 0, (P, 2), (256, CT), (1, P))),
                                      bank(bk, 0, P, 0, (256, 2), (P, CT), (1, P)),
                                      high_of(sl(x2T_h, 0, P, 0, (P, 2), (256, CT), (1, P))), ALU.subtract).then_inc(done, 1)
                elif kind == "scores":
                    for j, c in enumerate(COLS):
                        dve.wait_ge(scored, 4 * n + j + 1)
                        off, w = ctx_cols(c)
                        last = dve.tensor_reduce(sl(sm_part, 0, P, c, (1, 1)), bank(c, 0, P, 0, (1, w)), AX.X, ALU.max)
                        if n:
                            for g in TURNS[c]:
                                low_p(n - 1, g)
                    last.then_inc(maxed, 1)
                    dve.wait_ge(maxed, 2 * n + 1)
                    dve.tensor_reduce(sl(sm_max, 0, P, n % 8, (1, 1)), sm_part, AX.X, ALU.max).then_inc(maxed, 1)
                    dve.wait_ge(maxed, 2 * n + 2)
                    dve.tensor_scalar(sl(sm_neg, 0, P, n % 8, (1, 1)), sl(sm_max, 0, P, n % 8, (1, 1)), -1.0 / 16.0,
                                      None, ALU.mult).then_inc(neg_ready, 1)
                elif kind == "turn_last":
                    for g in range(4):
                        low_p(n, g)
                elif kind == "wo":
                    bk, done = filled(kind, b, i)
                    residual1(n, bank(bk, 0, P, 0, (1, D)))
                    dve.sem_inc(done, 1)
                    if i == TPB - 1:
                        norm1(b)
                elif kind == "post":
                    if i == 0:
                        dve.wait_ge(exped, TPB * (b + 1))
                        dve.reciprocal(sl(sm_inv, 0, P, (b % 2) * TPB, (1, TPB)),
                                       sl(sm_sum, 0, P, (b % 2) * TPB, (1, TPB))).then_inc(inv_ready, 1)
                        dve.wait_ge(inv_ready, b + 1)
                        dve.wait_ge(x1_bias, b + 1)
                    bk, done = filled(kind, b, i)
                    x = sl(x1, 0, P, n * D, (1, D))
                    dve.scalar_tensor_tensor(out=x, in0=bank(bk, 0, P, 0, (1, D)),
                                             scalar=sl(sm_inv, 0, P, n % 8, (1, 1)), in1=x,
                                             op0=ALU.mult, op1=ALU.add).then_inc(res2, 1)
                    statistics("post", b, i, x)
                    dve.sem_inc(done, 1)
                    if i == TPB - 1:
                        centre(2 * b, sl(x1, 0, P, b * TPB * D, (1, TPB * D)), x2, x2_ready)
                elif kind == "ffn":
                    bk, done = filled(kind, b, i)
                    k = 2 * FT * b + i
                    dve.wait_ge(silu_g, k + 1)
                    dve.tensor_tensor(sl(hF_l, 0, P, k % FT * 256, (1, 256)), sl(sg, 0, P, (k % 2) * 256, (1, 256)),
                                      bank(bk, 0, P, 256, (1, 256)), ALU.mult).then_inc(h_product, 1)
                    dve.wait_ge(h_product, k + 1)
                    dve.sem_inc(done, 1)
                    if i % FT:
                        low_h(k - 1)
                    if i % FT == FT - 1:
                        low_h(k)
                elif kind == "down":
                    bk, done = filled(kind, b, i)
                    x = sl(x2, 0, P, i * D, (1, D))
                    dve.tensor_tensor(x, x, bank(bk, 0, P, 0, (1, D)), ALU.add).then_inc(res2, 1)
                    statistics("down", b, i, x)
                    dve.sem_inc(done, 1)
                    if i == TPB - 1:
                        if b:
                            dve.wait_ge(stored, 16 * b)
                        centre(2 * b + 1, x2, y_out, y_ready)



def constants():
    import numpy as np

    row = np.arange(P)
    gram = np.zeros((P, 4, C), np.float32)
    behind = np.arange(C)[None, :] - (row % C)[:, None]
    gram[:, 0:2, :] = -(behind > 0).astype(np.float32)[:, None, :]
    gram[:, 2:4, :] = (behind >= 0).astype(np.float32)[:, None, :]
    heads = (row[:, None] // DV == row[None, :] // DV).astype(np.float32)
    h, kind = row // 32, row // 8 % 4
    expand = np.zeros((P, NPATH, P), np.float32)
    for p in range(NPATH):
        expand[row, p, 64 * (h // 2) + 8 * p + 4 * (h % 2) + kind] = 1.0
    eps = np.zeros((P, 4), np.float32)
    eps[:, 0], eps[:, 1] = 1e-6, LN_EPS
    return {"ident": np.eye(P, dtype=np.float32), "mask_gram": gram.reshape(P, -1), "mask_heads": heads,
            "expand": expand.reshape(P, -1), "eps": eps}


def laid_out(inputs):
    import numpy as np

    a, x, f = "L0_attn_", "L0_xattn_", "L0_ffn_"
    get = {k: np.asarray(v) for k, v in inputs.items()}
    own = {"xT": get["x"].reshape(TOK, D).T, "x": get["x"].reshape(TOK, D),
           "ctx": get["ctx_1024"].reshape(-1, D), "ctxT": get["ctx_1024"].transpose(0, 2, 1).reshape(NB * D, S_CTX)}
    for k in ("Wq", "Wk", "Wv", "Wb", "Wo", "conv_q", "conv_k", "conv_v", "gW1", "gW2", "gb2", "log_tau", "norm_w"):
        own[k] = get[a + k]
    own["gb1"] = get[a + "gb1"].reshape(-1, P).T
    own["eps_logit"] = get[a + "eps_logit"].reshape(-1)
    taps = np.zeros((D, WIN + C - 1, NF), np.float32)
    for i, k in enumerate(("fir_s", "fir_m", "fir_l")):
        taps[:, WIN - FIRS[i]:WIN, i] = get[a + k]
    own["taps"] = taps.reshape(D, -1)
    own.update({"xWq": get[x + "Wq"], "xWk": get[x + "Wk"], "xWv": get[x + "Wv"], "xWoT": get[x + "Wo"].T,
                "xbq": get[x + "bq"].reshape(CT, P).T, "xbv": get[x + "bv"].reshape(CT, P).T, "xbo": get[x + "bo"],
                "wgT": get[f + "w_gate"].T, "wuT": get[f + "w_up"].T, "wdT": get[f + "w_down"].T})
    own.update(constants())
    return {k: np.ascontiguousarray(v) for k, v in own.items()}


def kernel(**inputs):
    import concourse.bacc as bacc
    from concourse.bass_utils import run_bass_kernel_spmd

    nc = bacc.Bacc("TRN2", target_bir_lowering=False, num_devices=1)
    arrays = {f"in_{k}_dram": v for k, v in laid_out(inputs).items()}
    a = {k[3:-5]: nc.dram_tensor(k, list(v.shape), mybir.dt.from_np(v.dtype), kind="ExternalInput").ap()
         for k, v in arrays.items()}
    for k in ("scr_a", "scr_u"):
        a[k] = nc.dram_tensor(k, [2, P, C * C], F32, kind="Internal").ap()
    out = nc.dram_tensor("out_0_dram", [TOK, D], F32, kind="ExternalOutput").ap()
    build(nc, a, out)
    r = run_bass_kernel_spmd(nc, [arrays], core_ids=[0])
    return r.results[0]["out_0_dram"].reshape(NB, L, D)
```
